# Optimizing a Trainium2 kernel written in Bass

```python
import numpy as np
import jax
import jax.numpy as jnp

def _softmax(x, axis=-1):
    return jax.nn.softmax(x, axis=axis)

def _gelu(x):
    return jax.nn.gelu(x, approximate=True)

def _silu(x):
    return jax.nn.silu(x)

def _sigmoid(x):
    return jax.nn.sigmoid(x)

def _layernorm(x, axis=-1, eps=1e-05):
    m = jnp.mean(x, axis=axis, keepdims=True)
    v = jnp.var(x, axis=axis, keepdims=True)
    return (x - m) / jnp.sqrt(v + eps)

def _scatter_add(tgt, idx, src, axis=0):
    return tgt.at[idx].add(src)

def _segment_sum(src, seg, n):
    return jax.ops.segment_sum(src, seg, n)
kernel_name = 'mk_flamingo_gated_d4_seqx_r8_05593f'

def setup_inputs(seed: int=0):
    np.random.seed(seed)
    _w = jnp.asarray

    def _rec_inputs():
        import jax
        import jax.numpy as jnp
        _rk = jax.random.key(seed)
        x = -0.0002928 + 1 * jax.random.normal(jax.random.fold_in(_rk, 1), (4, 256, 256), jnp.float32)
        _lenS = 256 - jax.random.randint(jax.random.fold_in(_rk, 7), (4,), 0, max(1, 256 // 4) + 1, jnp.int32)
        _lenS2 = 64 - jax.random.randint(jax.random.fold_in(_rk, 8), (4,), 0, max(1, 64 // 4) + 1, jnp.int32)
        _ctx_512P = jax.random.normal(jax.random.fold_in(_rk, 11), (4, 16, 64), jnp.float32)
        _ctx_512c = jax.random.dirichlet(jax.random.fold_in(_rk, 511), 0.3 * jnp.ones((16,), jnp.float32), (4, 64))
        _ctx_512t = jnp.einsum('bsk,bkd->bsd', _ctx_512c, _ctx_512P)
        _ctx_512t = _ctx_512t * jax.lax.rsqrt(jnp.mean(jnp.square(_ctx_512t)) + 1e-12) * 0.953939
        ctx_512 = 0.000227908 + 0.99994 * (_ctx_512t + 0.3 * jax.random.normal(jax.random.fold_in(_rk, 611), (4, 64, 64), jnp.float32))
        _g = jax.random.normal(jax.random.fold_in(_rk, 9001), (2, 4), jnp.float32)
        _g = jnp.sign(_g) * jnp.maximum(jnp.abs(_g), 1.0) + (_g == 0) * 1.0
        g_xattn = _g[0]
        g_ffn = _g[1]
        return (x, ctx_512, g_xattn, g_ffn)
    x, ctx_512, g_xattn, g_ffn = _rec_inputs()

    def _L0_xattn_setup():
        import jax, jax.numpy as jnp
        import numpy as np
        B, S, L = (2, 128, 128)
        DIM_Q, H, K, D_C, D_CQ, R = (256, 16, 128, 64, 192, 64)

        def _rope_tables(length, dim):
            inv = 1.0 / 10000.0 ** (jnp.arange(0, dim, 2, dtype=jnp.float32) / dim)
            f = jnp.arange(length, dtype=jnp.float32)[:, None] * inv[None, :]
            sin = jnp.repeat(jnp.sin(f), 2, axis=-1)
            cos = jnp.repeat(jnp.cos(f), 2, axis=-1)
            return (sin, cos)

        def _rotate_half(x):
            half = x.shape[-1] // 2
            return jnp.concatenate([-x[..., half:], x[..., :half]], axis=-1)

        def _apply_rope(x, sin, cos):
            return x * cos + _rotate_half(x) * sin
        key = jax.random.key(seed)
        ks = jax.random.split(key, 8)
        return {'hidden_q': jax.random.normal(ks[0], (B, S, DIM_Q), jnp.float32), 'kv_c': jax.random.normal(ks[1], (B, L, D_C), jnp.float32), 'Wq': jax.random.normal(ks[2], (H * K, DIM_Q), jnp.float32) / np.sqrt(DIM_Q).astype(np.float32), 'w_kc_q': jax.random.normal(ks[3], (H, K, D_CQ), jnp.float32) / np.sqrt(K).astype(np.float32), 'w_kc_kv': jax.random.normal(ks[4], (H, K, D_C), jnp.float32) / np.sqrt(K).astype(np.float32), 'W_qr': jax.random.normal(ks[5], (H, D_CQ, R), jnp.float32) / np.float32(np.sqrt(D_CQ) * np.sqrt(R)), 'W_kr': jax.random.normal(ks[6], (H, D_C, R), jnp.float32) / np.sqrt(D_C).astype(np.float32), 'Wo': jax.random.normal(ks[7], (DIM_Q, H * K), jnp.float32) / np.sqrt(H * K).astype(np.float32)}
    _L0_xattn_all = _L0_xattn_setup()
    _L0_xattn_in = {k: v for k, v in _L0_xattn_all.items() if k in ('Wq', 'w_kc_q', 'w_kc_kv', 'W_qr', 'W_kr', 'Wo')}
    del _L0_xattn_all

    def _L0_ffn_setup():
        import jax, jax.numpy as jnp
        import numpy as np
        E = 16
        D = 256
        H = 176
        HS = 2 * 176
        TOP_K = 6
        ROUTE_SCALE = 1.0
        key = jax.random.key(seed)
        ks = jax.random.split(key, 16)
        s = 0.02
        return {'x': jax.random.normal(ks[0], (4, 128, D), dtype=jnp.float32), 'gate_w': jax.random.normal(ks[1], (E, D), dtype=jnp.float32) * s, 'gate_b': jax.random.normal(ks[2], (E,), dtype=jnp.float32) * s, 'w1': jax.random.normal(ks[3], (E, H, D), dtype=jnp.float32) * s, 'b1': jax.random.normal(ks[4], (E, H), dtype=jnp.float32) * s, 'w2': jax.random.normal(ks[5], (E, D, H), dtype=jnp.float32) * s, 'b2': jax.random.normal(ks[6], (E, D), dtype=jnp.float32) * s, 'w3': jax.random.normal(ks[7], (E, H, D), dtype=jnp.float32) * s, 'b3': jax.random.normal(ks[8], (E, H), dtype=jnp.float32) * s, 'ws1': jax.random.normal(ks[9], (HS, D), dtype=jnp.float32) * s, 'bs1': jax.random.normal(ks[10], (HS,), dtype=jnp.float32) * s, 'ws2': jax.random.normal(ks[11], (D, HS), dtype=jnp.float32) * s, 'bs2': jax.random.normal(ks[12], (D,), dtype=jnp.float32) * s, 'ws3': jax.random.normal(ks[13], (HS, D), dtype=jnp.float32) * s, 'bs3': jax.random.normal(ks[14], (HS,), dtype=jnp.float32) * s}
    _L0_ffn_all = _L0_ffn_setup()
    _L0_ffn_in = {k: v for k, v in _L0_ffn_all.items() if k in ('gate_w', 'gate_b', 'w1', 'b1', 'w2', 'b2', 'w3', 'b3', 'ws1', 'bs1', 'ws2', 'bs2', 'ws3', 'bs3')}
    del _L0_ffn_all

    def _L1_xattn_setup():
        import jax, jax.numpy as jnp
        import numpy as np
        B, S, L = (2, 128, 128)
        DIM_Q, H, K, D_C, D_CQ, R = (256, 16, 128, 64, 192, 64)

        def _rope_tables(seq_len, dim, dtype):
            inv_freq = 1.0 / 10000.0 ** (jnp.arange(0, dim, 2, dtype=dtype) / dim)
            t = jnp.arange(seq_len, dtype=dtype)
            freqs = t[:, None] * inv_freq[None, :]
            sin = jnp.repeat(jnp.sin(freqs), 2, axis=-1)
            cos = jnp.repeat(jnp.cos(freqs), 2, axis=-1)
            return (sin, cos)

        def _rotate_half(x):
            h = x.shape[-1] // 2
            return jnp.concatenate([-x[..., h:], x[..., :h]], axis=-1)
        key = jax.random.key(seed)
        ks = jax.random.split(key, 8)
        s_in = 1.0 / np.sqrt(DIM_Q)
        s_k = 1.0 / np.sqrt(K)
        s_cq = 1.0 / np.sqrt(D_CQ)
        s_c = 1.0 / np.sqrt(D_C)
        return {'hidden_q': jax.random.normal(ks[0], (B, S, DIM_Q), jnp.float32), 'kv_c': jax.random.normal(ks[1], (B, L, D_C), jnp.float32), 'Wq': jax.random.normal(ks[2], (H * K, DIM_Q), jnp.float32) * s_in, 'w_kc_q': jax.random.normal(ks[3], (H, K, D_CQ), jnp.float32) * s_k, 'w_kc_kv': jax.random.normal(ks[4], (H, K, D_C), jnp.float32) * s_k, 'W_qr': jax.random.normal(ks[5], (H, D_CQ, R), jnp.float32) * s_cq / np.sqrt(R), 'W_kr': jax.random.normal(ks[6], (H, D_C, R), jnp.float32) * s_c, 'Wo': jax.random.normal(ks[7], (DIM_Q, H * K), jnp.float32) * s_k}
    _L1_xattn_all = _L1_xattn_setup()
    _L1_xattn_in = {k: v for k, v in _L1_xattn_all.items() if k in ('Wq', 'w_kc_q', 'w_kc_kv', 'W_qr', 'W_kr', 'Wo')}
    del _L1_xattn_all

    def _L1_ffn_setup():
        import jax, jax.numpy as jnp
        import numpy as np
        D_MODEL = 256
        D_FF = 1024

        def absmean_quant(w):
            scale = jnp.mean(jnp.abs(w))
            mask = (jnp.abs(w) >= scale * 0.7).astype(w.dtype)
            return jnp.sign(w) * mask
        key = jax.random.key(seed)
        k_x, k_w1, k_w2 = jax.random.split(key, 3)
        x = jax.random.normal(k_x, (4, 512, D_MODEL), dtype=jnp.float32)
        w1 = jax.random.normal(k_w1, (D_FF, D_MODEL), dtype=jnp.float32)
        b1 = jnp.zeros((D_FF,), dtype=jnp.float32)
        w2 = jax.random.normal(k_w2, (D_MODEL, D_FF), dtype=jnp.float32)
        b2 = jnp.zeros((D_MODEL,), dtype=jnp.float32)
        return {'x': x, 'w1': w1, 'b1': b1, 'w2': w2, 'b2': b2}
    _L1_ffn_all = _L1_ffn_setup()
    _L1_ffn_in = {k: v for k, v in _L1_ffn_all.items() if k in ('w1', 'b1', 'w2', 'b2')}
    del _L1_ffn_all

    def _L2_xattn_setup():
        import jax, jax.numpy as jnp
        import numpy as np
        B, S, H, NH, L = (2, 256, 256, 16, 64)
        HD = H // NH
        key = jax.random.key(seed)
        k1, k2, k3, k4, k5 = jax.random.split(key, 5)
        scale = 0.02
        return {'q': jax.random.normal(k1, (B, S, H), dtype=jnp.float32), 'latent_kv': jax.random.normal(k2, (B, S, L), dtype=jnp.float32), 'Wq': jax.random.normal(k3, (H, H), dtype=jnp.float32) * scale, 'Wkv_expand': jax.random.normal(k4, (2 * H, L), dtype=jnp.float32) * scale, 'Wout': jax.random.normal(k5, (H, H), dtype=jnp.float32) * scale}
    _L2_xattn_all = _L2_xattn_setup()
    _L2_xattn_in = {k: v for k, v in _L2_xattn_all.items() if k in ('Wq', 'Wkv_expand', 'Wout')}
    del _L2_xattn_all

    def _L2_ffn_setup():
        import jax, jax.numpy as jnp
        import numpy as np
        QMAX = 127.0
        QMIN = -128.0
        key = jax.random.key(seed)
        k1, k2, k3 = jax.random.split(key, 3)
        B, N, D, O = (4, 512, 256, 256)
        x = jax.random.normal(k1, (B, N, D), dtype=jnp.float32)
        weight = jax.random.normal(k2, (O, D), dtype=jnp.float32)
        bias = jax.random.normal(k3, (O,), dtype=jnp.float32)
        return {'x': x, 'weight': weight, 'bias': bias}
    _L2_ffn_all = _L2_ffn_setup()
    _L2_ffn_in = {k: v for k, v in _L2_ffn_all.items() if k in ('weight', 'bias')}
    del _L2_ffn_all

    def _L3_xattn_setup():
        import jax, jax.numpy as jnp
        import numpy as np
        B, S, H, NH, L = (2, 256, 256, 16, 64)
        HD = H // NH
        key = jax.random.key(seed)
        k1, k2, k3, k4, k5 = jax.random.split(key, 5)
        scale = 0.02
        return {'q': jax.random.normal(k1, (B, S, H), dtype=jnp.float32), 'latent_kv': jax.random.normal(k2, (B, S, L), dtype=jnp.float32), 'Wq': jax.random.normal(k3, (H, H), dtype=jnp.float32) * scale, 'Wkv_expand': jax.random.normal(k4, (2 * H, L), dtype=jnp.float32) * scale, 'Wout': jax.random.normal(k5, (H, H), dtype=jnp.float32) * scale}
    _L3_xattn_all = _L3_xattn_setup()
    _L3_xattn_in = {k: v for k, v in _L3_xattn_all.items() if k in ('Wq', 'Wkv_expand', 'Wout')}
    del _L3_xattn_all

    def _L3_ffn_setup():
        import jax, jax.numpy as jnp
        import numpy as np
        from jax import lax
        E = 8
        K = 2
        H = 256
        I = 512
        B, S = (2, 256)
        SCALE = 0.02

        def _silu_and_mul(gu):
            g, u = jnp.split(gu, 2, axis=-1)
            return jax.nn.silu(g) * u
        key = jax.random.key(seed)
        ks = jax.random.split(key, 6)
        return {'hidden_states': jax.random.normal(ks[0], (B, S, H), dtype=jnp.float32), 'gate_w': jax.random.normal(ks[1], (H, E), dtype=jnp.float32) * SCALE, 'w_gate_up': jax.random.normal(ks[2], (E, H, 2 * I), dtype=jnp.float32) * SCALE, 'w_down': jax.random.normal(ks[3], (E, I, H), dtype=jnp.float32) * SCALE, 'shared_gate_up': jax.random.normal(ks[4], (H, 2 * I), dtype=jnp.float32) * SCALE, 'shared_down': jax.random.normal(ks[5], (I, H), dtype=jnp.float32) * SCALE}
    _L3_ffn_all = _L3_ffn_setup()
    _L3_ffn_in = {k: v for k, v in _L3_ffn_all.items() if k in ('gate_w', 'w_gate_up', 'w_down', 'shared_gate_up', 'shared_down')}
    del _L3_ffn_all
    return {'x': x, 'ctx_512': ctx_512, 'g_xattn': g_xattn, 'g_ffn': g_ffn, 'L0_xattn_Wq': _L0_xattn_in['Wq'], 'L0_xattn_w_kc_q': _L0_xattn_in['w_kc_q'], 'L0_xattn_w_kc_kv': _L0_xattn_in['w_kc_kv'], 'L0_xattn_W_qr': _L0_xattn_in['W_qr'], 'L0_xattn_W_kr': _L0_xattn_in['W_kr'], 'L0_xattn_Wo': _L0_xattn_in['Wo'], 'L0_ffn_gate_w': _L0_ffn_in['gate_w'], 'L0_ffn_gate_b': _L0_ffn_in['gate_b'], 'L0_ffn_w1': _L0_ffn_in['w1'], 'L0_ffn_b1': _L0_ffn_in['b1'], 'L0_ffn_w2': _L0_ffn_in['w2'], 'L0_ffn_b2': _L0_ffn_in['b2'], 'L0_ffn_w3': _L0_ffn_in['w3'], 'L0_ffn_b3': _L0_ffn_in['b3'], 'L0_ffn_ws1': _L0_ffn_in['ws1'], 'L0_ffn_bs1': _L0_ffn_in['bs1'], 'L0_ffn_ws2': _L0_ffn_in['ws2'], 'L0_ffn_bs2': _L0_ffn_in['bs2'], 'L0_ffn_ws3': _L0_ffn_in['ws3'], 'L0_ffn_bs3': _L0_ffn_in['bs3'], 'L1_xattn_Wq': _L1_xattn_in['Wq'], 'L1_xattn_w_kc_q': _L1_xattn_in['w_kc_q'], 'L1_xattn_w_kc_kv': _L1_xattn_in['w_kc_kv'], 'L1_xattn_W_qr': _L1_xattn_in['W_qr'], 'L1_xattn_W_kr': _L1_xattn_in['W_kr'], 'L1_xattn_Wo': _L1_xattn_in['Wo'], 'L1_ffn_w1': _L1_ffn_in['w1'], 'L1_ffn_b1': _L1_ffn_in['b1'], 'L1_ffn_w2': _L1_ffn_in['w2'], 'L1_ffn_b2': _L1_ffn_in['b2'], 'L2_xattn_Wq': _L2_xattn_in['Wq'], 'L2_xattn_Wkv_expand': _L2_xattn_in['Wkv_expand'], 'L2_xattn_Wout': _L2_xattn_in['Wout'], 'L2_ffn_weight': _L2_ffn_in['weight'], 'L2_ffn_bias': _L2_ffn_in['bias'], 'L3_xattn_Wq': _L3_xattn_in['Wq'], 'L3_xattn_Wkv_expand': _L3_xattn_in['Wkv_expand'], 'L3_xattn_Wout': _L3_xattn_in['Wout'], 'L3_ffn_gate_w': _L3_ffn_in['gate_w'], 'L3_ffn_w_gate_up': _L3_ffn_in['w_gate_up'], 'L3_ffn_w_down': _L3_ffn_in['w_down'], 'L3_ffn_shared_gate_up': _L3_ffn_in['shared_gate_up'], 'L3_ffn_shared_down': _L3_ffn_in['shared_down']}

def reference(x, ctx_512, g_xattn, g_ffn, L0_xattn_Wq, L0_xattn_w_kc_q, L0_xattn_w_kc_kv, L0_xattn_W_qr, L0_xattn_W_kr, L0_xattn_Wo, L0_ffn_gate_w, L0_ffn_gate_b, L0_ffn_w1, L0_ffn_b1, L0_ffn_w2, L0_ffn_b2, L0_ffn_w3, L0_ffn_b3, L0_ffn_ws1, L0_ffn_bs1, L0_ffn_ws2, L0_ffn_bs2, L0_ffn_ws3, L0_ffn_bs3, L1_xattn_Wq, L1_xattn_w_kc_q, L1_xattn_w_kc_kv, L1_xattn_W_qr, L1_xattn_W_kr, L1_xattn_Wo, L1_ffn_w1, L1_ffn_b1, L1_ffn_w2, L1_ffn_b2, L2_xattn_Wq, L2_xattn_Wkv_expand, L2_xattn_Wout, L2_ffn_weight, L2_ffn_bias, L3_xattn_Wq, L3_xattn_Wkv_expand, L3_xattn_Wout, L3_ffn_gate_w, L3_ffn_w_gate_up, L3_ffn_w_down, L3_ffn_shared_gate_up, L3_ffn_shared_down):
    import jax
    import jax.numpy as jnp

    def _L0_xattn_ref(hidden_q, kv_c, Wq, w_kc_q, w_kc_kv, W_qr, W_kr, Wo):
        import jax, jax.numpy as jnp
        import numpy as np
        B, S, L = (2, 128, 128)
        DIM_Q, H, K, D_C, D_CQ, R = (256, 16, 128, 64, 192, 64)

        def _rope_tables(length, dim):
            inv = 1.0 / 10000.0 ** (jnp.arange(0, dim, 2, dtype=jnp.float32) / dim)
            f = jnp.arange(length, dtype=jnp.float32)[:, None] * inv[None, :]
            sin = jnp.repeat(jnp.sin(f), 2, axis=-1)
            cos = jnp.repeat(jnp.cos(f), 2, axis=-1)
            return (sin, cos)

        def _rotate_half(x):
            half = x.shape[-1] // 2
            return jnp.concatenate([-x[..., half:], x[..., :half]], axis=-1)

        def _apply_rope(x, sin, cos):
            return x * cos + _rotate_half(x) * sin
        Bv, Sv, _ = hidden_q.shape
        _, Lv, _ = kv_c.shape
        q_hk = (hidden_q @ Wq.T).reshape(Bv, Sv, H, K)
        q_big = jnp.einsum('bshk,hkq->bshq', q_hk, w_kc_q)
        sin_q, cos_q = _rope_tables(Sv, D_CQ)
        q_big = _apply_rope(q_big, sin_q[None, :, None, :], cos_q[None, :, None, :])
        sin_k, cos_k = _rope_tables(Lv, D_C)
        kv_r = _apply_rope(kv_c, sin_k[None], cos_k[None])
        q_r = jnp.einsum('bshq,hqr->bhsr', q_big, W_qr)
        k_r = jnp.einsum('bld,hdr->bhlr', kv_r, W_kr)
        scores = jnp.einsum('bhsr,bhlr->bhsl', q_r, k_r)
        attn = jax.nn.softmax(scores, axis=-1)
        ctx_c = jnp.einsum('bhsl,bld->bhsd', attn, kv_r)
        ctx_lat = jnp.einsum('bhsd,hkd->bhsk', ctx_c, w_kc_kv)
        ctx = ctx_lat.transpose(0, 2, 1, 3).reshape(Bv, Sv, H * K)
        return ctx @ Wo.T

    def _L0_ffn_ref(x, gate_w, gate_b, w1, b1, w2, b2, w3, b3, ws1, bs1, ws2, bs2, ws3, bs3):
        import jax, jax.numpy as jnp
        import numpy as np
        E = 16
        D = 256
        H = 176
        HS = 2 * 176
        TOP_K = 6
        ROUTE_SCALE = 1.0
        shape = x.shape
        xf = x.reshape(-1, shape[-1])
        scores = xf @ gate_w.T
        probs = jax.nn.softmax(scores.astype(jnp.float32), axis=-1)
        biased = probs + gate_b
        _, idx = jax.lax.top_k(biased, TOP_K)
        weights = jnp.take_along_axis(probs, idx, axis=1) * ROUTE_SCALE
        weights = weights.astype(x.dtype)
        onehot = jax.nn.one_hot(idx, E, dtype=weights.dtype)
        cw = jnp.einsum('tk,tke->te', weights, onehot)

        def expert_step(y, params):
            W1, B1, W2, B2, W3, B3, c = params
            h = jax.nn.silu(xf @ W1.T + B1) * (xf @ W3.T + B3)
            out = h @ W2.T + B2
            return (y + c[:, None] * out, None)
        y0 = jnp.zeros_like(xf)
        y, _ = jax.lax.scan(expert_step, y0, (w1, b1, w2, b2, w3, b3, cw.T))
        z = jax.nn.silu(xf @ ws1.T + bs1) * (xf @ ws3.T + bs3) @ ws2.T + bs2
        return (y + z).reshape(shape)

    def _L1_xattn_ref(hidden_q, kv_c, Wq, w_kc_q, w_kc_kv, W_qr, W_kr, Wo):
        import jax, jax.numpy as jnp
        import numpy as np
        B, S, L = (2, 128, 128)
        DIM_Q, H, K, D_C, D_CQ, R = (256, 16, 128, 64, 192, 64)

        def _rope_tables(seq_len, dim, dtype):
            inv_freq = 1.0 / 10000.0 ** (jnp.arange(0, dim, 2, dtype=dtype) / dim)
            t = jnp.arange(seq_len, dtype=dtype)
            freqs = t[:, None] * inv_freq[None, :]
            sin = jnp.repeat(jnp.sin(freqs), 2, axis=-1)
            cos = jnp.repeat(jnp.cos(freqs), 2, axis=-1)
            return (sin, cos)

        def _rotate_half(x):
            h = x.shape[-1] // 2
            return jnp.concatenate([-x[..., h:], x[..., :h]], axis=-1)
        b, s, _ = hidden_q.shape
        l = kv_c.shape[1]
        q_hk = (hidden_q @ Wq.T).reshape(b, s, H, K)
        q_big = jnp.einsum('bshk,hkq->bshq', q_hk, w_kc_q)
        sin, cos = _rope_tables(l, D_C, kv_c.dtype)
        kv_rope = kv_c * cos[None] + _rotate_half(kv_c) * sin[None]
        q_r = jnp.einsum('bshq,hqr->bhsr', q_big, W_qr)
        k_r = jnp.einsum('bld,hdr->bhlr', kv_rope, W_kr)
        scores = jnp.einsum('bhsr,bhlr->bhsl', q_r, k_r)
        attn = jax.nn.softmax(scores, axis=-1)
        ctx_c = jnp.einsum('bhsl,bld->bhsd', attn, kv_rope)
        ctx_lat = jnp.einsum('bhsd,hkd->bshk', ctx_c, w_kc_kv)
        out = ctx_lat.reshape(b, s, H * K) @ Wo.T
        return out

    def _L1_ffn_ref(x, w1, b1, w2, b2):
        import jax, jax.numpy as jnp
        import numpy as np
        D_MODEL = 256
        D_FF = 1024

        def absmean_quant(w):
            scale = jnp.mean(jnp.abs(w))
            mask = (jnp.abs(w) >= scale * 0.7).astype(w.dtype)
            return jnp.sign(w) * mask
        w1_q = absmean_quant(w1)
        w2_q = absmean_quant(w2)
        h = jnp.einsum('bsd,fd->bsf', x, w1_q) + b1
        h = jax.nn.gelu(h, approximate=False)
        out = jnp.einsum('bsf,df->bsd', h, w2_q) + b2
        return out

    def _L2_xattn_ref(q, latent_kv, Wq, Wkv_expand, Wout):
        import jax, jax.numpy as jnp
        import numpy as np
        B, S, H, NH, L = (2, 256, 256, 16, 64)
        HD = H // NH
        b, sq, _ = q.shape
        sk = latent_kv.shape[1]
        qp = q @ Wq.T
        kv = latent_kv @ Wkv_expand.T
        k, v = jnp.split(kv, 2, axis=-1)
        qh = qp.reshape(b, sq, NH, HD).transpose(0, 2, 1, 3)
        kh = k.reshape(b, sk, NH, HD).transpose(0, 2, 1, 3)
        vh = v.reshape(b, sk, NH, HD).transpose(0, 2, 1, 3)
        inv_sqrt_d = 1.0 / jnp.sqrt(jnp.float32(HD))
        scores = jnp.einsum('bhqd,bhkd->bhqk', qh, kh) * inv_sqrt_d
        causal = jnp.tril(jnp.ones((sq, sk), dtype=bool))
        scores = jnp.where(causal, scores, jnp.finfo(scores.dtype).min)
        attn = jax.nn.softmax(scores, axis=-1)
        out = jnp.einsum('bhqk,bhkd->bhqd', attn, vh)
        out = out.transpose(0, 2, 1, 3).reshape(b, sq, H)
        return out @ Wout.T

    def _L2_ffn_ref(x, weight, bias):
        import jax, jax.numpy as jnp
        import numpy as np
        QMAX = 127.0
        QMIN = -128.0
        w_max = jnp.clip(jnp.max(jnp.abs(weight), axis=1, keepdims=True), 1e-08, None)
        w_scale = w_max / QMAX
        w_q = jnp.clip(jnp.round(weight / w_scale), QMIN, QMAX).astype(jnp.int8)
        w_scale = w_scale.squeeze(1).astype(jnp.float32)
        x_max = jnp.max(jnp.abs(x), axis=2, keepdims=True)
        x_scale = jnp.maximum(x_max / QMAX, 1e-12)
        x_q = jnp.clip(jnp.round(x / x_scale), QMIN, QMAX).astype(jnp.int8)
        acc = jnp.einsum('bnd,od->bno', x_q.astype(jnp.int32), w_q.astype(jnp.int32))
        y = acc.astype(jnp.float32) * x_scale.astype(jnp.float32) * w_scale[None, None, :]
        y = y + bias
        return y.astype(x.dtype)

    def _L3_xattn_ref(q, latent_kv, Wq, Wkv_expand, Wout):
        import jax, jax.numpy as jnp
        import numpy as np
        B, S, H, NH, L = (2, 256, 256, 16, 64)
        HD = H // NH
        b, sq, _ = q.shape
        sk = latent_kv.shape[1]
        qp = q @ Wq.T
        kv = latent_kv @ Wkv_expand.T
        k, v = jnp.split(kv, 2, axis=-1)
        qh = qp.reshape(b, sq, NH, HD).transpose(0, 2, 1, 3)
        kh = k.reshape(b, sk, NH, HD).transpose(0, 2, 1, 3)
        vh = v.reshape(b, sk, NH, HD).transpose(0, 2, 1, 3)
        inv_sqrt_d = 1.0 / jnp.sqrt(jnp.float32(HD))
        scores = jnp.einsum('bhqd,bhkd->bhqk', qh, kh) * inv_sqrt_d
        causal = jnp.tril(jnp.ones((sq, sk), dtype=bool))
        scores = jnp.where(causal, scores, jnp.finfo(scores.dtype).min)
        attn = jax.nn.softmax(scores, axis=-1)
        out = jnp.einsum('bhqk,bhkd->bhqd', attn, vh)
        out = out.transpose(0, 2, 1, 3).reshape(b, sq, H)
        return out @ Wout.T

    def _L3_ffn_ref(hidden_states, gate_w, w_gate_up, w_down, shared_gate_up, shared_down):
        import jax, jax.numpy as jnp
        import numpy as np
        from jax import lax
        E = 8
        K = 2
        H = 256
        I = 512
        B, S = (2, 256)
        SCALE = 0.02

        def _silu_and_mul(gu):
            g, u = jnp.split(gu, 2, axis=-1)
            return jax.nn.silu(g) * u
        orig_shape = hidden_states.shape
        x = hidden_states.reshape(-1, orig_shape[-1])
        shared_out = _silu_and_mul(x @ shared_gate_up) @ shared_down
        router_logits = x @ gate_w
        probs = jax.nn.softmax(router_logits, axis=-1)
        topk_w, topk_i = lax.top_k(probs, K)
        topk_w = topk_w / jnp.sum(topk_w, axis=-1, keepdims=True)
        combine = jnp.sum(jax.nn.one_hot(topk_i, E, dtype=x.dtype) * topk_w[..., None], axis=1)

        def body(acc, we):
            wg, wd, cw = we
            h = _silu_and_mul(x @ wg) @ wd
            return (acc + cw[:, None] * h, None)
        moe_out, _ = lax.scan(body, jnp.zeros_like(x), (w_gate_up, w_down, combine.T))
        return (moe_out + shared_out).reshape(orig_shape)
    x = x + jnp.tanh(g_xattn[0]) * _L0_xattn_ref(_layernorm(x, axis=-1), ctx_512, L0_xattn_Wq, L0_xattn_w_kc_q, L0_xattn_w_kc_kv, L0_xattn_W_qr, L0_xattn_W_kr, L0_xattn_Wo)
    x = x + jnp.tanh(g_ffn[0]) * _L0_ffn_ref(_layernorm(x, axis=-1), L0_ffn_gate_w, L0_ffn_gate_b, L0_ffn_w1, L0_ffn_b1, L0_ffn_w2, L0_ffn_b2, L0_ffn_w3, L0_ffn_b3, L0_ffn_ws1, L0_ffn_bs1, L0_ffn_ws2, L0_ffn_bs2, L0_ffn_ws3, L0_ffn_bs3)
    x = x + jnp.tanh(g_xattn[1]) * _L1_xattn_ref(_layernorm(x, axis=-1), ctx_512, L1_xattn_Wq, L1_xattn_w_kc_q, L1_xattn_w_kc_kv, L1_xattn_W_qr, L1_xattn_W_kr, L1_xattn_Wo)
    x = x + jnp.tanh(g_ffn[1]) * _L1_ffn_ref(_layernorm(x, axis=-1), L1_ffn_w1, L1_ffn_b1, L1_ffn_w2, L1_ffn_b2)
    x = x + jnp.tanh(g_xattn[2]) * _L2_xattn_ref(_layernorm(x, axis=-1), ctx_512, L2_xattn_Wq, L2_xattn_Wkv_expand, L2_xattn_Wout)
    x = x + jnp.tanh(g_ffn[2]) * _L2_ffn_ref(_layernorm(x, axis=-1), L2_ffn_weight, L2_ffn_bias)
    x = x + jnp.tanh(g_xattn[3]) * _L3_xattn_ref(_layernorm(x, axis=-1), ctx_512, L3_xattn_Wq, L3_xattn_Wkv_expand, L3_xattn_Wout)
    x = x + jnp.tanh(g_ffn[3]) * _L3_ffn_ref(_layernorm(x, axis=-1), L3_ffn_gate_w, L3_ffn_w_gate_up, L3_ffn_w_down, L3_ffn_shared_gate_up, L3_ffn_shared_down)
    return x

_drawn_inputs = setup_inputs


def setup_inputs(seed=0):
    import zlib

    import numpy as np

    out = dict(_drawn_inputs(seed))
    spreads = {'L1_ffn_b1': (0.0, 0.8), 'L1_ffn_b2': (0.0, 2.0)}
    factors = {'L0_ffn_gate_w': 8.0,
     'L0_ffn_gate_b': 8.0,
     'L0_ffn_w1': 8.0,
     'L0_ffn_b1': 8.0,
     'L0_ffn_w2': 8.0,
     'L0_ffn_b2': 30.542,
     'L0_ffn_w3': 8.0,
     'L0_ffn_b3': 8.0,
     'L0_ffn_ws1': 4.971,
     'L0_ffn_bs1': 8.0,
     'L0_ffn_ws2': 4.864,
     'L0_ffn_bs2': 18.563,
     'L0_ffn_ws3': 4.896,
     'L0_ffn_bs3': 8.0,
     'L2_xattn_Wq': 52.361,
     'L2_xattn_Wkv_expand': 39.223,
     'L2_xattn_Wout': 38.582,
     'L2_ffn_bias': 8.0,
     'L3_xattn_Wq': 52.426,
     'L3_xattn_Wkv_expand': 39.536,
     'L3_xattn_Wout': 38.763,
     'L3_ffn_gate_w': 8.0,
     'L3_ffn_w_gate_up': 8.0,
     'L3_ffn_w_down': 8.0,
     'L3_ffn_shared_gate_up': 8.0,
     'L3_ffn_shared_down': 8.0}
    for name, (base, spread) in spreads.items():
        noise = np.random.default_rng([zlib.crc32(name.encode()), seed]).standard_normal(out[name].shape)
        drawn = base * np.exp(spread * noise) if base else spread * noise
        out[name] = jnp.asarray(drawn.astype(out[name].dtype))
    for name, factor in factors.items():
        out[name] = (out[name] * factor).astype(out[name].dtype)
    return out
```

```python
from contextlib import ExitStack

import numpy as np

import concourse.bass as bass
from concourse import mybir

P = 128
F32 = mybir.dt.float32
F32R = mybir.dt.float32r
BF16 = mybir.dt.bfloat16
ALU = mybir.AluOpType
ACT = mybir.ActivationFunctionType
AX = mybir.AxisListType.X

B, S, D = 4, 256, 256
L, DC = 64, 64
T = B * S // P
TB = S // P
KD = D // P
H = 16
NP = H // 2
HALF = B * S // 2
MAGIC = 12582912.0
FMIN = float(np.finfo(np.float32).min)

ROT, CQ, R, K = 96, 192, 64, 128
O_WQ = 0
O_CQ = O_WQ + 2 * D
CQ_N = {0: 2 * CQ, 1: 2 * 2 * K}


def pair_columns(layer):
    o_qr = O_CQ + CQ_N[layer]
    o_kr = o_qr + 2 * CQ
    o_ck = o_kr + 2 * R
    o_wo = o_ck + 2 * 2 * DC
    return o_qr, o_kr, o_ck, o_wo, o_wo + 2 * D


class Count:

    def __init__(self, sem):
        self.sem, self.n, self.grow = sem, 0, None

    def inc(self, ins):
        ins.then_inc(self.sem, 1)
        self.n += 1
        return self.n

    def wait(self, eng, n=None):
        n = self.n if n is None else n
        eng.wait_ge(self.sem, n if self.grow is None else self.grow[0] * self.grow[1] + n)

    def inside(self, i, per):
        self.grow, self.start = (i, per), self.n

    def outside(self, trips):
        assert self.n - self.start == self.grow[1]
        self.n = self.start + self.grow[1] * trips
        self.grow = None


def mm3(pe, out, a, b, first=True, last=True):
    pe.matmul(out, a[0], b[0], start=first, stop=False)
    pe.matmul(out, a[0], b[1], start=False, stop=False)
    return pe.matmul(out, a[1], b[0], start=False, stop=last)


def program(nc, A, out):
    with ExitStack() as top:
        phase = [""]

        def sbuf(ctx, name, shape, dt=F32):
            return ctx.enter_context(nc.sbuf_tensor(phase[0] + name, shape, dt))

        def split(ctx, name, shape):
            return sbuf(ctx, name + "_hi", shape, F32R), sbuf(ctx, name + "_lo", shape, F32R)

        def psum(ctx, name, shape, dt=F32):
            return ctx.enter_context(nc.psum_tensor(phase[0] + name, shape, dt))

        used = []

        def sem(ctx, name):
            used.append(nc.alloc_semaphore(phase[0] + name))
            return used[-1]

        def clear_semaphores():
            nc.clear_and_free_semaphores(list(used))
            nc.all_engine_barrier()
            used.clear()

        X = sbuf(top, "X", [P, T, D])
        XN = sbuf(top, "XN", [P, T, D])
        XT = split(top, "XT", [P, KD, B * S])
        IDENT = sbuf(top, "IDENT", [P, P])
        IDENTB = sbuf(top, "IDENTB", [P, P], BF16)
        ONES = sbuf(top, "ONES", [P, P])
        EPS = sbuf(top, "EPS", [P, 1])
        GATE = sbuf(top, "GATE", [P, 8])
        STATS = sbuf(top, "STATS", [P, T, 6])
        MOM = sbuf(top, "MOM", [P, T, 2])
        STD = sbuf(top, "STD", [P, T])
        RSTD = sbuf(top, "RSTD", [P, T])
        KV = split(top, "KV", [P, B * L])
        KVB = split(top, "KVB", [P, B, 2 * L])

        xt = (XT[0], XT[1])

        with ExitStack() as ctx:
            kvt = sbuf(ctx, "kvt", [P, B * L])
            kvs = sbuf(ctx, "kvs", [P, B * L])
            kcos = sbuf(ctx, "kcos", [P, B * L])
            ksin = sbuf(ctx, "ksin", [P, B * L])
            prod = sbuf(ctx, "prod", [P, 2, B * L])
            graw = sbuf(ctx, "graw", [P, 8])
            loaded = sem(ctx, "loaded")
            x_loaded = sem(ctx, "x_loaded")
            gates_done = sem(ctx, "gates_done")
            rope = Count(sem(ctx, "rope_done"))
            with nc.Block() as block:
                @block.sync
                def _(sp):
                    for dst, src in ((graw, "gates"), (IDENT, "ident"), (kvt, "kvT"), (kvs, "kvT_swapped"), (kcos, "kcos"), (ksin, "ksin")):
                        sp.dma_start(dst[:, :], A[src]).then_inc(loaded, 16)
                    sp.dma_start(X[:, :, :], A["x"].rearrange("(t p) d -> p t d", p=P)).then_inc(x_loaded, 16)
                    sp.wait_ge(x_loaded, 16)

                @block.scalar
                def _(act):
                    act.wait_ge(loaded, 96)
                    act.activation(GATE[:, :], graw[:, :], ACT.Tanh).then_inc(gates_done, 1)

                @block.gpsimd
                def _(pool):
                    pool.memset(EPS[:, :], 1e-5)
                    pool.memset(ONES[:, :], 1.0)

                @block.vector
                def _(dve):
                    for part in KVB:
                        rope.inc(dve.memset(part[:, :, :].bitcast(F32), 0.0))
                    dve.wait_ge(loaded, 96)
                    rope.inc(dve.tensor_copy(IDENTB[:, :], IDENT[:, :]))
                    rope.inc(dve.tensor_tensor(prod[:, 0, :], kvt[:, :], kcos[:, :], ALU.mult))
                    rope.inc(dve.tensor_tensor(prod[:, 1, :], kvs[:, :], ksin[:, :], ALU.mult))
                    rope.wait(dve)
                    rope.inc(dve.tensor_tensor(kvt[:, :], prod[:, 0, :], prod[:, 1, :], ALU.add))
                    rope.wait(dve)
                    rope.inc(dve.tensor_copy(KV[0][:, :], kvt[:, :]))
                    rope.wait(dve)
                    rope.inc(dve.tensor_tensor(KV[1][:, :], kvt[:, :], KV[0][:, :].bitcast(F32), ALU.subtract))
                    rope.wait(dve)
                    for part, src in zip(KVB, KV):
                        for h in range(2):
                            rope.inc(dve.tensor_copy(part[64 * h:64 * h + 64, :, L * h:L * h + L],
                                                     src[64 * h:64 * h + 64, :].bitcast(F32).rearrange("p (b l) -> p b l", b=B)))

        def norm(ctx, tag, banks, transposed=True):
            var_ready = sem(ctx, f"{tag}_var_ready")
            std_ready = sem(ctx, f"{tag}_std_ready")
            stats = Count(sem(ctx, f"{tag}_norm_steps"))
            xn_ready = sem(ctx, f"{tag}_xn_ready")
            xt_turned = sem(ctx, f"{tag}_xt_turned")
            xt_hi = sem(ctx, f"{tag}_xt_hi")
            xt_ready = sem(ctx, f"{tag}_xt_ready")

            def half(j):
                return slice(j // 2 * HALF, j // 2 * HALF + HALF)

            def vector(dve):
                for t in range(T):
                    stats.inc(dve.bn_stats(STATS[:, t, :], X[:, t, :]))
                for h in range(2):
                    stats.wait(dve, T // 2 * (h + 1))
                    for t in range(T // 2 * h, T // 2 * (h + 1)):
                        dve.bn_aggr(MOM[:, t, :], STATS[:, t, :]).then_inc(var_ready, 1)
                for h in range(2):
                    tiles = slice(T // 2 * h, T // 2 * (h + 1))
                    dve.wait_ge(std_ready, h + 1)
                    stats.inc(dve.reciprocal(RSTD[:, tiles], STD[:, tiles]))
                    stats.wait(dve)
                    for t in range(T // 2 * h, T // 2 * (h + 1)):
                        dve.tensor_scalar(XN[:, t, :], X[:, t, :], MOM[:, t, 0:1], RSTD[:, t:t + 1],
                                          ALU.subtract, ALU.mult).then_inc(xn_ready, 1)

            def vector_low(dve):
                for j in range(4):
                    dve.wait_ge(xt_hi, j + 1)
                    dve.tensor_tensor(xt[1][:, j % 2, half(j)], banks[j], xt[0][:, j % 2, half(j)].bitcast(F32),
                                      ALU.subtract).then_inc(xt_ready, 1)

            def scalar(act, high=True):
                for h in range(2):
                    tiles = slice(T // 2 * h, T // 2 * (h + 1))
                    act.wait_ge(var_ready, T // 2 * (h + 1))
                    act.activation(STD[:, tiles], MOM[:, tiles, 1], ACT.Sqrt, bias=EPS[:, 0:1]).then_inc(std_ready, 1)
                if high:
                    for j in range(4):
                        act.wait_ge(xt_turned, j + 1)
                        act.activation(xt[0][:, j % 2, half(j)], banks[j], ACT.Copy).then_inc(xt_hi, 1)

            def tensor(pe):
                for j in range(4):
                    pe.wait_ge(xn_ready, T // 2 * (j // 2 + 1))
                    for q in range(T // 2):
                        t = j // 2 * (T // 2) + q
                        last = pe.transpose(banks[j][:, q * P:(q + 1) * P], XN[:, t, (j % 2) * P:(j % 2 + 1) * P], IDENT[:, :])
                    last.then_inc(xt_turned, 1)

            return dict(vector=vector, vector_low=vector_low, scalar=scalar, tensor=tensor, ready=xt_ready, xn_ready=xn_ready)

        def latent_rope(Y, AT):
            o_qr, o_kr, o_ck, o_wo, width = pair_columns(0)
            with ExitStack() as ctx:
                W = sbuf(ctx, "W", [P, width])
                WS = split(ctx, "WS", [P, width])
                KR = split(ctx, "KR", [R, 2, B * L])
                C = split(ctx, "C", [P, 2, KD, CQ])
                U = split(ctx, "U", [ROT, 2, 2, B * L])
                COS = sbuf(ctx, "COS", [ROT, 2, S])
                SIN = sbuf(ctx, "SIN", [ROT, 2, S])
                RP = sbuf(ctx, "RP", [ROT, 2, 4, HALF])
                QR = (sbuf(ctx, "QR_hi", [ROT, 2, 2, HALF], F32R), sbuf(ctx, "QR_lo", [ROT, 2, 2, HALF], F32R))
                SM = sbuf(ctx, "SM", [P, 4, H])
                DIFF = XN[:, 0:4, :].rearrange("p t d -> p (t d)").rearrange("p (h t l) -> p h t l", h=2, t=T)
                PROB = XN[:, 4:8, :].rearrange("p t d -> p (t d)").rearrange("p (t h l) -> p t h l", h=2, t=T)
                QB = psum(ctx, "QB", [P, 4, 512])
                SC = psum(ctx, "SC", [P, 2, 512])
                TR = psum(ctx, "TR", [P, 2, 512])
                nrm = norm(ctx, "a0", [QB[:, j, :] for j in range(4)])
                tables = sem(ctx, "tables")
                w_in, w_hi, w_lo = sem(ctx, "w_in"), sem(ctx, "w_hi"), sem(ctx, "w_lo")
                chain_ps = sem(ctx, "chain_in_psum")
                chain_hi = sem(ctx, "chain_hi")
                chain_lo = sem(ctx, "chain_lo")
                q_ps = sem(ctx, "q_in_psum")
                rope_mul = sem(ctx, "rope_products")
                rope_add = sem(ctx, "rope_sums")
                rope_hi = sem(ctx, "rope_hi")
                rope_lo = sem(ctx, "rope_lo")
                scored = sem(ctx, "scored")
                smax = sem(ctx, "row_max")
                shifted = sem(ctx, "shifted")
                expd = sem(ctx, "exponentials")
                ssum = sem(ctx, "row_sums")
                normed = sem(ctx, "probabilities")
                turned = sem(ctx, "turned")
                at_hi, at_lo = sem(ctx, "at_hi"), sem(ctx, "at_lo")
                N_CHAIN = 6

                def w(c, n, part, rows=P):
                    return WS[part][0:rows, c:c + n]

                def both(f):
                    return f(0), f(1)

                def chain_slot(k, p):
                    if k == 0:
                        return TR[0:R, 0, :], [part[:, :, :].rearrange("p h n -> p (h n)") for part in KR]
                    if k in (1, 2):
                        return QB[:, k - 1, 0:KD * CQ], [part[:, k - 1, :, :].rearrange("p k n -> p (k n)") for part in C]
                    if k == 3:
                        return TR[:, 1, 0:D], [part[:, bass.ds(p * D, D)] for part in Y]
                    return QB[0:ROT, k - 2, :], [part[:, k - 4, :, :].rearrange("p q n -> p (q n)") for part in U]

                with nc.Block() as block:
                    @block.sync
                    def _(sp):
                        sp.dma_start(COS[:, :, :], A["qcos"]).then_inc(tables, 16)
                        sp.dma_start(SIN[:, :, :], A["qsin"]).then_inc(tables, 16)
                        sp.dma_start(W[:, :], A["L0_pairs"][0]).then_inc(w_in, 16)
                        with sp.Fori(1, NP) as p:
                            sp.wait_ge(w_lo, p)
                            sp.dma_start(W[:, :], A["L0_pairs"][bass.ds(p, 1), :, :].rearrange("a p n -> (a p) n")).then_inc(w_in, 16)

                    @block.gpsimd
                    def _(pool):
                        def low(p1):
                            pool.wait_ge(w_hi, p1)
                            pool.tensor_tensor(WS[1][:, :], W[:, :], WS[0][:, :].bitcast(F32), ALU.subtract).then_inc(w_lo, 1)

                        def add(p, u):
                            pool.wait_ge(rope_mul, 8 * p + 2 * (u + 1))
                            pool.tensor_tensor(RP[:, u % 2, 0, :], RP[:, u % 2, 0, :], RP[:, u % 2, 3, :], ALU.add).then_inc(rope_add, 1)
                            pool.tensor_tensor(RP[:, u % 2, 1, :], RP[:, u % 2, 1, :], RP[:, u % 2, 2, :], ALU.add).then_inc(rope_add, 1)

                        low(1)

                        def step(p, more):
                            add(p, 0)
                            add(p, 1)
                            if more:
                                low(p + 2)
                            add(p, 2)
                            add(p, 3)
                        with pool.Fori(0, NP - 1) as p:
                            step(p, True)
                        step(NP - 1, False)

                    @block.scalar
                    def _(act):
                        def high(p1):
                            act.wait_ge(w_in, 16 * p1)
                            act.activation(WS[0][:, :], W[:, :], ACT.Copy).then_inc(w_hi, 1)

                        def chain(p, k):
                            src, dst = chain_slot(k, p)
                            act.wait_ge(chain_ps, N_CHAIN * p + k + 1)
                            act.activation(dst[0], src, ACT.Copy).then_inc(chain_hi, 1)

                        def rope_high(p, u):
                            act.wait_ge(rope_add, 8 * p + 2 * (u + 1))
                            act.activation(QR[0][:, u % 2, :, :], RP[:, u % 2, 0:2, :], ACT.Copy).then_inc(rope_hi, 1)

                        def exps(p):
                            act.wait_ge(shifted, p + 1)
                            act.activation(DIFF, DIFF, ACT.Exp).then_inc(expd, 1)

                        def at_high(p):
                            act.wait_ge(turned, p + 1)
                            act.activation(AT[0][:, bass.ds(p * B * S, B * S)], TR[:, :, :].rearrange("p a n -> p (a n)"), ACT.Copy).then_inc(at_hi, 1)

                        high(1)
                        nrm["scalar"](act)

                        def step(p, first, more):
                            chain(p, 0)
                            if not first:
                                act.wait_ge(scored, 4 * p - 2)
                                rope_high(p - 1, 3)
                            for k in range(1, N_CHAIN):
                                if k == N_CHAIN - 1 and not first:
                                    act.wait_ge(scored, 4 * p)
                                chain(p, k)
                            if not first:
                                exps(p - 1)
                            rope_high(p, 0)
                            if more:
                                high(p + 2)
                            rope_high(p, 1)
                            if not first:
                                at_high(p - 1)
                            act.wait_ge(scored, 4 * p + 1)
                            rope_high(p, 2)
                        step(0, True, True)
                        with act.Fori(1, NP - 1) as p:
                            step(p, False, True)
                        step(NP - 1, False, False)
                        act.wait_ge(scored, 4 * NP - 2)
                        rope_high(NP - 1, 3)
                        exps(NP - 1)
                        at_high(NP - 1)

                    @block.vector
                    def _(dve):
                        nrm["vector"](dve)
                        nrm["vector_low"](dve)
                        dve.wait_ge(tables, 32)

                        def chain(p, k):
                            src, dst = chain_slot(k, p)
                            dve.wait_ge(chain_hi, N_CHAIN * p + k + 1)
                            dve.tensor_tensor(dst[1], src, dst[0].bitcast(F32), ALU.subtract).then_inc(chain_lo, 1)

                        def mul(p, u, first=False):
                            half = u % 2
                            src = QB[0:ROT, 2 * half:2 * half + 2, :].rearrange("p q (b s) -> p q b s", b=2)
                            cos = COS[:, :, :].unsqueeze(2).broadcast_to((ROT, 2, 2, S))
                            dve.wait_ge(q_ps, 4 * p + u + 1)
                            if not (first and u < 2):
                                dve.wait_ge(rope_lo, 4 * p + u - 1)
                            dve.tensor_tensor(RP[:, half, 0:2, :].rearrange("p q (b s) -> p q b s", b=2), src, cos, ALU.mult).then_inc(rope_mul, 1)
                            sin = SIN[:, :, :].unsqueeze(2).broadcast_to((ROT, 2, 2, S))
                            dve.tensor_tensor(RP[:, half, 2:4, :].rearrange("p q (b s) -> p q b s", b=2), src, sin, ALU.mult).then_inc(rope_mul, 1)

                        def rope_low(p, u):
                            dve.wait_ge(rope_hi, 4 * p + u + 1)
                            dve.tensor_tensor(QR[1][:, u % 2, :, :], RP[:, u % 2, 0:2, :], QR[0][:, u % 2, :, :].bitcast(F32), ALU.subtract).then_inc(rope_lo, 1)

                        def shift(p, first):
                            dve.wait_ge(scored, 4 * p + 4)
                            src = SC[:, :, :].rearrange("p h (t l) -> p (h t) l", l=L)
                            dve.tensor_reduce(SM[:, 0, :], src, AX, ALU.max).then_inc(smax, 1)
                            dve.wait_ge(smax, p + 1)
                            if not first:
                                dve.wait_ge(normed, p)
                            dve.tensor_tensor(DIFF.rearrange("p h t l -> p (h t) l"), src, SM[:, 0, :].unsqueeze(2).broadcast_to((P, H, L)), ALU.subtract).then_inc(shifted, 1)

                        def normalise(p, first):
                            dve.wait_ge(expd, p + 1)
                            dve.tensor_reduce(SM[:, 1, :], DIFF.rearrange("p h t l -> p (h t) l"), AX, ALU.add).then_inc(ssum, 1)
                            dve.wait_ge(ssum, 2 * p + 1)
                            dve.reciprocal(SM[:, 2, :], SM[:, 1, :]).then_inc(ssum, 1)
                            dve.wait_ge(ssum, 2 * p + 2)
                            if not first:
                                dve.wait_ge(turned, p)
                            dve.tensor_tensor(PROB.rearrange("p t h l -> p h t l"), DIFF,
                                              SM[:, 2, :].rearrange("p (h t) -> p h t", h=2).unsqueeze(3).broadcast_to((P, 2, T, L)), ALU.mult).then_inc(normed, 1)

                        def at_low(p):
                            dve.wait_ge(at_hi, p + 1)
                            dve.tensor_tensor(AT[1][:, bass.ds(p * B * S, B * S)], TR[:, :, :].rearrange("p a n -> p (a n)"),
                                              AT[0][:, bass.ds(p * B * S, B * S)].bitcast(F32), ALU.subtract).then_inc(at_lo, 1)

                        def step(p, first, second=False):
                            chain(p, 0)
                            if not first:
                                rope_low(p - 1, 3)
                            for k in range(1, N_CHAIN):
                                chain(p, k)
                            if not first:
                                shift(p - 1, second)
                            mul(p, 0, first)
                            if not first:
                                normalise(p - 1, second)
                            mul(p, 1, first)
                            rope_low(p, 0)
                            mul(p, 2)
                            if not first:
                                at_low(p - 1)
                            rope_low(p, 1)
                            mul(p, 3)
                            rope_low(p, 2)
                        step(0, True)
                        step(1, False, True)
                        with dve.Fori(2, NP) as p:
                            step(p, False)
                        rope_low(NP - 1, 3)
                        shift(NP - 1, False)
                        normalise(NP - 1, False)
                        at_low(NP - 1)

                    @block.tensor
                    def _(pe):
                        nrm["tensor"](pe)
                        pe.wait_ge(nrm["ready"], 4)

                        def chain(p, first, second):
                            pe.wait_ge(w_lo, p + 1)
                            if not (first or second):
                                pe.wait_ge(at_lo, p - 1)
                            for h in range(2):
                                last = mm3(pe, TR[0:R, 0, h * 256:(h + 1) * 256], both(lambda i: w(o_kr + R * h, R, i)), both(lambda i: KV[i][:, :]))
                            last.then_inc(chain_ps, 1)
                            if not first:
                                pe.wait_ge(rope_mul, 8 * p)
                            for h in range(2):
                                for k in range(KD):
                                    last = mm3(pe, QB[:, h, k * CQ:(k + 1) * CQ], both(lambda i: w(O_WQ + D * h + P * k, P, i)), both(lambda i: w(O_CQ + CQ * h, CQ, i)))
                                last.then_inc(chain_ps, 1)
                            for h in range(2):
                                last = mm3(pe, TR[:, 1, 0:D], both(lambda i: w(o_ck + P * h, P, i)), both(lambda i: w(o_wo + D * h, D, i)), first=h == 0, last=h == 1)
                            last.then_inc(chain_ps, 1)
                            if not first:
                                score(p - 1, 3)
                            for h in range(2):
                                pe.wait_ge(chain_lo, N_CHAIN * p + 1)
                                for q in range(2):
                                    last = mm3(pe, QB[0:ROT, 2 + h, q * 256:(q + 1) * 256], both(lambda i: w(o_qr + CQ * h + ROT * q, ROT, i, R)), both(lambda i: KR[i][:, h, :]))
                                last.then_inc(chain_ps, 1)

                        def query(p, u, first=False):
                            h, half = u // 2, u % 2
                            if u < 2:
                                pe.wait_ge(chain_lo, N_CHAIN * p + N_CHAIN)
                            else:
                                pe.wait_ge(rope_mul, 8 * p + 2 * (u - 1))
                            for q in range(2):
                                for k in range(KD):
                                    last = mm3(pe, QB[0:ROT, 2 * half + q, :], both(lambda i: C[i][:, h, k, ROT * q:ROT * (q + 1)]),
                                               both(lambda i: xt[i][:, k, half * HALF:(half + 1) * HALF]), first=k == 0, last=k == KD - 1)
                            last.then_inc(q_ps, 1)

                        def score(p, u, first=False):
                            h, half = u // 2, u % 2
                            pe.wait_ge(rope_lo, 4 * p + u + 1)
                            if u == 0 and not first:
                                pe.wait_ge(shifted, p)
                            for t in range(T // 2):
                                b = (half * (T // 2) + t) // TB
                                for q in range(2):
                                    last = mm3(pe, SC[:, h, (half * 4 + t) * L:(half * 4 + t + 1) * L], both(lambda i: QR[i][:, half, q, t * P:(t + 1) * P]),
                                               both(lambda i: U[i][:, h, q, b * L:(b + 1) * L]), first=q == 0, last=q == 1)
                            last.then_inc(scored, 1)

                        def turn(p):
                            pe.wait_ge(normed, p + 1)
                            for t in range(T):
                                last = pe.transpose(TR[:, t // 4, (t % 4) * P:(t % 4 + 1) * P], PROB[:, t, :, :].rearrange("p h l -> p (h l)"), IDENT[:, :])
                            last.then_inc(turned, 1)

                        def step(p, first, second=False):
                            chain(p, first, second)
                            query(p, 0)
                            query(p, 1)
                            score(p, 0, first)
                            query(p, 2)
                            if not first:
                                turn(p - 1)
                            score(p, 1)
                            query(p, 3)
                            score(p, 2)
                        step(0, True)
                        step(1, False, True)
                        with pe.Fori(2, NP) as p:
                            step(p, False)
                        score(NP - 1, 3)
                        turn(NP - 1)

        def latent_out(Y, AT, gate):
            with ExitStack() as ctx:
                Z = split(ctx, "Z", [P, 2, NP * D])
                ZP = psum(ctx, "ZP", [P, 4, 512])
                OP = psum(ctx, "OP", [P, 2, 512])
                z_ps, z_hi, z_lo = sem(ctx, "z_in_psum"), sem(ctx, "z_hi"), sem(ctx, "z_lo")
                out_ps, added = sem(ctx, "out_in_psum"), sem(ctx, "added")
                ROUNDS = NP // 2
                with nc.Block() as block:
                    @block.tensor
                    def _(pe):
                        def values(b):
                            for r in range(ROUNDS):
                                n = b * ROUNDS + r
                                if n >= 4:
                                    pe.wait_ge(z_lo, n - 3)
                                for q in range(2):
                                    pair = 2 * r + q
                                    last = mm3(pe, ZP[:, n % 4, q * D:(q + 1) * D], (KVB[0][:, b, :], KVB[1][:, b, :]),
                                               (Y[0][:, pair * D:(pair + 1) * D], Y[1][:, pair * D:(pair + 1) * D]))
                                last.then_inc(z_ps, 1)
                        values(0)
                        for b in range(B):
                            if b + 1 < B:
                                values(b + 1)
                            pe.wait_ge(z_lo, ROUNDS * (b + 1))
                            for t in range(TB * b, TB * (b + 1)):
                                if t >= 2:
                                    pe.wait_ge(added, t - 1)
                                for pair in range(NP):
                                    at = slice(pair * B * S + t * P, pair * B * S + (t + 1) * P)
                                    last = mm3(pe, OP[:, t % 2, 0:D], (AT[0][:, at], AT[1][:, at]),
                                               (Z[0][:, b % 2, pair * D:(pair + 1) * D], Z[1][:, b % 2, pair * D:(pair + 1) * D]), first=pair == 0, last=pair == NP - 1)
                                last.then_inc(out_ps, 1)

                    @block.scalar
                    def _(act):
                        for n in range(B * ROUNDS):
                            b, r = divmod(n, ROUNDS)
                            act.wait_ge(z_ps, n + 1)
                            if b >= 2:
                                act.wait_ge(out_ps, TB * (b - 1))
                            act.activation(Z[0][:, b % 2, 2 * r * D:2 * (r + 1) * D], ZP[:, n % 4, :], ACT.Copy).then_inc(z_hi, 1)

                    @block.vector
                    def _(dve):
                        def low(b):
                            for r in range(ROUNDS):
                                n = b * ROUNDS + r
                                at = slice(2 * r * D, 2 * (r + 1) * D)
                                dve.wait_ge(z_hi, n + 1)
                                dve.tensor_tensor(Z[1][:, b % 2, at], ZP[:, n % 4, :], Z[0][:, b % 2, at].bitcast(F32), ALU.subtract).then_inc(z_lo, 1)
                        low(0)
                        for b in range(B):
                            if b + 1 < B:
                                low(b + 1)
                            for t in range(TB * b, TB * (b + 1)):
                                dve.wait_ge(out_ps, t + 1)
                                dve.scalar_tensor_tensor(out=X[:, t, :], in0=OP[:, t % 2, 0:D], scalar=GATE[:, gate:gate + 1], in1=X[:, t, :],
                                                         op0=ALU.mult, op1=ALU.add).then_inc(added, 1)

        def experts(tag, gate, NE, NC, E, TOP, biased):
            OUTS = [[(0, 0), (1, 1)], [(1, 2), (2, 3)]] if biased else [[(m, m) for m in range(NC)]]
            NO = len(OUTS)
            ND = 4
            EC = NE * NO
            with ExitStack() as ctx:
                WU = sbuf(ctx, "WU", [P, NC, 4 * P])
                WUS = split(ctx, "WUS", [P, NC, 4 * P])
                WD = sbuf(ctx, "WD", [P, ND * D])
                WDS = split(ctx, "WDS", [P, ND * D])
                HG = sbuf(ctx, "HG", [P, 2, HALF])
                HF = sbuf(ctx, "HF", [P, 2, HALF])
                HS = split(ctx, "HS", [P, 2, NC, HALF])
                RW = sbuf(ctx, "RW", [P, KD, E])
                RWS = split(ctx, "RWS", [P, KD, E])
                CG = sbuf(ctx, "CG", [P, EC, T])
                PR = sbuf(ctx, "PR", [P, 4, T, E])
                SM = sbuf(ctx, "SM", [P, 6, T])
                CMP = sbuf(ctx, "CMP", [P, 2, T * E * E])
                BEFORE = sbuf(ctx, "BEFORE", [P, E * E])
                G = psum(ctx, "G", [P, 2, 512])
                U = psum(ctx, "U", [P, 2, 512])
                DN = psum(ctx, "DN", [P, 4, 512])
                if biased:
                    BIAS = sbuf(ctx, "BIAS", [P, NE * NC * 2])
                    UB = sbuf(ctx, "UB", [P, 2 * NC])
                    unit_bias = sem(ctx, f"{tag}_unit_bias")
                    GB = sbuf(ctx, "GB", [P, E])
                    B2 = sbuf(ctx, "B2", [E + 1, D])
                    B2S = split(ctx, "B2S", [E + 1, D])
                    CTS = split(ctx, "CTS", [E + 1, B * S])
                nrm = norm(ctx, tag, [DN[:, j, :] for j in range(4)])
                small_in = sem(ctx, f"{tag}_small_in")
                small_split = Count(sem(ctx, f"{tag}_small_split"))
                wu_in, wu_hi, wu_lo = (sem(ctx, f"{tag}_wu_{s}") for s in ("in", "hi", "lo"))
                wd_in, wd_hi, wd_lo = (sem(ctx, f"{tag}_wd_{s}") for s in ("in", "hi", "lo"))
                up_done, silu_done, h_full, h_hi, h_lo = (sem(ctx, f"{tag}_{s}") for s in ("up_done", "silu_done", "h_full", "h_hi", "h_lo"))
                down_done, added, first_added = (sem(ctx, f"{tag}_{s}") for s in ("down_done", "added", "first_added"))
                logits_ready = sem(ctx, f"{tag}_logits_ready")
                r_shift, r_exp = sem(ctx, f"{tag}_router_shifted"), sem(ctx, f"{tag}_router_exp")
                route = Count(sem(ctx, f"{tag}_router_steps"))
                combine_ready = sem(ctx, f"{tag}_combine_ready")
                ct_turned, ct_hi, ct_lo = (sem(ctx, f"{tag}_ct_{s}") for s in ("turned", "hi", "lo"))
                bias_ps, bias_added = sem(ctx, f"{tag}_bias_in_psum"), sem(ctx, f"{tag}_bias_added")
                LOG = DN[:, 0, 0:T * E].rearrange("p (t e) -> p t e", t=T)
                CT = DN[:, 1:3, :].rearrange("p a n -> p (a n)")
                SMALL = 5 if biased else 2
                UPS = 2 * NC

                def dram(name, e):
                    return A[name][bass.ds(e, 1), :, :].rearrange("a p n -> (a p) n")

                with nc.Block() as block:
                    @block.sync
                    def _(sp):
                        sp.dma_start(RW[:, :, :], A[f"{tag}_router"]).then_inc(small_in, 16)
                        sp.dma_start(BEFORE[:, :], A[f"before{E}"]).then_inc(small_in, 16)
                        if biased:
                            sp.dma_start(BIAS[:, :], A[f"{tag}_bias"]).then_inc(small_in, 16)
                            sp.dma_start(GB[:, :], A[f"{tag}_router_bias"]).then_inc(small_in, 16)
                            sp.dma_start(B2[:, :], A[f"{tag}_b2"]).then_inc(small_in, 16)

                        wu = WU[:, :, :].rearrange("p m n -> p (m n)")
                        sp.dma_start(wu, A[f"{tag}_up"][0]).then_inc(wu_in, 16)
                        sp.dma_start(WD[:, :], A[f"{tag}_down"][0]).then_inc(wd_in, 16)
                        with sp.Fori(1, NE) as e:
                            sp.wait_ge(wu_lo, NC * e)
                            sp.dma_start(wu, dram(f"{tag}_up", e)).then_inc(wu_in, 16)
                            sp.wait_ge(wd_lo, e)
                            sp.dma_start(WD[:, :], dram(f"{tag}_down", e)).then_inc(wd_in, 16)

                    @block.gpsimd
                    def _(pool):
                        def up_low(e, m):
                            pool.wait_ge(wu_hi, NC * e + m + 1)
                            pool.tensor_tensor(WUS[1][:, m, :], WU[:, m, :], WUS[0][:, m, :].bitcast(F32), ALU.subtract).then_inc(wu_lo, 1)

                        def down_low(e):
                            pool.wait_ge(wd_hi, e + 1)
                            pool.tensor_tensor(WDS[1][:, :], WD[:, :], WDS[0][:, :].bitcast(F32), ALU.subtract).then_inc(wd_lo, 1)

                        for m in range(NC):
                            up_low(0, m)
                        with pool.Fori(0, NE - 1) as e:
                            down_low(e)
                            for m in range(NC):
                                up_low(e + 1, m)
                        down_low(NE - 1)

                    @block.scalar
                    def _(act):
                        def up_high(e, m):
                            act.wait_ge(wu_in, 16 * e + 16)
                            act.activation(WUS[0][:, m, :], WU[:, m, :], ACT.Copy).then_inc(wu_hi, 1)

                        def down_high(e):
                            act.wait_ge(wd_in, 16 * e + 16)
                            act.activation(WDS[0][:, :], WD[:, :], ACT.Copy).then_inc(wd_hi, 1)

                        def silu(e, k, first):
                            half, m = divmod(k, NC)
                            act.wait_ge(up_done, UPS * e + k + 1)
                            if not (first and k < 2):
                                act.wait_ge(h_full, UPS * e + k - 1)
                            if biased and k == 0:
                                act.wait_ge(unit_bias, e + 1)
                            bias = UB[:, 2 * m:2 * m + 1] if biased else 0.0
                            act.activation(HG[:, k % 2, :], G[:, k % 2, :], ACT.Silu, bias=bias).then_inc(silu_done, 1)

                        def high(e, k, first):
                            half, m = divmod(k, NC)
                            act.wait_ge(h_full, UPS * e + k + 1)
                            if not first:
                                act.wait_ge(down_done, 8 * e - 4 + 4 * half)
                            act.activation(HS[0][:, half, m, :], HF[:, k % 2, :], ACT.Copy).then_inc(h_hi, 1)

                        def step(e, first=False, second=False, more=True):
                            for k in range(UPS):
                                silu(e, k, first)
                                if k > 0:
                                    high(e, k - 1, first)
                                elif not first:
                                    high(e - 1, UPS - 1, second)
                                if k == NC:
                                    down_high(e)
                                if k >= NC and more:
                                    up_high(e + 1, k - NC)

                        for m in range(NC):
                            up_high(0, m)
                        nrm["scalar"](act)
                        act.wait_ge(small_in, 16 * SMALL)
                        act.wait_ge(r_shift, 1)
                        act.activation(PR[:, 1, :, :], PR[:, 0, :, :], ACT.Exp).then_inc(r_exp, 1)
                        step(0, first=True)
                        if biased:
                            act.wait_ge(ct_turned, 1)
                            act.activation(CTS[0][:, :], CT[0:E + 1, :], ACT.Copy).then_inc(ct_hi, 1)
                        step(1, second=True)
                        with act.Fori(2, NE - 1) as e:
                            step(e)
                        step(NE - 1, more=False)
                        high(NE - 1, UPS - 1, False)

                    @block.vector
                    def _(dve):
                        nrm["vector"](dve)
                        dve.wait_ge(small_in, 16 * SMALL)
                        small_split.inc(dve.tensor_copy(RWS[0][:, :, :], RW[:, :, :]))
                        small_split.wait(dve)
                        small_split.inc(dve.tensor_tensor(RWS[1][:, :, :], RW[:, :, :], RWS[0][:, :, :].bitcast(F32), ALU.subtract))
                        if biased:
                            small_split.inc(dve.tensor_copy(B2S[0][:, :], B2[:, :]))
                            small_split.wait(dve)
                            small_split.inc(dve.tensor_tensor(B2S[1][:, :], B2[:, :], B2S[0][:, :].bitcast(F32), ALU.subtract))
                        nrm["vector_low"](dve)

                        def row(i):
                            return SM[:, i, :].unsqueeze(2).broadcast_to((P, T, E))
                        dve.wait_ge(logits_ready, 1)
                        route.inc(dve.tensor_reduce(SM[:, 0, :], LOG, AX, ALU.max))
                        route.wait(dve)
                        dve.tensor_tensor(PR[:, 0, :, :], LOG, row(0), ALU.subtract).then_inc(r_shift, 1)
                        dve.wait_ge(r_exp, 1)
                        route.inc(dve.tensor_reduce(SM[:, 1, :], PR[:, 1, :, :], AX, ALU.add))
                        route.wait(dve)
                        route.inc(dve.reciprocal(SM[:, 2, :], SM[:, 1, :]))
                        route.wait(dve)
                        route.inc(dve.tensor_tensor(PR[:, 2, :, :], PR[:, 1, :, :], row(2), ALU.mult))
                        route.wait(dve)
                        rank_by = PR[:, 2, :, :]
                        if biased:
                            route.inc(dve.tensor_tensor(PR[:, 0, :, :], PR[:, 2, :, :], GB[:, :].unsqueeze(1).broadcast_to((P, T, E)), ALU.add))
                            route.wait(dve)
                            rank_by = PR[:, 0, :, :]
                        other = rank_by.unsqueeze(2).broadcast_to((P, T, E, E))
                        mine = rank_by.unsqueeze(3).broadcast_to((P, T, E, E))
                        gt = CMP[:, 0, :].rearrange("p (t i j) -> p t i j", t=T, i=E)
                        eq = CMP[:, 1, :].rearrange("p (t i j) -> p t i j", t=T, i=E)
                        route.inc(dve.tensor_tensor(gt, other, mine, ALU.is_gt))
                        route.inc(dve.tensor_tensor(eq, other, mine, ALU.is_equal))
                        route.wait(dve)
                        eq2 = CMP[:, 1, :].rearrange("p (t n) -> p t n", t=T)
                        route.inc(dve.tensor_tensor(eq2, eq2, BEFORE[:, :].unsqueeze(1).broadcast_to((P, T, E * E)), ALU.mult))
                        route.wait(dve)
                        route.inc(dve.tensor_tensor(CMP[:, 0, :], CMP[:, 0, :], CMP[:, 1, :], ALU.add))
                        route.wait(dve)
                        route.inc(dve.tensor_reduce(PR[:, 1, :, :].rearrange("p t e -> p (t e)"), CMP[:, 0, :].rearrange("p (n j) -> p n j", j=E), AX, ALU.add))
                        route.wait(dve)
                        route.inc(dve.scalar_tensor_tensor(out=PR[:, 3, :, :], in0=PR[:, 1, :, :], scalar=float(TOP), in1=PR[:, 2, :, :], op0=ALU.is_lt, op1=ALU.mult))
                        route.wait(dve)
                        if not biased:
                            route.inc(dve.tensor_reduce(SM[:, 3, :], PR[:, 3, :, :], AX, ALU.add))
                            route.wait(dve)
                            route.inc(dve.reciprocal(SM[:, 4, :], SM[:, 3, :]))
                            route.wait(dve)
                            route.inc(dve.tensor_tensor(PR[:, 3, :, :], PR[:, 3, :, :], row(4), ALU.mult))
                            route.wait(dve)
                        dve.tensor_scalar(CG[:, 0:E, :].rearrange("p e t -> p t e"), PR[:, 3, :, :], GATE[:, gate:gate + 1], None, ALU.mult).then_inc(combine_ready, 1)
                        dve.tensor_scalar(CG[:, E:EC, :].rearrange("p e t -> p (e t)"), ONES[:, 0:(EC - E) * T], GATE[:, gate:gate + 1], None, ALU.mult).then_inc(combine_ready, 1)

                        def full(e, k, first):
                            half, m = divmod(k, NC)
                            dve.wait_ge(silu_done, UPS * e + k + 1)
                            if not (first and k < 2):
                                dve.wait_ge(h_lo, UPS * e + k - 1)
                            if biased:
                                dve.scalar_tensor_tensor(out=HF[:, k % 2, :], in0=U[:, k % 2, :], scalar=BIAS[:, bass.ds(e * (2 * NC) + 2 * m + 1, 1)],
                                                         in1=HG[:, k % 2, :], op0=ALU.add, op1=ALU.mult).then_inc(h_full, 1)
                            else:
                                dve.tensor_tensor(HF[:, k % 2, :], U[:, k % 2, :], HG[:, k % 2, :], ALU.mult).then_inc(h_full, 1)

                        def low(e, k):
                            half, m = divmod(k, NC)
                            dve.wait_ge(h_hi, UPS * e + k + 1)
                            dve.tensor_tensor(HS[1][:, half, m, :], HF[:, k % 2, :], HS[0][:, half, m, :].bitcast(F32), ALU.subtract).then_inc(h_lo, 1)

                        def add(e, half):
                            for q in range(4):
                                t, n = 4 * half + q, 4 * half + q
                                dve.wait_ge(down_done, 8 * e + n + 1)
                                for o in range(NO):
                                    ins = dve.scalar_tensor_tensor(out=X[:, t, :], in0=DN[:, q, o * D:(o + 1) * D], scalar=CG[:, :, :].rearrange("p e t -> p (e t)")[:, bass.ds(e * (NO * T) + o * T + t, 1)],
                                                                   in1=X[:, t, :], op0=ALU.mult, op1=ALU.add)
                                    if o < NO - 1:
                                        ins.then_inc(first_added, 1)
                                        dve.wait_ge(first_added, 8 * e + n + 1)
                                    else:
                                        ins.then_inc(added, 1)

                        def unit_biases(e):
                            dve.tensor_scalar(UB[:, :], BIAS[:, bass.ds(e * (2 * NC), 2 * NC)], 1.0, None, ALU.mult).then_inc(unit_bias, 1)

                        def step(e, first=False, more=True):
                            for k in range(UPS):
                                full(e, k, first)
                                if k == UPS - 1 and biased and more:
                                    unit_biases(e + 1)
                                if k > 0:
                                    low(e, k - 1)
                                elif not first:
                                    low(e - 1, UPS - 1)
                                if k == NC - 1 and not first:
                                    add(e - 1, 1)
                            if first and biased:
                                dve.wait_ge(ct_hi, 1)
                                dve.tensor_tensor(CTS[1][:, :], CT[0:E + 1, :], CTS[0][:, :].bitcast(F32), ALU.subtract).then_inc(ct_lo, 1)
                                for t in range(T):
                                    dve.wait_ge(bias_ps, t + 1)
                                    dve.tensor_tensor(X[:, t, :], DN[:, t % 4, 0:D], X[:, t, :], ALU.add).then_inc(bias_added, 1)
                                dve.wait_ge(bias_added, T)
                            add(e, 0)
                        if biased:
                            unit_biases(0)
                        step(0, first=True)
                        with dve.Fori(1, NE - 1) as e:
                            step(e)
                        step(NE - 1, more=False)
                        low(NE - 1, UPS - 1)
                        add(NE - 1, 1)

                    @block.tensor
                    def _(pe):
                        nrm["tensor"](pe)
                        pe.wait_ge(nrm["ready"], 4)
                        pe.wait_ge(small_split.sem, 4 if biased else 2)
                        for t in range(T):
                            for k in range(KD):
                                last = mm3(pe, DN[:, 0, t * E:(t + 1) * E], (xt[0][:, k, t * P:(t + 1) * P], xt[1][:, k, t * P:(t + 1) * P]),
                                           (RWS[0][:, k, :], RWS[1][:, k, :]), first=k == 0, last=k == KD - 1)
                        last.then_inc(logits_ready, 1)

                        def up(e, k, first):
                            half, m = divmod(k, NC)
                            if half == 0:
                                pe.wait_ge(wu_lo, NC * e + m + 1)
                            if not (first and k < 2):
                                pe.wait_ge(h_full, UPS * e + k - 1)
                            for mat, bank in ((0, G), (1, U)):
                                for c in range(KD):
                                    at = slice((2 * c + mat) * P, (2 * c + mat + 1) * P)
                                    last = mm3(pe, bank[:, k % 2, :], (WUS[0][:, m, at], WUS[1][:, m, at]),
                                               (xt[0][:, c, half * HALF:(half + 1) * HALF], xt[1][:, c, half * HALF:(half + 1) * HALF]), first=c == 0, last=c == KD - 1)
                            last.then_inc(up_done, 1)

                        def down(e, half, first):
                            pe.wait_ge(h_lo, UPS * e + NC * (half + 1))
                            if half == 0:
                                pe.wait_ge(wd_lo, e + 1)
                            for q in range(4):
                                if not (first and half == 0):
                                    pe.wait_ge(added, 8 * e + 4 * half + q - 3)
                                for o, rows in enumerate(OUTS):
                                    for j, (m, n) in enumerate(rows):
                                        last = mm3(pe, DN[:, q, o * D:(o + 1) * D], (HS[0][:, half, m, q * P:(q + 1) * P], HS[1][:, half, m, q * P:(q + 1) * P]),
                                                   (WDS[0][:, n * D:(n + 1) * D], WDS[1][:, n * D:(n + 1) * D]), first=j == 0, last=j == len(rows) - 1)
                                last.then_inc(down_done, 1)

                        def step(e, first=False, second=False):
                            for k in range(NC):
                                up(e, k, first)
                            if not first:
                                down(e - 1, 1, second)
                            for k in range(NC, UPS):
                                up(e, k, first)
                            if first and biased:
                                pe.wait_ge(combine_ready, 2)
                                for t in range(T):
                                    last = pe.transpose(CT[0:E + 1, t * P:(t + 1) * P], CG[:, 0:E + 1, t], IDENT[:, :])
                                last.then_inc(ct_turned, 1)
                                pe.wait_ge(ct_lo, 1)
                                for t in range(T):
                                    if t >= 4:
                                        pe.wait_ge(bias_added, t - 3)
                                    mm3(pe, DN[:, t % 4, 0:D], (CTS[0][:, t * P:(t + 1) * P], CTS[1][:, t * P:(t + 1) * P]), (B2S[0][:, :], B2S[1][:, :])).then_inc(bias_ps, 1)
                                pe.wait_ge(bias_added, T)
                            if first and not biased:
                                pe.wait_ge(combine_ready, 2)
                            down(e, 0, first)
                        step(0, first=True)
                        step(1, second=False)
                        with pe.Fori(2, NE) as e:
                            step(e)
                        down(NE - 1, 1, False)

        def latent_chain(GS, Y):
            o_qr, o_kr, o_ck, o_wo, width = pair_columns(1)
            with ExitStack() as ctx:
                W = sbuf(ctx, "W", [P, 2, width])
                WS = split(ctx, "WS", [P, 2, width])
                KR = split(ctx, "KR", [R, 4, B * L])
                UU = split(ctx, "UU", [ROT, 4, 2, B * L])
                VV = split(ctx, "VV", [P, 4, B * L])
                PB = psum(ctx, "PB", [P, 4, 512])
                NB = psum(ctx, "NB", [P, 4, 512])
                nrm = norm(ctx, "a1", [NB[:, j, :] for j in range(4)])
                w_in, w_hi, w_lo = sem(ctx, "w_in"), sem(ctx, "w_hi"), sem(ctx, "w_lo")
                in_ps, part_hi, part_lo = sem(ctx, "in_psum"), sem(ctx, "part_hi"), sem(ctx, "part_lo")
                STEPS = 2 + 2 + 4 + 2 + 4
                ROUNDS = NP // 2

                def place(s, g):
                    if s < 2:
                        return R, 512, [part[:, 2 * s:2 * s + 2, :].rearrange("p h n -> p (h n)") for part in KR]
                    if s < 4:
                        return P, D, [part[:, bass.ds(g * (2 * D) + (s - 2) * D, D)] for part in Y]
                    if s < 8:
                        return ROT, 512, [part[:, s - 4, :, :].rearrange("p q n -> p (q n)") for part in UU]
                    if s < 10:
                        return P, 512, [part[:, 2 * (s - 8):2 * (s - 8) + 2, :].rearrange("p h n -> p (h n)") for part in VV]
                    return P, 512, None

                def g_parts(s, g, i):
                    return GS[i][:, :, :, bass.ds(g * (4 * L) + (s - 10) * L, L)]

                with nc.Block() as block:
                    @block.sync
                    def _(sp):
                        w2 = W[:, :, :].rearrange("p a n -> p a n")
                        sp.dma_start(w2, A["L1_pairs"][0:2].rearrange("a p n -> p a n")).then_inc(w_in, 16)
                        with sp.Fori(1, ROUNDS) as g:
                            sp.wait_ge(w_lo, g)
                            sp.dma_start(w2, A["L1_pairs"][bass.ds(g * 2, 2), :, :].rearrange("a p n -> p a n")).then_inc(w_in, 16)

                    @block.gpsimd
                    def _(pool):
                        with pool.Fori(0, ROUNDS) as g:
                            pool.wait_ge(w_hi, g + 1)
                            pool.tensor_tensor(WS[1][:, :, :], W[:, :, :], WS[0][:, :, :].bitcast(F32), ALU.subtract).then_inc(w_lo, 1)

                    @block.scalar
                    def _(act):
                        def step(g, first=False):
                            act.wait_ge(w_in, 16 * g + 16)
                            if not first:
                                act.wait_ge(in_ps, STEPS * g)
                            act.activation(WS[0][:, :, :], W[:, :, :], ACT.Copy).then_inc(w_hi, 1)
                            if first:
                                nrm["scalar"](act)
                            for s in range(STEPS):
                                rows, n, dst = place(s, g)
                                act.wait_ge(in_ps, STEPS * g + s + 1)
                                if s < 10:
                                    act.activation(dst[0], PB[0:rows, s % 4, 0:n], ACT.Copy).then_inc(part_hi, 1)
                                else:
                                    act.activation(g_parts(s, g, 0), PB[:, s % 4, :].rearrange("p (k b l) -> p k b l", k=KD, b=B), ACT.Copy).then_inc(part_hi, 1)
                        step(0, True)
                        with act.Fori(1, ROUNDS) as g:
                            step(g)

                    @block.vector
                    def _(dve):
                        nrm["vector"](dve)
                        nrm["vector_low"](dve)
                        with dve.Fori(0, ROUNDS) as g:
                            for s in range(STEPS):
                                rows, n, dst = place(s, g)
                                dve.wait_ge(part_hi, STEPS * g + s + 1)
                                if s < 10:
                                    dve.tensor_tensor(dst[1], PB[0:rows, s % 4, 0:n], dst[0].bitcast(F32), ALU.subtract).then_inc(part_lo, 1)
                                else:
                                    src = PB[:, s % 4, :].rearrange("p (k b l) -> p k b l", k=KD, b=B)
                                    dve.tensor_tensor(g_parts(s, g, 1), src, g_parts(s, g, 0).bitcast(F32), ALU.subtract).then_inc(part_lo, 1)

                    @block.tensor
                    def _(pe):
                        nrm["tensor"](pe)

                        def w(a, c, n, rows=P):
                            return WS[0][0:rows, a, c:c + n], WS[1][0:rows, a, c:c + n]

                        def step(g, first=False):
                            def free(s, need=None):
                                n = (s - 4 if s >= 4 else (s - 2 if s < 2 else s - 6)) if need is None else max(need, s - 4)
                                if not (first and n < 0):
                                    pe.wait_ge(part_lo, STEPS * g + n + 1)
                            pe.wait_ge(w_lo, g + 1)
                            for s in range(2):
                                free(s)
                                for j in range(2):
                                    last = mm3(pe, PB[0:R, s % 4, j * 256:(j + 1) * 256], w(s, o_kr + R * j, R), (KV[0][:, :], KV[1][:, :]))
                                last.then_inc(in_ps, 1)
                            for s in range(2, 4):
                                free(s)
                                for j in range(2):
                                    last = mm3(pe, PB[:, s % 4, 0:D], w(s - 2, o_ck + P * j, P), w(s - 2, o_wo + D * j, D), first=j == 0, last=j == 1)
                                last.then_inc(in_ps, 1)
                            for s in range(4, 8):
                                h = s - 4
                                free(s, need=h // 2)
                                for q in range(2):
                                    last = mm3(pe, PB[0:ROT, s % 4, q * 256:(q + 1) * 256], w(h // 2, o_qr + CQ * (h % 2) + ROT * q, ROT, R), (KR[0][:, h, :], KR[1][:, h, :]))
                                last.then_inc(in_ps, 1)
                            for s in range(8, 10):
                                for j in range(2):
                                    h = 2 * (s - 8) + j
                                    free(s, need=4 + h)
                                    for q in range(2):
                                        last = mm3(pe, PB[:, s % 4, j * 256:(j + 1) * 256], w(h // 2, O_CQ + 2 * K * (h % 2) + K * q, K, ROT),
                                                   (UU[0][:, h, q, :], UU[1][:, h, q, :]), first=q == 0, last=q == 1)
                                last.then_inc(in_ps, 1)
                            for s in range(10, 14):
                                h = s - 10
                                free(s, need=8 + h // 2)
                                for k in range(KD):
                                    last = mm3(pe, PB[:, s % 4, k * 256:(k + 1) * 256], w(h // 2, O_WQ + D * (h % 2) + P * k, P), (VV[0][:, h, :], VV[1][:, h, :]))
                                last.then_inc(in_ps, 1)
                        step(0, True)
                        with pe.Fori(1, ROUNDS) as g:
                            step(g)

        def plain_chain(tag, GS, VB, WO):
            with ExitStack() as ctx:
                CW = sbuf(ctx, "CW", [DC, B * L + 2 * D])
                CWS = split(ctx, "CWS", [DC, B * L + 2 * D])
                QO = sbuf(ctx, "QO", [P, 4, D])
                WQ = split(ctx, "WQ", [P, 2, D])
                MASK = sbuf(ctx, "MASK", [P, 8])
                KVF = sbuf(ctx, "KVF", [P, 4, B * L])
                KVH = sbuf(ctx, "KVH", [P, 4, B * L], F32R)
                KVL = sbuf(ctx, "KVL", [P, 4, B * L], F32R)
                KB = split(ctx, "KB", [P, 2, 512])
                PB = psum(ctx, "PB", [P, 4, 512])
                NB = psum(ctx, "NB", [P, 4, 512])
                nrm = norm(ctx, tag, [NB[:, j, :] for j in range(4)])
                loaded = sem(ctx, f"{tag}_loaded")
                w_hi, w_lo = sem(ctx, f"{tag}_w_hi"), sem(ctx, f"{tag}_w_lo")
                kv_ps, kv_hi, kv_lo = (sem(ctx, f"{tag}_kv_{s}") for s in ("in_psum", "hi", "lo"))
                kb_hi, kb_lo = sem(ctx, f"{tag}_kb_hi"), sem(ctx, f"{tag}_kb_lo")
                vb_hi, vb_lo = sem(ctx, f"{tag}_vb_hi"), sem(ctx, f"{tag}_vb_lo")
                g_ps, g_hi, g_lo = (sem(ctx, f"{tag}_g_{s}") for s in ("in_psum", "hi", "lo"))
                UNITS = [(b, j) for b in range(B) for j in range(2)]

                def spread(dst, src):
                    return (dst.rearrange("p (h l) -> p h l", h=8), src.bitcast(F32).unsqueeze(1).broadcast_to((P, 8, L)),
                            MASK[:, :].unsqueeze(2).broadcast_to((P, 8, L)), ALU.mult)

                with nc.Block() as block:
                    @block.sync
                    def _(sp):
                        sp.dma_start(CW[:, :], A[f"{tag}_cw"]).then_inc(loaded, 16)
                        sp.dma_start(MASK[:, :], A["headmask"]).then_inc(loaded, 16)
                        sp.dma_start(QO[:, :, :], A[f"{tag}_qo"]).then_inc(loaded, 16)

                    @block.tensor
                    def _(pe):
                        pe.wait_ge(w_lo, 1)
                        for j in range(2):
                            for q in range(2):
                                c = B * L + j * D + q * P
                                last = mm3(pe, PB[:, j, q * 256:(q + 1) * 256], (CWS[0][:, c:c + P], CWS[1][:, c:c + P]), (CWS[0][:, 0:B * L], CWS[1][:, 0:B * L]))
                            last.then_inc(kv_ps, 1)
                        nrm["tensor"](pe)
                        pe.wait_ge(w_lo, 3)
                        for u, (b, j) in enumerate(UNITS):
                            pe.wait_ge(kb_hi, u + 1)
                            pe.wait_ge(kb_lo, u + 1)
                            for k in range(KD):
                                n = 2 * u + k
                                if n >= 4:
                                    pe.wait_ge(g_lo, n - 3)
                                elif n < 2:
                                    pe.wait_ge(kv_lo, 2)
                                mm3(pe, PB[:, n % 4, :], (WQ[0][:, j, k * P:(k + 1) * P], WQ[1][:, j, k * P:(k + 1) * P]),
                                    (KB[0][:, u % 2, :], KB[1][:, u % 2, :])).then_inc(g_ps, 1)

                    @block.scalar
                    def _(act):
                        act.wait_ge(loaded, 48)
                        act.activation(CWS[0][:, :], CW[:, :], ACT.Copy).then_inc(w_hi, 1)
                        act.activation(WQ[0][:, :, :], QO[:, 0:2, :], ACT.Copy).then_inc(w_hi, 1)
                        act.activation(WO[0][:, :, :], QO[:, 2:4, :], ACT.Copy).then_inc(w_hi, 1)
                        for j in range(2):
                            act.wait_ge(kv_ps, j + 1)
                            act.activation(KVH[:, 2 * j:2 * j + 2, :].rearrange("p q n -> p (q n)"), PB[:, j, :], ACT.Copy).then_inc(kv_hi, 1)
                        nrm["scalar"](act)
                        for n in range(2 * len(UNITS)):
                            (b, j), k = UNITS[n // 2], n % 2
                            act.wait_ge(g_ps, n + 1)
                            act.activation(GS[0][:, k, b, j * 512:(j + 1) * 512], PB[:, n % 4, :], ACT.Copy).then_inc(g_hi, 1)

                    @block.gpsimd
                    def _(pool):
                        for n, (dst, src, full) in enumerate(((CWS[1][:, :], CWS[0][:, :], CW[:, :]), (WQ[1][:, :, :], WQ[0][:, :, :], QO[:, 0:2, :]),
                                                              (WO[1][:, :, :], WO[0][:, :, :], QO[:, 2:4, :]))):
                            pool.wait_ge(w_hi, n + 1)
                            pool.tensor_tensor(dst, full, src.bitcast(F32), ALU.subtract).then_inc(w_lo, 1)
                        pool.wait_ge(kv_lo, 2)
                        for u, (b, j) in enumerate(UNITS):
                            if u >= 2:
                                pool.wait_ge(g_ps, 2 * (u - 1))
                            pool.tensor_tensor(*spread(KB[1][:, u % 2, :], KVL[:, j, b * L:(b + 1) * L])).then_inc(kb_lo, 1)
                        for u, (b, j) in enumerate(UNITS):
                            pool.tensor_tensor(*spread(VB[1][:, j, b, :], KVL[:, 2 + j, b * L:(b + 1) * L])).then_inc(vb_lo, 1)

                    @block.vector
                    def _(dve):
                        nrm["vector"](dve)
                        for j in range(2):
                            dve.wait_ge(kv_hi, j + 1)
                            at = KVL[:, 2 * j:2 * j + 2, :].rearrange("p q n -> p (q n)")
                            dve.tensor_tensor(at, PB[:, j, :], KVH[:, 2 * j:2 * j + 2, :].bitcast(F32).rearrange("p q n -> p (q n)"), ALU.subtract).then_inc(kv_lo, 1)

                        def keys(u):
                            b, j = UNITS[u]
                            if u >= 2:
                                dve.wait_ge(g_ps, 2 * (u - 1))
                            dve.tensor_tensor(*spread(KB[0][:, u % 2, :], KVH[:, j, b * L:(b + 1) * L])).then_inc(kb_hi, 1)
                        keys(0)
                        keys(1)
                        nrm["vector_low"](dve)
                        for u, (b, j) in enumerate(UNITS):
                            for n in (2 * u, 2 * u + 1):
                                dve.wait_ge(g_hi, n + 1)
                                at = slice(j * 512, (j + 1) * 512)
                                dve.tensor_tensor(GS[1][:, n % 2, b, at], PB[:, n % 4, :], GS[0][:, n % 2, b, at].bitcast(F32), ALU.subtract).then_inc(g_lo, 1)
                            if u + 2 < len(UNITS):
                                keys(u + 2)
                            dve.tensor_tensor(*spread(VB[0][:, j, b, :], KVH[:, 2 + j, b * L:(b + 1) * L])).then_inc(vb_hi, 1)

        def attend(tag, GS, values, gate, scale, causal):
            with ExitStack() as ctx:
                Z = split(ctx, "Z", [P, 2, NP * D])
                DIFF = sbuf(ctx, "DIFF", [P, 2, H * L])
                PROB = sbuf(ctx, "PROB", [P, 2, H * L])
                AT = split(ctx, "ATT", [P, 2, NP * P])
                SM = sbuf(ctx, "SM", [P, 2, 3, H])
                SC = psum(ctx, "SC", [P, 2, 512])
                TR = psum(ctx, "TR", [P, 2, 512])
                ZP = psum(ctx, "ZP", [P, 2, 512])
                OP = psum(ctx, "OP", [P, 2, 512])
                scored, raw, masked = sem(ctx, f"{tag}_scored"), sem(ctx, f"{tag}_scores_copied"), sem(ctx, f"{tag}_scores_masked")
                smax, shifted, expd, ssum, normed = (sem(ctx, f"{tag}_{s}") for s in ("row_max", "shifted", "exponentials", "row_sums", "probabilities"))
                turned, at_hi, at_lo = (sem(ctx, f"{tag}_{s}") for s in ("turned", "at_hi", "at_lo"))
                z_ps, z_hi, z_lo = (sem(ctx, f"{tag}_{s}") for s in ("z_in_psum", "z_hi", "z_lo"))
                out_ps, added = sem(ctx, f"{tag}_out_in_psum"), sem(ctx, f"{tag}_added")
                stats = sem(ctx, f"{tag}_stats")
                ROUNDS = NP // 2

                def masks(t):
                    return causal and t % TB == 0

                def wide(ap):
                    return ap.rearrange("p (h l) -> p h l", l=L)

                def flat(bank):
                    return bank[:, :, :].rearrange("p a n -> p (a n)")

                with nc.Block() as block:
                    @block.tensor
                    def _(pe):
                        def score(t):
                            b = t // TB
                            if t >= 1:
                                pe.wait_ge(shifted, t)
                                if masks(t - 1):
                                    pe.wait_ge(raw, (t - 1) // TB + 1)
                            for j in range(2):
                                for k in range(KD):
                                    last = mm3(pe, SC[:, j, :], (xt[0][:, k, t * P:(t + 1) * P], xt[1][:, k, t * P:(t + 1) * P]),
                                               (GS[0][:, k, b, j * 512:(j + 1) * 512], GS[1][:, k, b, j * 512:(j + 1) * 512]), first=k == 0, last=k == KD - 1)
                            last.then_inc(scored, 1)

                        def value(n):
                            b, r = divmod(n, ROUNDS)
                            if n >= 2:
                                pe.wait_ge(z_lo, n - 1)
                            for q in range(2):
                                a, w = values(b, 2 * r + q)
                                last = mm3(pe, ZP[:, n % 2, q * D:(q + 1) * D], a, w)
                            last.then_inc(z_ps, 1)

                        def turn(t):
                            pe.wait_ge(normed, t + 1)
                            if t >= 1:
                                pe.wait_ge(at_lo, t)
                            for pair in range(NP):
                                last = pe.transpose(TR[:, pair // 4, (pair % 4) * P:(pair % 4 + 1) * P], PROB[:, t % 2, pair * P:(pair + 1) * P], IDENT[:, :])
                            last.then_inc(turned, 1)

                        def mix(t):
                            pe.wait_ge(at_lo, t + 1)
                            pe.wait_ge(z_lo, ROUNDS * (t // TB + 1))
                            if t >= 2:
                                pe.wait_ge(added, t - 1)
                            for pair in range(NP):
                                last = mm3(pe, OP[:, t % 2, 0:D], (AT[0][:, t % 2, pair * P:(pair + 1) * P], AT[1][:, t % 2, pair * P:(pair + 1) * P]),
                                           (Z[0][:, t // TB % 2, pair * D:(pair + 1) * D], Z[1][:, t // TB % 2, pair * D:(pair + 1) * D]), first=pair == 0, last=pair == NP - 1)
                            last.then_inc(out_ps, 1)

                        for i in range(T + 2):
                            if i < T:
                                score(i)
                                value(2 * i)
                            if 1 <= i <= T:
                                turn(i - 1)
                            if i < T:
                                value(2 * i + 1)
                            if i >= 2:
                                mix(i - 2)

                    @block.scalar
                    def _(act):
                        def z_high(n):
                            b, r = divmod(n, ROUNDS)
                            act.wait_ge(z_ps, n + 1)
                            if b >= 2:
                                act.wait_ge(out_ps, TB * (b - 1))
                            act.activation(Z[0][:, b % 2, 2 * r * D:2 * (r + 1) * D], ZP[:, n % 2, :], ACT.Copy).then_inc(z_hi, 1)

                        for i in range(T + 1):
                            if i < T:
                                if masks(i):
                                    act.wait_ge(scored, i + 1)
                                    if i >= 2:
                                        act.wait_ge(normed, i - 1)
                                    act.activation(DIFF[:, i % 2, :], flat(SC), ACT.Copy).then_inc(raw, 1)
                                z_high(2 * i)
                                act.wait_ge(shifted, i + 1)
                                act.activation(DIFF[:, i % 2, :], DIFF[:, i % 2, :], ACT.Exp, scale=scale).then_inc(expd, 1)
                            if i >= 1:
                                act.wait_ge(turned, i)
                                if i >= 3:
                                    act.wait_ge(out_ps, i - 2)
                                act.activation(AT[0][:, (i - 1) % 2, :], flat(TR), ACT.Copy).then_inc(at_hi, 1)
                            if i < T:
                                z_high(2 * i + 1)

                    @block.gpsimd
                    def _(pool):
                        for t in range(T):
                            if masks(t):
                                pool.wait_ge(raw, t // TB + 1)
                                at = wide(DIFF[:, t % 2, :])
                                pool.affine_select(out=at, in_=at, compare_op=ALU.is_ge, fill=FMIN, base=0, pattern=[[0, H], [-1, L]], channel_multiplier=1).then_inc(masked, 1)
                            pool.wait_ge(ssum, 2 * t + 2)
                            if t >= 2:
                                pool.wait_ge(turned, t - 1)
                            pool.tensor_tensor(wide(PROB[:, t % 2, :]), wide(DIFF[:, t % 2, :]), SM[:, t % 2, 2, :].unsqueeze(2).broadcast_to((P, H, L)), ALU.mult).then_inc(normed, 1)

                    @block.vector
                    def _(dve):
                        def z_low(n):
                            b, r = divmod(n, ROUNDS)
                            at = slice(2 * r * D, 2 * (r + 1) * D)
                            dve.wait_ge(z_hi, n + 1)
                            dve.tensor_tensor(Z[1][:, b % 2, at], ZP[:, n % 2, :], Z[0][:, b % 2, at].bitcast(F32), ALU.subtract).then_inc(z_lo, 1)

                        def shift(t):
                            if masks(t):
                                dve.wait_ge(masked, t // TB + 1)
                                src = wide(DIFF[:, t % 2, :])
                            else:
                                dve.wait_ge(scored, t + 1)
                                src = wide(flat(SC))
                            if t >= 2:
                                dve.wait_ge(normed, t - 1)
                            dve.tensor_reduce(SM[:, t % 2, 0, :], src, AX, ALU.max).then_inc(smax, 1)
                            dve.wait_ge(smax, t + 1)
                            dve.tensor_tensor(wide(DIFF[:, t % 2, :]), src, SM[:, t % 2, 0, :].unsqueeze(2).broadcast_to((P, H, L)), ALU.subtract).then_inc(shifted, 1)

                        def sums(t):
                            dve.wait_ge(expd, t + 1)
                            dve.tensor_reduce(SM[:, t % 2, 1, :], wide(DIFF[:, t % 2, :]), AX, ALU.add).then_inc(ssum, 1)
                            dve.wait_ge(ssum, 2 * t + 1)
                            dve.reciprocal(SM[:, t % 2, 2, :], SM[:, t % 2, 1, :]).then_inc(ssum, 1)

                        def add(t):
                            dve.wait_ge(out_ps, t + 1)
                            dve.scalar_tensor_tensor(out=X[:, t, :], in0=OP[:, t % 2, 0:D], scalar=GATE[:, gate:gate + 1], in1=X[:, t, :],
                                                     op0=ALU.mult, op1=ALU.add).then_inc(added, 1)

                        for i in range(T + 2):
                            if i >= 3:
                                add(i - 3)
                            if i < T:
                                shift(i)
                                z_low(2 * i)
                                sums(i)
                            if 1 <= i <= T:
                                at = (i - 1) % 2
                                dve.wait_ge(at_hi, i)
                                dve.tensor_tensor(AT[1][:, at, :], flat(TR), AT[0][:, at, :].bitcast(F32), ALU.subtract).then_inc(at_lo, 1)
                            if i < T:
                                z_low(2 * i + 1)
                        add(T - 1)

        def ternary(gate):
            NF = 8
            with ExitStack() as ctx:
                WT = sbuf(ctx, "WT", [P, 2, 2048])
                LE = sbuf(ctx, "LE", [P, 2048])
                WQT = sbuf(ctx, "WQT", [P, 2, 2048], F32R)
                ASUM = sbuf(ctx, "ASUM", [P, 2])
                THR = sbuf(ctx, "THR", [P, 2, 2])
                B1 = sbuf(ctx, "B1", [P, NF])
                B2 = sbuf(ctx, "B2", [P, D])
                B2G = sbuf(ctx, "B2G", [P, D])
                HF = sbuf(ctx, "HF", [P, 2, HALF])
                HS = split(ctx, "HS", [P, NF, B * S])
                UP = psum(ctx, "UP", [P, 4, 512])
                NB = psum(ctx, "NB", [P, 4, 512])
                nrm = norm(ctx, "f1", [NB[:, j, :] for j in range(4)])
                w_in, b_in = sem(ctx, "w_in"), sem(ctx, "b_in")
                quant = Count(sem(ctx, "quantise_steps"))
                sums_ready, mean_ps = sem(ctx, "sums_ready"), sem(ctx, "mean_in_psum")
                wq_ready = sem(ctx, "ternary_ready")
                b2_ready, b2_added = sem(ctx, "b2_ready"), sem(ctx, "b2_added")
                up_done, gelu_done, h_hi, h_lo = (sem(ctx, s) for s in ("up_done", "gelu_done", "h_hi", "h_lo"))
                down_done, added = sem(ctx, "down_done"), sem(ctx, "added")
                CHUNKS = [(half, f) for half in range(2) for f in range(NF)]
                with nc.Block() as block:
                    @block.sync
                    def _(sp):
                        sp.dma_start(WT[:, :, :], A["f1_w"]).then_inc(w_in, 16)
                        sp.dma_start(B1[:, :], A["f1_b1"]).then_inc(b_in, 16)
                        sp.dma_start(B2[:, :], A["f1_b2"]).then_inc(b_in, 16)

                    @block.gpsimd
                    def _(pool):
                        pool.wait_ge(b2_ready, 1)
                        pool.wait_ge(nrm["xn_ready"], T)
                        pool.tensor_tensor(X[:, :, :], X[:, :, :], B2G[:, :].unsqueeze(1).broadcast_to((P, T, D)), ALU.add).then_inc(b2_added, 1)

                    @block.vector
                    def _(dve):
                        nrm["vector"](dve)
                        dve.wait_ge(w_in, 16)
                        for i in range(2):
                            dve.tensor_reduce(ASUM[:, i:i + 1], WT[:, i, :], AX, ALU.add, apply_absolute_value=True).then_inc(sums_ready, 1)
                        nrm["vector_low"](dve)
                        dve.wait_ge(mean_ps, 1)
                        quant.inc(dve.tensor_scalar(THR[:, 0, :], UP[:, 0, 0:2], 1.0 / (P * 2048), 0.7, ALU.mult, ALU.mult))
                        quant.wait(dve)
                        quant.inc(dve.tensor_scalar(THR[:, 1, :], THR[:, 0, :], -1.0, None, ALU.mult))
                        quant.wait(dve)
                        for i in range(2):
                            quant.inc(dve.tensor_scalar(LE[:, :], WT[:, i, :], THR[:, 1, i:i + 1], None, ALU.is_le))
                            quant.wait(dve)
                            dve.scalar_tensor_tensor(out=WQT[:, i, :], in0=WT[:, i, :], scalar=THR[:, 0, i:i + 1], in1=LE[:, :],
                                                     op0=ALU.is_ge, op1=ALU.subtract).then_inc(wq_ready, 1)
                            dve.wait_ge(wq_ready, i + 1)
                        dve.wait_ge(b_in, 32)
                        dve.tensor_scalar(B2G[:, :], B2[:, :], GATE[:, gate:gate + 1], None, ALU.mult).then_inc(b2_ready, 1)

                        def parts(n):
                            half, f = CHUNKS[n]
                            at = slice(half * HALF, (half + 1) * HALF)
                            dve.wait_ge(gelu_done, n + 1)
                            dve.tensor_copy(HS[0][:, f, at], HF[:, n % 2, :]).then_inc(h_hi, 1)
                            dve.wait_ge(h_hi, n + 1)
                            dve.tensor_tensor(HS[1][:, f, at], HF[:, n % 2, :], HS[0][:, f, at].bitcast(F32), ALU.subtract).then_inc(h_lo, 1)

                        def add(t):
                            if t == 0:
                                dve.wait_ge(b2_added, 1)
                            dve.wait_ge(down_done, t + 1)
                            dve.scalar_tensor_tensor(out=X[:, t, :], in0=NB[:, t % 4, 0:D], scalar=GATE[:, gate:gate + 1], in1=X[:, t, :],
                                                     op0=ALU.mult, op1=ALU.add).then_inc(added, 1)
                        for n in range(2 * NF):
                            parts(n)
                        for t in range(T):
                            add(t)

                    @block.scalar
                    def _(act):
                        nrm["scalar"](act)
                        act.wait_ge(b_in, 32)
                        for n, (half, f) in enumerate(CHUNKS):
                            act.wait_ge(up_done, n + 1)
                            if n >= 2:
                                act.wait_ge(h_lo, n - 1)
                            act.activation(HF[:, n % 2, :], UP[:, n % 4, :], ACT.Gelu, bias=B1[:, f:f + 1]).then_inc(gelu_done, 1)

                    @block.tensor
                    def _(pe):
                        pe.wait_ge(sums_ready, 2)
                        pe.matmul(UP[:, 0, 0:2], ONES[:, :], ASUM[:, :], start=True, stop=True).then_inc(mean_ps, 1)
                        nrm["tensor"](pe)
                        pe.wait_ge(nrm["ready"], 4)
                        pe.wait_ge(wq_ready, 1)
                        for n, (half, f) in enumerate(CHUNKS):
                            if n >= 4:
                                pe.wait_ge(gelu_done, n - 3)
                            for k in range(KD):
                                for i in range(2):
                                    last = pe.matmul(UP[:, n % 4, :], WQT[:, 0, k * 1024 + f * P:k * 1024 + (f + 1) * P], xt[i][:, k, half * HALF:(half + 1) * HALF],
                                                     start=k + i == 0, stop=k + i == KD)
                            last.then_inc(up_done, 1)
                        pe.wait_ge(wq_ready, 2)
                        for t in range(T):
                            pe.wait_ge(h_lo, NF * (t // 4 + 1))
                            if t >= 4:
                                pe.wait_ge(added, t - 3)
                            for f in range(NF):
                                for i in range(2):
                                    last = pe.matmul(NB[:, t % 4, 0:D], HS[i][:, f, t * P:(t + 1) * P], WQT[:, 1, f * D:(f + 1) * D], start=f + i == 0, stop=f + i == NF)
                            last.then_inc(down_done, 1)

        def int8(gate):
            with ExitStack() as ctx:
                WF = sbuf(ctx, "WF", [P, KD, D])
                WR = sbuf(ctx, "WR", [P, KD, D])
                WQ = sbuf(ctx, "WQ8", [P, KD, D], BF16)
                WQT = sbuf(ctx, "WQT8", [P, KD, D], BF16)
                WM = sbuf(ctx, "WM", [P, 4, KD])
                WMH = sbuf(ctx, "WMH", [P, KD], F32R)
                WML = sbuf(ctx, "WML", [P, KD])
                IDENTR = sbuf(ctx, "IDENTR", [P, P], F32R)
                WSC = split(ctx, "WSC", [P, KD, P])
                WSB = sbuf(ctx, "WSB", [P, D])
                BI = sbuf(ctx, "BI", [P, D])
                BIG = sbuf(ctx, "BIG", [P, D])
                XR = sbuf(ctx, "XR", [P, T, D])
                XQ = sbuf(ctx, "XQ8", [P, T, D], BF16)
                XQT = sbuf(ctx, "XQT8", [P, KD, B * S], BF16)
                XM = sbuf(ctx, "XM", [P, 3, T])
                YS = sbuf(ctx, "YS", [P, 2, D])
                TP = psum(ctx, "TP", [P, 2, 1024], BF16)
                WP = psum(ctx, "WP", [P, 512], BF16)
                SP = psum(ctx, "SP", [P, 512])
                OP = psum(ctx, "OP", [P, 4, 512])
                nrm = norm(ctx, "f2", None)
                loaded = sem(ctx, "loaded")
                wst = Count(sem(ctx, "weight_steps"))
                xst = Count(sem(ctx, "token_steps"))
                ws_ready, wq_ready, x_ready = sem(ctx, "scales_ready"), sem(ctx, "weights_ready"), sem(ctx, "tokens_ready")
                ws_ps, wt_ps, wt_ready, xt_ps, xt_sb = (sem(ctx, s) for s in ("scales_in_psum", "weights_turned", "weights_there", "tokens_turned", "tokens_there"))
                out_ps, added = sem(ctx, "out_in_psum"), sem(ctx, "added")
                bias_ready, bias_added = sem(ctx, "bias_ready"), sem(ctx, "bias_added")
                ysteps = sem(ctx, "scaled")

                def rounded(dve, count, dst, tmp, src, inv):
                    count.inc(dve.tensor_scalar(tmp, src, inv, MAGIC, ALU.mult, ALU.add))
                    count.wait(dve)
                    count.inc(dve.tensor_scalar(tmp, tmp, MAGIC, 127.0, ALU.subtract, ALU.min))
                    count.wait(dve)
                    return dve.tensor_scalar(dst, tmp, -128.0, None, ALU.max)

                with nc.Block() as block:
                    @block.sync
                    def _(sp):
                        sp.dma_start(WF[:, :, :], A["f2_w"].rearrange("(k p) d -> p k d", p=P)).then_inc(loaded, 16)
                        sp.dma_start(BI[:, :], A["f2_bias"]).then_inc(loaded, 16)

                    @block.gpsimd
                    def _(pool):
                        pool.wait_ge(bias_ready, 1)
                        pool.wait_ge(nrm["xn_ready"], T)
                        pool.tensor_tensor(X[:, :, :], X[:, :, :], BIG[:, :].unsqueeze(1).broadcast_to((P, T, D)), ALU.add).then_inc(bias_added, 1)

                    @block.scalar
                    def _(act):
                        nrm["scalar"](act, high=False)
                        act.wait_ge(wt_ps, 1)
                        act.activation(WQT[:, :, :].rearrange("p k o -> p (k o)"), WP[:, :], ACT.Copy).then_inc(wt_ready, 1)
                        for h in range(2):
                            act.wait_ge(xt_ps, h + 1)
                            act.activation(XQT[:, :, h * HALF:(h + 1) * HALF], TP[:, h, :].rearrange("p (k n) -> p k n", k=KD), ACT.Copy).then_inc(xt_sb, 1)

                    @block.vector
                    def _(dve):
                        nrm["vector"](dve)
                        for h in range(2):
                            t4 = slice(4 * h, 4 * h + 4)
                            dve.wait_ge(nrm["xn_ready"], 4 * (h + 1))
                            xst.inc(dve.tensor_reduce(XM[:, 0, t4], XN[:, t4, :], AX, ALU.max, apply_absolute_value=True))
                            xst.wait(dve)
                            xst.inc(dve.tensor_scalar(XM[:, 1, t4], XM[:, 0, t4], 1.0 / 127.0, 1e-12, ALU.mult, ALU.max))
                            xst.wait(dve)
                            xst.inc(dve.reciprocal(XM[:, 2, t4], XM[:, 1, t4]))
                            xst.wait(dve)
                            for t in range(4 * h, 4 * h + 4):
                                xst.inc(dve.tensor_scalar(XR[:, t, :], XN[:, t, :], XM[:, 2, t:t + 1], MAGIC, ALU.mult, ALU.add))
                            xst.wait(dve)
                            xst.inc(dve.tensor_scalar(XR[:, t4, :], XR[:, t4, :], MAGIC, 127.0, ALU.subtract, ALU.min))
                            xst.wait(dve)
                            dve.tensor_scalar(XQ[:, t4, :], XR[:, t4, :], -128.0, None, ALU.max).then_inc(x_ready, 1)
                        dve.wait_ge(loaded, 32)
                        wst.inc(dve.tensor_reduce(WM[:, 0, :], WF[:, :, :], AX, ALU.max, apply_absolute_value=True))
                        wst.wait(dve)
                        wst.inc(dve.tensor_scalar(WM[:, 2, :], WM[:, 0, :], 1e-8, 1.0 / 127.0, ALU.max, ALU.mult))
                        wst.wait(dve)
                        wst.inc(dve.tensor_copy(WMH[:, :], WM[:, 2, :]))
                        wst.wait(dve)
                        wst.inc(dve.tensor_tensor(WML[:, :], WM[:, 2, :], WMH[:, :].bitcast(F32), ALU.subtract))
                        wst.wait(dve)
                        dve.tensor_copy(IDENTR[:, :], IDENT[:, :]).then_inc(ws_ready, 1)
                        for i, part in enumerate((WMH[:, :].bitcast(F32), WML[:, :])):
                            for k in range(KD):
                                dve.tensor_scalar(WSC[i][:, k, :], ONES[:, :], part[:, k:k + 1], None, ALU.mult).then_inc(ws_ready, 1)
                        wst.inc(dve.reciprocal(WM[:, 3, :], WM[:, 2, :]))
                        wst.wait(dve)
                        for k in range(KD):
                            rounded(dve, wst, WQ[:, k, :], WR[:, k, :], WF[:, k, :], WM[:, 3, k:k + 1]).then_inc(wq_ready, 1)
                        dve.tensor_scalar(BIG[:, :], BI[:, :], GATE[:, gate:gate + 1], None, ALU.mult).then_inc(bias_ready, 1)
                        dve.wait_ge(ws_ps, 1)
                        wst.inc(dve.tensor_copy(WSB[:, :], SP[:, 0:D]))
                        wst.wait(dve)
                        dve.wait_ge(bias_added, 1)
                        for t in range(T):
                            dve.wait_ge(out_ps, t + 1)
                            dve.scalar_tensor_tensor(out=YS[:, t % 2, :], in0=OP[:, t % 4, 0:D], scalar=XM[:, 1, t:t + 1], in1=WSB[:, :],
                                                     op0=ALU.mult, op1=ALU.mult).then_inc(ysteps, 1)
                            dve.wait_ge(ysteps, t + 1)
                            dve.scalar_tensor_tensor(out=X[:, t, :], in0=YS[:, t % 2, :], scalar=GATE[:, gate:gate + 1], in1=X[:, t, :],
                                                     op0=ALU.mult, op1=ALU.add).then_inc(added, 1)

                    @block.tensor
                    def _(pe):
                        def turn_tokens(h):
                            pe.wait_ge(x_ready, h + 1)
                            for k in range(KD):
                                for q in range(4):
                                    last = pe.transpose(TP[:, h, k * HALF + q * P:k * HALF + (q + 1) * P], XQ[:, 4 * h + q, k * P:(k + 1) * P], IDENTB[:, :])
                            last.then_inc(xt_ps, 1)
                        turn_tokens(0)
                        turn_tokens(1)
                        pe.wait_ge(ws_ready, 1 + 2 * KD)
                        for k in range(KD):
                            for i in range(2):
                                last = pe.matmul(SP[:, k * P:(k + 1) * P], WSC[i][:, k, :], IDENTR[:, :], start=i == 0, stop=i == 1)
                        last.then_inc(ws_ps, 1)
                        pe.wait_ge(wq_ready, KD)
                        for k in range(KD):
                            for o in range(KD):
                                last = pe.transpose(WP[:, k * D + o * P:k * D + (o + 1) * P], WQ[:, o, k * P:(k + 1) * P], IDENTB[:, :])
                        last.then_inc(wt_ps, 1)
                        pe.wait_ge(wt_ready, 1)
                        for t in range(T):
                            pe.wait_ge(xt_sb, t // 4 + 1)
                            if t >= 4:
                                pe.wait_ge(added, t - 3)
                            for k in range(KD):
                                last = pe.matmul(OP[:, t % 4, 0:D], XQT[:, k, t * P:(t + 1) * P], WQT[:, k, :], start=k == 0, stop=k == KD - 1)
                            last.then_inc(out_ps, 1)

        with ExitStack() as ctx:
            phase[0] = "attn0_"
            Y = split(ctx, "Y", [P, NP * D])
            AT = split(ctx, "AT", [P, NP * B * S])
            latent_rope(Y, AT)
            phase[0] = "attn0_out_"
            latent_out(Y, AT, 0)
        phase[0] = "ffn0_"
        experts("f0", 4, 9, 3, 16, 6, True)
        with ExitStack() as ctx:
            phase[0] = "chain1_"
            GS = split(ctx, "GS", [P, KD, B, H * L])
            Y = split(ctx, "Y", [P, NP * D])
            latent_chain(GS, Y)

            def latent_values(b, pair):
                at = slice(pair * D, (pair + 1) * D)
                return (KVB[0][:, b, :], KVB[1][:, b, :]), (Y[0][:, at], Y[1][:, at])
            phase[0] = "attn1_"
            attend("a1", GS, latent_values, 1, 1.0, False)
        phase[0] = "ffn1_"
        ternary(5)
        clear_semaphores()
        for layer in (2, 3):
            with ExitStack() as ctx:
                phase[0] = f"chain{layer}_"
                GS = split(ctx, "GS", [P, KD, B, H * L])
                VB = split(ctx, "VB", [P, 2, B, 512])
                WO = split(ctx, "WO", [P, 2, D])
                plain_chain(f"a{layer}", GS, VB, WO)

                def values(b, pair):
                    j, c = pair // 4, (pair % 4) * P
                    return (VB[0][:, j, b, c:c + P], VB[1][:, j, b, c:c + P]), (WO[0][:, j, :], WO[1][:, j, :])
                phase[0] = f"attn{layer}_"
                attend(f"b{layer}", GS, values, layer, 0.25, True)
            if layer == 2:
                phase[0] = "ffn2_"
                int8(6)
                clear_semaphores()
        phase[0] = "ffn3_"
        experts("f3", 7, 9, 4, 8, 2, False)
        phase[0] = ""

        with ExitStack() as ctx:
            stored = sem(ctx, "stored")
            with nc.Block() as block:
                @block.sync
                def _(sp):
                    sp.dma_start(out.rearrange("(t p) d -> p t d", p=P), X[:, :, :]).then_inc(stored, 16)
                    sp.wait_ge(stored, 16)


def rope_table(length, dim):
    inv = (np.float32(1.0) / np.power(np.float32(10000.0), np.arange(0, dim, 2, dtype=np.float32) / np.float32(dim))).astype(np.float32)
    f = np.arange(length, dtype=np.float32)[:, None] * inv[None, :]
    return np.repeat(np.sin(f), 2, axis=-1).astype(np.float32), np.repeat(np.cos(f), 2, axis=-1).astype(np.float32)


def constants():
    sin, cos = rope_table(L, DC)
    sin = np.concatenate([-sin[:, :DC // 2], sin[:, DC // 2:]], axis=1)
    qsin, qcos = rope_table(S, CQ)
    c = {
        "ident": np.eye(P, dtype=np.float32),
        "kcos": np.tile(cos.T, (2, B)), "ksin": np.tile(sin.T, (2, B)),
        "qcos": np.stack([qcos.T[:ROT], qcos.T[ROT:]], 1), "qsin": np.stack([qsin.T[ROT:], -qsin.T[:ROT]], 1),
        "headmask": (np.arange(P)[:, None] // 16 == np.arange(8)[None, :]).astype(np.float32),
    }
    for e in (8, 16):
        c[f"before{e}"] = np.broadcast_to((np.arange(e)[None, :] < np.arange(e)[:, None]).astype(np.float32).reshape(1, e * e), (P, e * e))
    return {k: np.ascontiguousarray(v, dtype=np.float32) for k, v in c.items()}


def pairs(layer, Wq, w_kc_q, w_kc_kv, W_qr, W_kr, Wo):
    o_qr, o_kr, o_ck, o_wo, width = pair_columns(layer)
    w = np.zeros((NP, P, width), np.float32)
    for h in range(H):
        p, j = divmod(h, 2)
        w[p, :, O_WQ + D * j:O_WQ + D * (j + 1)] = Wq[h * K:(h + 1) * K]
        if layer == 0:
            w[p, :, O_CQ + CQ * j:O_CQ + CQ * (j + 1)] = w_kc_q[h]
        else:
            for q in range(2):
                c = O_CQ + 2 * K * j + K * q
                w[p, :ROT, c:c + K] = w_kc_q[h][:, ROT * q:ROT * (q + 1)].T
        w[p, :R, o_qr + CQ * j:o_qr + CQ * (j + 1)] = W_qr[h].T
        w[p, :DC, o_kr + R * j:o_kr + R * (j + 1)] = W_kr[h]
        w[p, :, o_ck + P * j + DC * j:o_ck + P * j + DC * (j + 1)] = w_kc_kv[h]
        w[p, :, o_wo + D * j:o_wo + D * (j + 1)] = Wo[:, h * K:(h + 1) * K].T
    return w


def expert_pairs(a):
    n, hid = 18, 176
    up = np.zeros((n // 2, P, 3, KD, 2, P), np.float32)
    down = np.zeros((n // 2, P, 4, D), np.float32)
    bias = np.zeros((P, n // 2, 3, 2), np.float32)
    for e in range(n):
        if e < 16:
            g, u, gb, ub, d = a["w1"][e], a["w3"][e], a["b1"][e], a["b3"][e], a["w2"][e]
        else:
            s = slice(hid * (e - 16), hid * (e - 15))
            g, u, gb, ub, d = a["ws1"][s], a["ws3"][s], a["bs1"][s], a["bs3"][s], a["ws2"][:, s]
        p, j = divmod(e, 2)
        for chunk, tile, to, rows in ((2 * j, 3 * j, 0, slice(0, P)), (1, 1 + j, 64 * j, slice(P, hid))):
            k = rows.stop - rows.start
            for m, w in ((0, g), (1, u)):
                up[p, :, chunk, :, m, to:to + k] = w[rows].T.reshape(KD, P, k).transpose(1, 0, 2)
            down[p, to:to + k, tile] = d[:, rows].T
            bias[to:to + k, p, chunk, 0], bias[to:to + k, p, chunk, 1] = gb[rows], ub[rows]
    return up.reshape(n // 2, P, -1), down.reshape(n // 2, P, -1), bias.reshape(P, -1)


def layout(i):
    i = {k: np.asarray(v) for k, v in i.items()}
    a = constants()
    a["x"] = i["x"].reshape(B * S, D)
    a["gates"] = np.broadcast_to(np.concatenate([i["g_xattn"], i["g_ffn"]])[None], (P, 8))
    ctxT = i["ctx_512"].reshape(B * L, DC).T
    a["kvT"] = np.concatenate([ctxT, ctxT])
    swapped = np.concatenate([ctxT[DC // 2:], ctxT[:DC // 2]])
    a["kvT_swapped"] = np.concatenate([swapped, swapped])
    for l in (0, 1):
        a[f"L{l}_pairs"] = pairs(l, *(i[f"L{l}_xattn_{n}"] for n in ("Wq", "w_kc_q", "w_kc_kv", "W_qr", "W_kr", "Wo")))
    f0 = {k[7:]: v for k, v in i.items() if k.startswith("L0_ffn_")}
    a["f0_up"], a["f0_down"], a["f0_bias"] = expert_pairs(f0)
    a["f0_router"] = f0["gate_w"].T.reshape(KD, P, 16).transpose(1, 0, 2)
    a["f0_router_bias"] = np.broadcast_to(f0["gate_b"][None], (P, 16))
    a["f0_b2"] = np.concatenate([f0["b2"], f0["bs2"][None]])
    w1, w2 = i["L1_ffn_w1"], i["L1_ffn_w2"]
    a["f1_w"] = np.stack([w1.T.reshape(KD, P, 1024).transpose(1, 0, 2).reshape(P, 2048), w2.T.reshape(8, P, D).transpose(1, 0, 2).reshape(P, 2048)], 1)
    a["f1_b1"] = i["L1_ffn_b1"].reshape(8, P).T
    a["f1_b2"] = np.broadcast_to(i["L1_ffn_b2"][None], (P, D))
    for l in (2, 3):
        a[f"a{l}_cw"] = np.concatenate([ctxT, i[f"L{l}_xattn_Wkv_expand"].T], axis=1)
        a[f"a{l}_qo"] = np.concatenate([i[f"L{l}_xattn_Wq"].reshape(2, P, D), i[f"L{l}_xattn_Wout"].T.reshape(2, P, D)]).transpose(1, 0, 2)
    a["f2_w"] = i["L2_ffn_weight"]
    a["f2_bias"] = np.broadcast_to(i["L2_ffn_bias"][None], (P, D))
    gu = np.concatenate([i["L3_ffn_w_gate_up"], i["L3_ffn_shared_gate_up"][None]])
    gu = gu.reshape(9, KD, P, 2, 4, P)
    a["f3_up"] = gu.transpose(0, 2, 4, 1, 3, 5).reshape(9, P, -1)
    dn = np.concatenate([i["L3_ffn_w_down"], i["L3_ffn_shared_down"][None]])
    a["f3_down"] = dn.reshape(9, 4, P, D).transpose(0, 2, 1, 3).reshape(9, P, -1)
    a["f3_router"] = i["L3_ffn_gate_w"].reshape(KD, P, 8).transpose(1, 0, 2)
    return {k: np.ascontiguousarray(v) for k, v in a.items()}


def kernel(**inputs):
    import concourse.bacc as bacc
    from concourse.bass_utils import run_bass_kernel_spmd

    nc = bacc.Bacc("TRN2", target_bir_lowering=False, num_devices=1)
    arrays = {f"in_{k}": v for k, v in layout(inputs).items()}
    aps = {k[3:]: nc.dram_tensor(k, v.shape, mybir.dt.from_np(v.dtype), kind="ExternalInput").ap() for k, v in arrays.items()}
    out = nc.dram_tensor("out_x", (B * S, D), F32, kind="ExternalOutput").ap()
    program(nc, aps, out)
    r = run_bass_kernel_spmd(nc, [arrays], core_ids=[0])
    return r.results[0]["out_x"].reshape(B, S, D)
```

```python
from contextlib import ExitStack

import numpy as np

import concourse.bass as bass
from concourse import mybir

P = 128
F32 = mybir.dt.float32
F32R = mybir.dt.float32r
BF16 = mybir.dt.bfloat16
ALU = mybir.AluOpType
ACT = mybir.ActivationFunctionType
AX = mybir.AxisListType.X

B, S, D = 4, 256, 256
L, DC = 64, 64
T = B * S // P
TB = S // P
KD = D // P
H = 16
NP = H // 2
HALF = B * S // 2
MAGIC = 12582912.0
MASKED = -2.0 ** 127

ROT, CQ, R, K = 96, 192, 64, 128
O_WQ = 0
O_CQ = O_WQ + 2 * D
CQ_N = {0: 2 * CQ, 1: 2 * 2 * K}


def pair_columns(layer):
    o_kr = O_CQ + CQ_N[layer]
    o_ck = o_kr + 2 * R
    o_wo = o_ck + 2 * 2 * DC
    o_qr = o_wo + 2 * D
    return o_qr, o_kr, o_ck, o_wo, o_qr + 2 * CQ


class Count:

    def __init__(self, sem):
        self.sem, self.n, self.grow = sem, 0, None

    def inc(self, ins):
        ins.then_inc(self.sem, 1)
        self.n += 1
        return self.n

    def wait(self, eng, n=None):
        n = self.n if n is None else n
        eng.wait_ge(self.sem, n if self.grow is None else self.grow[0] * self.grow[1] + n)

    def inside(self, i, per):
        self.grow, self.start = (i, per), self.n

    def outside(self, trips):
        assert self.n - self.start == self.grow[1]
        self.n = self.start + self.grow[1] * trips
        self.grow = None


def mm3(pe, out, a, b, first=True, last=True):
    pe.matmul(out, a[0], b[0], start=first, stop=False)
    pe.matmul(out, a[0], b[1], start=False, stop=False)
    return pe.matmul(out, a[1], b[0], start=False, stop=last)


def program(nc, A, out):
    with ExitStack() as top:
        phase = [""]

        def sbuf(ctx, name, shape, dt=F32):
            return ctx.enter_context(nc.sbuf_tensor(phase[0] + name, shape, dt))

        def split(ctx, name, shape):
            return sbuf(ctx, name + "_hi", shape, F32R), sbuf(ctx, name + "_lo", shape, F32R)

        def psum(ctx, name, shape, dt=F32):
            return ctx.enter_context(nc.psum_tensor(phase[0] + name, shape, dt))

        used = []

        def sem(ctx, name):
            used.append(nc.alloc_semaphore(phase[0] + name))
            return used[-1]

        def clear_semaphores():
            nc.clear_and_free_semaphores(list(used))
            nc.all_engine_barrier()
            used.clear()

        X = sbuf(top, "X", [P, T, D])
        XN = sbuf(top, "XN", [P, T, D])
        XT = split(top, "XT", [P, KD, B * S])
        IDENT = sbuf(top, "IDENT", [P, P])
        IDENTB = sbuf(top, "IDENTB", [P, P], BF16)
        ONES = sbuf(top, "ONES", [P, P])
        EPS = sbuf(top, "EPS", [P, 1])
        GATE = sbuf(top, "GATE", [P, 8])
        STATS = sbuf(top, "STATS", [P, T, 6])
        MOM = sbuf(top, "MOM", [P, T, 2])
        STD = sbuf(top, "STD", [P, T])
        RSTD = sbuf(top, "RSTD", [P, T])
        KV = split(top, "KV", [P, B * L])
        KVB = split(top, "KVB", [P, B, 2 * L])
        MASK = sbuf(top, "CAUSAL", [P, L], BF16)

        xt = (XT[0], XT[1])

        def measure(dve, stats, t):
            dve.bn_stats(STATS[:, t, :], X[:, t, :]).then_inc(stats, 1)
            dve.wait_ge(stats, t + 1)
            dve.bn_aggr(MOM[:, t, :], STATS[:, t, :])

        with ExitStack() as ctx:
            kvt = sbuf(ctx, "kvt", [P, B * L])
            kvs = sbuf(ctx, "kvs", [P, B * L])
            kcos = sbuf(ctx, "kcos", [P, B * L])
            ksin = sbuf(ctx, "ksin", [P, B * L])
            prod = sbuf(ctx, "prod", [P, 2, B * L])
            graw = sbuf(ctx, "graw", [P, 8])
            loaded = sem(ctx, "loaded")
            x_loaded = sem(ctx, "x_loaded")
            gates_done = sem(ctx, "gates_done")
            rope = Count(sem(ctx, "rope_done"))
            maskf = sbuf(ctx, "maskf", [P, L])
            mask_steps = sem(ctx, "mask_steps")
            x_stats = sem(ctx, "x_measured")
            with nc.Block() as block:
                @block.sync
                def _(sp):
                    for dst, src in ((graw, "gates"), (IDENT, "ident"), (kvt, "kvT"), (kvs, "kvT_swapped"), (kcos, "kcos"), (ksin, "ksin")):
                        sp.dma_start(dst[:, :], A[src]).then_inc(loaded, 16)
                    sp.dma_start(X[:, :, :], A["x"].rearrange("(t p) d -> p t d", p=P)).then_inc(x_loaded, 16)
                    sp.wait_ge(x_loaded, 16)

                @block.scalar
                def _(act):
                    act.wait_ge(loaded, 96)
                    act.activation(GATE[:, :], graw[:, :], ACT.Tanh).then_inc(gates_done, 1)

                @block.gpsimd
                def _(pool):
                    pool.memset(EPS[:, :], 1e-5)
                    pool.memset(ONES[:, :], 1.0)
                    pool.memset(maskf[:, :], 0.0).then_inc(mask_steps, 1)
                    pool.wait_ge(mask_steps, 1)
                    pool.affine_select(out=maskf[:, :], in_=maskf[:, :], compare_op=ALU.is_ge, fill=MASKED, base=0, pattern=[[-1, L]], channel_multiplier=1).then_inc(mask_steps, 1)

                @block.vector
                def _(dve):
                    for part in KVB:
                        rope.inc(dve.memset(part[:, :, :].bitcast(F32), 0.0))
                    dve.wait_ge(loaded, 96)
                    rope.inc(dve.tensor_copy(IDENTB[:, :], IDENT[:, :]))
                    rope.inc(dve.tensor_tensor(prod[:, 0, :], kvt[:, :], kcos[:, :], ALU.mult))
                    rope.inc(dve.tensor_tensor(prod[:, 1, :], kvs[:, :], ksin[:, :], ALU.mult))
                    rope.wait(dve)
                    rope.inc(dve.tensor_tensor(kvt[:, :], prod[:, 0, :], prod[:, 1, :], ALU.add))
                    rope.wait(dve)
                    rope.inc(dve.tensor_copy(KV[0][:, :], kvt[:, :]))
                    rope.wait(dve)
                    rope.inc(dve.tensor_tensor(KV[1][:, :], kvt[:, :], KV[0][:, :].bitcast(F32), ALU.subtract))
                    rope.wait(dve)
                    for part, src in zip(KVB, KV):
                        for h in range(2):
                            rope.inc(dve.tensor_copy(part[64 * h:64 * h + 64, :, L * h:L * h + L],
                                                     src[64 * h:64 * h + 64, :].bitcast(F32).rearrange("p (b l) -> p b l", b=B)))
                    dve.wait_ge(mask_steps, 2)
                    dve.tensor_copy(MASK[:, :], maskf[:, :])
                    dve.wait_ge(x_loaded, 16)
                    for t in range(T):
                        measure(dve, x_stats, t)

        def fetch_ahead(sp, ahead, fetched):
            for dst, src in ahead:
                sp.dma_start(dst, src).then_inc(fetched, 16)
            sp.wait_ge(fetched, 16 * len(ahead))

        def norm(ctx, tag, banks):
            std_ready = sem(ctx, f"{tag}_std_ready")
            stats = Count(sem(ctx, f"{tag}_norm_steps"))
            xn_ready = sem(ctx, f"{tag}_xn_ready")
            xt_turned = sem(ctx, f"{tag}_xt_turned")
            xt_hi = sem(ctx, f"{tag}_xt_hi")
            xt_ready = sem(ctx, f"{tag}_xt_ready")

            def half(j):
                return slice(j // 2 * HALF, j // 2 * HALF + HALF)

            def vector(dve):
                for h in range(2):
                    tiles = slice(T // 2 * h, T // 2 * (h + 1))
                    dve.wait_ge(std_ready, h + 1)
                    stats.inc(dve.reciprocal(RSTD[:, tiles], STD[:, tiles]))
                    stats.wait(dve)
                    for t in range(T // 2 * h, T // 2 * (h + 1)):
                        dve.tensor_scalar(XN[:, t, :], X[:, t, :], MOM[:, t, 0:1], RSTD[:, t:t + 1],
                                          ALU.subtract, ALU.mult).then_inc(xn_ready, 1)

            def vector_low(dve):
                for j in range(4):
                    dve.wait_ge(xt_hi, j + 1)
                    dve.tensor_tensor(xt[1][:, j % 2, half(j)], banks[j], xt[0][:, j % 2, half(j)].bitcast(F32),
                                      ALU.subtract).then_inc(xt_ready, 1)

            def deviation(act):
                for h in range(2):
                    tiles = slice(T // 2 * h, T // 2 * (h + 1))
                    act.activation(STD[:, tiles], MOM[:, tiles, 1], ACT.Sqrt, bias=EPS[:, 0:1]).then_inc(std_ready, 1)

            def scalar(act):
                for j in range(4):
                    act.wait_ge(xt_turned, j + 1)
                    act.activation(xt[0][:, j % 2, half(j)], banks[j], ACT.Copy).then_inc(xt_hi, 1)

            def tensor(pe):
                for j in range(4):
                    pe.wait_ge(xn_ready, T // 2 * (j // 2 + 1))
                    for q in range(T // 2):
                        t = j // 2 * (T // 2) + q
                        last = pe.transpose(banks[j][:, q * P:(q + 1) * P], XN[:, t, (j % 2) * P:(j % 2 + 1) * P], IDENT[:, :])
                    last.then_inc(xt_turned, 1)

            return dict(vector=vector, vector_low=vector_low, deviation=deviation, scalar=scalar, tensor=tensor, ready=xt_ready, xn_ready=xn_ready)

        def latent_rope(Y, AT):
            o_qr, o_kr, o_ck, o_wo, width = pair_columns(0)
            with ExitStack() as ctx:
                W = sbuf(ctx, "W", [P, width])
                WS = split(ctx, "WS", [P, width])
                KR = split(ctx, "KR", [R, 2, B * L])
                C = split(ctx, "C", [P, 2, KD, CQ])
                U = split(ctx, "U", [ROT, 2, 2, B, 2 * L])
                COS = sbuf(ctx, "COS", [ROT, 2, S])
                SIN = sbuf(ctx, "SIN", [ROT, 2, S])
                RP = sbuf(ctx, "RP", [ROT, 2, 4, HALF])
                QR = (sbuf(ctx, "QR_hi", [ROT, 2, 2, HALF], F32R), sbuf(ctx, "QR_lo", [ROT, 2, 2, HALF], F32R))
                SM = sbuf(ctx, "SM", [P, 4, H])
                DIFF = XN[:, 0:4, :].rearrange("p t d -> p (t d)")
                PROB = XN[:, 4:8, :].rearrange("p t d -> p (t d)")

                def wide(ap):
                    return ap.rearrange("p (n l) -> p n l", l=L)
                QB = psum(ctx, "QB", [P, 4, 512])
                ST = psum(ctx, "ST", [P, 2, HALF])
                TR = psum(ctx, "TR", [P, 2, 512])
                nrm = norm(ctx, "a0", [QB[:, j, :] for j in range(4)])
                tables = sem(ctx, "tables")
                SECTIONS = (slice(0, o_kr), slice(o_kr, o_qr), slice(o_qr, width))
                ROWS = (P, P, R)
                w_in = sem(ctx, "w_in")
                w_hi, w_lo = [sem(ctx, f"w_hi_{c}") for c in range(3)], [sem(ctx, f"w_lo_{c}") for c in range(3)]
                chain_ps = sem(ctx, "chain_in_psum")
                chain_hi = sem(ctx, "chain_hi")
                chain_lo = sem(ctx, "chain_lo")
                q_ps = sem(ctx, "q_in_psum")
                rope_mul = sem(ctx, "rope_products")
                rope_add = sem(ctx, "rope_sums")
                rope_hi = sem(ctx, "rope_hi")
                rope_lo = sem(ctx, "rope_lo")
                padded = sem(ctx, "keys_padded")
                scored = sem(ctx, "scored")
                scores_out, scores_turned = sem(ctx, "scores_out"), sem(ctx, "scores_turned")
                smax = sem(ctx, "row_max")
                shifted = sem(ctx, "shifted")
                expd = sem(ctx, "exponentials")
                ssum = sem(ctx, "row_sums")
                normed = sem(ctx, "probabilities")
                turned = sem(ctx, "turned")
                at_hi, at_lo = sem(ctx, "at_hi"), sem(ctx, "at_lo")
                N_CHAIN = 6

                def w(c, n, part, rows=P):
                    return WS[part][0:rows, c:c + n]

                def both(f):
                    return f(0), f(1)

                def chain_slot(k, p):
                    if k < 2:
                        return QB[:, k, 0:KD * CQ], [part[:, k, :, :].rearrange("p k n -> p (k n)") for part in C]
                    if k == 2:
                        return TR[0:R, 0, :], [part[:, :, :].rearrange("p h n -> p (h n)") for part in KR]
                    if k == 3:
                        return TR[:, 1, 0:D], [part[:, bass.ds(p * D, D)] for part in Y]
                    h = k - 4
                    return (TR[0:ROT, h, :].rearrange("p (q b l) -> p q b l", q=2, b=B),
                            [part[:, h, :, :, L * h:L * h + L] for part in U])

                QUERY_W, KEY_W, KEYS = (0, 1), (2, 3), (4, 5)

                def steps(eng, step):
                    for p in range(2):
                        step(p, age=p)
                    with eng.Fori(2, NP - 1) as p:
                        step(p)
                    step(NP - 1, last=True)

                with nc.Block() as block:
                    @block.sync
                    def _(sp):
                        sp.dma_start(W[:, :], A["L0_pairs"][0]).then_inc(w_in, 16)
                        sp.dma_start(COS[:, :, :], A["qcos"]).then_inc(tables, 16)
                        sp.dma_start(SIN[:, :, :], A["qsin"]).then_inc(tables, 16)
                        with sp.Fori(1, NP) as p:
                            sp.wait_ge(w_lo[2], p)
                            sp.dma_start(W[:, :], A["L0_pairs"][bass.ds(p, 1), :, :].rearrange("a p n -> (a p) n")).then_inc(w_in, 16)

                    @block.gpsimd
                    def _(pool):
                        def low(p, c):
                            a = slice(0, ROWS[c])
                            pool.wait_ge(w_hi[c], p + 1)
                            pool.tensor_tensor(WS[1][a, SECTIONS[c]], W[a, SECTIONS[c]], WS[0][a, SECTIONS[c]].bitcast(F32), ALU.subtract).then_inc(w_lo[c], 1)

                        def add(p, u):
                            pool.wait_ge(rope_mul, 8 * p + 2 * (u + 1))
                            pool.tensor_tensor(RP[:, u % 2, 0, :], RP[:, u % 2, 0, :], RP[:, u % 2, 3, :], ALU.add).then_inc(rope_add, 1)
                            pool.tensor_tensor(RP[:, u % 2, 1, :], RP[:, u % 2, 1, :], RP[:, u % 2, 2, :], ALU.add).then_inc(rope_add, 1)

                        def normalise(p):
                            pool.wait_ge(ssum, 2 * p + 2)
                            pool.tensor_tensor(wide(PROB), wide(DIFF), SM[:, 2, :].unsqueeze(2).broadcast_to((P, H, L)), ALU.mult).then_inc(normed, 1)

                        for part in U:
                            pool.memset(part[:, :, :, :, :].rearrange("p h q b l -> p (h q b l)").bitcast(F32), 0.0).then_inc(padded, 1)
                        for c in range(3):
                            low(0, c)

                        def step(p, age=2, last=False):
                            if age > 1:
                                normalise(p - 2)
                            add(p, 0)
                            if not last:
                                low(p + 1, 0)
                            add(p, 1)
                            if not last:
                                low(p + 1, 1)
                                low(p + 1, 2)
                            add(p, 2)
                            add(p, 3)
                        steps(pool, step)
                        normalise(NP - 2)
                        normalise(NP - 1)

                    @block.scalar
                    def _(act):
                        def high(p, c, first=False):
                            a = slice(0, ROWS[c])
                            if c == 0:
                                act.wait_ge(w_in, 16 * (p + 1))
                            if not first:
                                act.wait_ge(chain_ps, N_CHAIN * (p - 1) + 2 * (c + 1))
                            act.activation(WS[0][a, SECTIONS[c]], W[a, SECTIONS[c]], ACT.Copy).then_inc(w_hi[c], 1)

                        def chain(p, ks):
                            for k in ks:
                                src, dst = chain_slot(k, p)
                                act.wait_ge(chain_ps, N_CHAIN * p + k + 1)
                                act.activation(dst[0], src, ACT.Copy).then_inc(chain_hi, 1)

                        def rope_high(p, u, fresh=False):
                            act.wait_ge(rope_add, 8 * p + 2 * (u + 1))
                            if not fresh:
                                act.wait_ge(scored, 4 * p + u - 1)
                            act.activation(QR[0][:, u % 2, :, :], RP[:, u % 2, 0:2, :], ACT.Copy).then_inc(rope_hi, 1)

                        def exps(p):
                            act.wait_ge(shifted, p + 1)
                            act.activation(DIFF, DIFF, ACT.Exp).then_inc(expd, 1)

                        def scores(p, half, first=False):
                            act.wait_ge(scored, 4 * p + 3 + half)
                            if not first:
                                act.wait_ge(turned, p)
                            act.activation(PROB[:, half * HALF:(half + 1) * HALF], ST[:, half, :], ACT.Copy).then_inc(scores_out, 1)

                        def at_high(p):
                            act.wait_ge(turned, p + 1)
                            act.activation(AT[0][:, bass.ds(p * B * S, B * S)], TR[:, :, :].rearrange("p a n -> p (a n)"), ACT.Copy).then_inc(at_hi, 1)

                        nrm["deviation"](act)
                        for c in range(3):
                            high(0, c, True)
                        nrm["scalar"](act)
                        chain(0, QUERY_W)
                        act.wait_ge(padded, 2)

                        def step(p, age=2, last=False):
                            if age > 1:
                                exps(p - 2)
                            if age > 0:
                                rope_high(p - 1, 3)
                            if not last:
                                high(p + 1, 0)
                            if age > 1:
                                at_high(p - 2)
                            if age > 0:
                                scores(p - 1, 0, age < 2)
                            rope_high(p, 0, age < 1)
                            chain(p, KEY_W)
                            if not last:
                                high(p + 1, 1)
                            rope_high(p, 1, age < 1)
                            if age > 0:
                                scores(p - 1, 1, age < 2)
                            chain(p, KEYS)
                            if not last:
                                high(p + 1, 2)
                                chain(p + 1, QUERY_W)
                            rope_high(p, 2)
                        steps(act, step)
                        exps(NP - 2)
                        rope_high(NP - 1, 3)
                        at_high(NP - 2)
                        scores(NP - 1, 0)
                        scores(NP - 1, 1)
                        exps(NP - 1)
                        at_high(NP - 1)

                    @block.vector
                    def _(dve):
                        nrm["vector"](dve)
                        nrm["vector_low"](dve)

                        def chain(p, ks):
                            for k in ks:
                                src, dst = chain_slot(k, p)
                                dve.wait_ge(chain_hi, N_CHAIN * p + k + 1)
                                dve.tensor_tensor(dst[1], src, dst[0].bitcast(F32), ALU.subtract).then_inc(chain_lo, 1)

                        def mul(p, u, fresh=False):
                            half = u % 2
                            src = QB[0:ROT, 2 * half:2 * half + 2, :].rearrange("p q (b s) -> p q b s", b=2)
                            cos = COS[:, :, :].unsqueeze(2).broadcast_to((ROT, 2, 2, S))
                            dve.wait_ge(q_ps, 4 * p + u + 1)
                            if not fresh:
                                dve.wait_ge(rope_lo, 4 * p + u - 1)
                            dve.tensor_tensor(RP[:, half, 0:2, :].rearrange("p q (b s) -> p q b s", b=2), src, cos, ALU.mult).then_inc(rope_mul, 1)
                            sin = SIN[:, :, :].unsqueeze(2).broadcast_to((ROT, 2, 2, S))
                            dve.tensor_tensor(RP[:, half, 2:4, :].rearrange("p q (b s) -> p q b s", b=2), src, sin, ALU.mult).then_inc(rope_mul, 1)

                        def rope_low(p, u):
                            dve.wait_ge(rope_hi, 4 * p + u + 1)
                            dve.tensor_tensor(QR[1][:, u % 2, :, :], RP[:, u % 2, 0:2, :], QR[0][:, u % 2, :, :].bitcast(F32), ALU.subtract).then_inc(rope_lo, 1)

                        def shift(p, first=False):
                            dve.wait_ge(scores_turned, p + 1)
                            src = wide(TR[:, :, :].rearrange("p a n -> p (a n)"))
                            if not first:
                                dve.wait_ge(normed, p)
                            dve.tensor_reduce(SM[:, 0, :], src, AX, ALU.max).then_inc(smax, 1)
                            dve.wait_ge(smax, p + 1)
                            dve.tensor_tensor(wide(DIFF), src, SM[:, 0, :].unsqueeze(2).broadcast_to((P, H, L)), ALU.subtract).then_inc(shifted, 1)

                        def sums(p):
                            dve.wait_ge(expd, p + 1)
                            dve.tensor_reduce(SM[:, 1, :], wide(DIFF), AX, ALU.add).then_inc(ssum, 1)
                            dve.wait_ge(ssum, 2 * p + 1)
                            dve.reciprocal(SM[:, 2, :], SM[:, 1, :]).then_inc(ssum, 1)

                        def at_low(p):
                            dve.wait_ge(at_hi, p + 1)
                            dve.tensor_tensor(AT[1][:, bass.ds(p * B * S, B * S)], TR[:, :, :].rearrange("p a n -> p (a n)"),
                                              AT[0][:, bass.ds(p * B * S, B * S)].bitcast(F32), ALU.subtract).then_inc(at_lo, 1)

                        chain(0, QUERY_W)
                        dve.wait_ge(tables, 32)

                        def step(p, age=2, last=False):
                            if age > 1:
                                sums(p - 2)
                            mul(p, 0, age < 1)
                            if age > 0:
                                rope_low(p - 1, 3)
                            mul(p, 1, age < 1)
                            if age > 1:
                                at_low(p - 2)
                            rope_low(p, 0)
                            chain(p, KEY_W)
                            mul(p, 2)
                            chain(p, KEYS)
                            rope_low(p, 1)
                            mul(p, 3)
                            if not last:
                                chain(p + 1, QUERY_W)
                            if age > 0:
                                shift(p - 1, age < 2)
                            rope_low(p, 2)
                        steps(dve, step)
                        sums(NP - 2)
                        rope_low(NP - 1, 3)
                        at_low(NP - 2)
                        shift(NP - 1)
                        sums(NP - 1)
                        at_low(NP - 1)

                    @block.tensor
                    def _(pe):
                        nrm["tensor"](pe)
                        pe.wait_ge(nrm["ready"], 4)

                        def query_weights(p, first=False):
                            pe.wait_ge(w_lo[0], p + 1)
                            if not first:
                                pe.wait_ge(rope_mul, 8 * p - 2)
                            for h in range(2):
                                for k in range(KD):
                                    last = mm3(pe, QB[:, h, k * CQ:(k + 1) * CQ], both(lambda i: w(O_WQ + D * h + P * k, P, i)), both(lambda i: w(O_CQ + CQ * h, CQ, i)))
                                last.then_inc(chain_ps, 1)

                        def key_weights(p, turned_before):
                            pe.wait_ge(w_lo[1], p + 1)
                            if turned_before:
                                pe.wait_ge(at_lo, p - 1)
                            for h in range(2):
                                last = mm3(pe, TR[0:R, 0, h * 256:(h + 1) * 256], both(lambda i: w(o_kr + R * h, R, i)), both(lambda i: KV[i][:, :]))
                            last.then_inc(chain_ps, 1)
                            for h in range(2):
                                last = mm3(pe, TR[:, 1, 0:D], both(lambda i: w(o_ck + P * h, P, i)), both(lambda i: w(o_wo + D * h, D, i)), first=h == 0, last=h == 1)
                            last.then_inc(chain_ps, 1)

                        def keys(p):
                            pe.wait_ge(chain_lo, N_CHAIN * p + 4)
                            pe.wait_ge(w_lo[2], p + 1)
                            for h in range(2):
                                for q in range(2):
                                    last = mm3(pe, TR[0:ROT, h, q * 256:(q + 1) * 256], both(lambda i: w(o_qr + CQ * h + ROT * q, ROT, i, R)), both(lambda i: KR[i][:, h, :]))
                                last.then_inc(chain_ps, 1)

                        def query(p, u, first=False):
                            h, half = u // 2, u % 2
                            if u == 0:
                                pe.wait_ge(chain_lo, N_CHAIN * p + 2)
                            elif not (first and u == 1):
                                pe.wait_ge(rope_mul, 8 * p + 2 * (u - 1))
                            for q in range(2):
                                for k in range(KD):
                                    last = mm3(pe, QB[0:ROT, 2 * half + q, :], both(lambda i: C[i][:, h, k, ROT * q:ROT * (q + 1)]),
                                               both(lambda i: xt[i][:, k, half * HALF:(half + 1) * HALF]), first=k == 0, last=k == KD - 1)
                            last.then_inc(q_ps, 1)

                        def score(p, u, first=False):
                            h, half = u // 2, u % 2
                            pe.wait_ge(rope_lo, 4 * p + u + 1)
                            if u == 0:
                                pe.wait_ge(chain_lo, N_CHAIN * p + N_CHAIN)
                            if h == 0 and not first:
                                pe.wait_ge(scores_out, 2 * p - 1 + half)
                            for b in range(2):
                                for q in range(2):
                                    for n, (i, j) in enumerate(((0, 0), (0, 1), (1, 0))):
                                        last = pe.matmul(ST[:, half, b * S:(b + 1) * S], U[i][:, h, q, 2 * half + b, :], QR[j][:, half, q, b * S:(b + 1) * S],
                                                         start=u < 2 and b == 0 and q == 0 and n == 0, stop=h == 1 and b == 1 and q == 1 and n == 2, skip_group_check=True)
                            last.then_inc(scored, 1)

                        def turn_scores(p):
                            pe.wait_ge(scores_out, 2 * p + 2)
                            for t in range(T):
                                last = pe.transpose(TR[:, t // 4, (t % 4) * P:(t % 4 + 1) * P], PROB[:, t * P:(t + 1) * P], IDENT[:, :])
                            last.then_inc(scores_turned, 1)

                        def turn(p):
                            pe.wait_ge(normed, p + 1)
                            for t in range(T):
                                last = pe.transpose(TR[:, t // 4, (t % 4) * P:(t % 4 + 1) * P], PROB[:, t * P:(t + 1) * P], IDENT[:, :])
                            last.then_inc(turned, 1)

                        query_weights(0, True)

                        def step(p, age=2, last=False):
                            query(p, 0)
                            if age > 0:
                                score(p - 1, 2)
                            query(p, 1, age < 1)
                            if age > 1:
                                turn(p - 2)
                            query(p, 2)
                            key_weights(p, age > 1)
                            if age > 0:
                                score(p - 1, 3)
                            keys(p)
                            query(p, 3)
                            if not last:
                                query_weights(p + 1)
                            if age > 0:
                                pe.wait_ge(chain_lo, N_CHAIN * p + N_CHAIN)
                                turn_scores(p - 1)
                            score(p, 0, age < 1)
                            score(p, 1, age < 1)
                        steps(pe, step)
                        score(NP - 1, 2)
                        turn(NP - 2)
                        score(NP - 1, 3)
                        pe.wait_ge(at_lo, NP - 1)
                        turn_scores(NP - 1)
                        turn(NP - 1)

        def latent_out(Y, AT, gate):
            with ExitStack() as ctx:
                Z = split(ctx, "Z", [P, 2, NP * D])
                ZP = psum(ctx, "ZP", [P, 4, 512])
                OP = psum(ctx, "OP", [P, 2, 512])
                z_ps, z_hi, z_lo = sem(ctx, "z_in_psum"), sem(ctx, "z_hi"), sem(ctx, "z_lo")
                out_ps, added, stats = sem(ctx, "out_in_psum"), sem(ctx, "added"), sem(ctx, "measured")
                ROUNDS = NP // 2
                with nc.Block() as block:
                    @block.tensor
                    def _(pe):
                        def values(b):
                            for r in range(ROUNDS):
                                n = b * ROUNDS + r
                                if n >= 4:
                                    pe.wait_ge(z_lo, n - 3)
                                for q in range(2):
                                    pair = 2 * r + q
                                    last = mm3(pe, ZP[:, n % 4, q * D:(q + 1) * D], (KVB[0][:, b, :], KVB[1][:, b, :]),
                                               (Y[0][:, pair * D:(pair + 1) * D], Y[1][:, pair * D:(pair + 1) * D]))
                                last.then_inc(z_ps, 1)
                        values(0)
                        for b in range(B):
                            if b + 1 < B:
                                values(b + 1)
                            pe.wait_ge(z_lo, ROUNDS * (b + 1))
                            for t in range(TB * b, TB * (b + 1)):
                                if t >= 2:
                                    pe.wait_ge(added, t - 1)
                                for pair in range(NP):
                                    at = slice(pair * B * S + t * P, pair * B * S + (t + 1) * P)
                                    last = mm3(pe, OP[:, t % 2, 0:D], (AT[0][:, at], AT[1][:, at]),
                                               (Z[0][:, b % 2, pair * D:(pair + 1) * D], Z[1][:, b % 2, pair * D:(pair + 1) * D]), first=pair == 0, last=pair == NP - 1)
                                last.then_inc(out_ps, 1)

                    @block.scalar
                    def _(act):
                        for n in range(B * ROUNDS):
                            b, r = divmod(n, ROUNDS)
                            act.wait_ge(z_ps, n + 1)
                            if b >= 2:
                                act.wait_ge(out_ps, TB * (b - 1))
                            act.activation(Z[0][:, b % 2, 2 * r * D:2 * (r + 1) * D], ZP[:, n % 4, :], ACT.Copy).then_inc(z_hi, 1)

                    @block.vector
                    def _(dve):
                        def low(b):
                            for r in range(ROUNDS):
                                n = b * ROUNDS + r
                                at = slice(2 * r * D, 2 * (r + 1) * D)
                                dve.wait_ge(z_hi, n + 1)
                                dve.tensor_tensor(Z[1][:, b % 2, at], ZP[:, n % 4, :], Z[0][:, b % 2, at].bitcast(F32), ALU.subtract).then_inc(z_lo, 1)
                        low(0)
                        for b in range(B):
                            if b + 1 < B:
                                low(b + 1)
                            for t in range(TB * b, TB * (b + 1)):
                                dve.wait_ge(out_ps, t + 1)
                                dve.scalar_tensor_tensor(out=X[:, t, :], in0=OP[:, t % 2, 0:D], scalar=GATE[:, gate:gate + 1], in1=X[:, t, :],
                                                         op0=ALU.mult, op1=ALU.add).then_inc(added, 1)
                                dve.wait_ge(added, t + 1)
                                measure(dve, stats, t)

        def experts(tag, gate, NE, NC, E, TOP, biased):
            OUTS = [[(0, 0), (1, 1)], [(1, 2), (2, 3)]] if biased else [[(m, m) for m in range(NC)]]
            NO = len(OUTS)
            ND = 4
            EC = NE * NO
            with ExitStack() as ctx:
                WU = sbuf(ctx, "WU", [P, NC, 4 * P])
                WUS = split(ctx, "WUS", [P, NC, 4 * P])
                WD = sbuf(ctx, "WD", [P, ND * D])
                WDS = split(ctx, "WDS", [P, ND * D])
                HG = sbuf(ctx, "HG", [P, 2, HALF])
                HF = sbuf(ctx, "HF", [P, 2, HALF])
                HS = split(ctx, "HS", [P, 2, NC, HALF])
                RW = sbuf(ctx, "RW", [P, KD, E])
                EP = 64
                RWS = split(ctx, "RWS", [P, KD, EP])
                LT = sbuf(ctx, "LT", [EP, B * S])
                CG = sbuf(ctx, "CG", [P, EC, T])
                PR = sbuf(ctx, "PR", [P, 4, T, E])
                SM = sbuf(ctx, "SM", [P, 6, T])
                CMP = sbuf(ctx, "CMP", [P, 2, T * E * E])
                BEFORE = sbuf(ctx, "BEFORE", [P, E * E])
                G = psum(ctx, "G", [P, 2, 512])
                U = psum(ctx, "U", [P, 2, 512])
                DN = psum(ctx, "DN", [P, 4, 512])
                if biased:
                    BIAS = sbuf(ctx, "BIAS", [P, NE * NC * 2])
                    UB = sbuf(ctx, "UB", [P, 2 * NC])
                    unit_bias = sem(ctx, f"{tag}_unit_bias")
                    GB = sbuf(ctx, "GB", [P, E])
                    B2 = sbuf(ctx, "B2", [E + 1, D])
                    B2S = split(ctx, "B2S", [E + 1, D])
                    CTS = split(ctx, "CTS", [E + 1, B * S])
                nrm = norm(ctx, tag, [DN[:, j, :] for j in range(4)])
                small_in = sem(ctx, f"{tag}_small_in")
                small_split = Count(sem(ctx, f"{tag}_small_split"))
                wu_in, wu_hi, wu_lo = (sem(ctx, f"{tag}_wu_{s}") for s in ("in", "hi", "lo"))
                wd_in, wd_hi, wd_lo = (sem(ctx, f"{tag}_wd_{s}") for s in ("in", "hi", "lo"))
                up_done, silu_done, h_full, h_hi, h_lo = (sem(ctx, f"{tag}_{s}") for s in ("up_done", "silu_done", "h_full", "h_hi", "h_lo"))
                down_done, added, first_added = (sem(ctx, f"{tag}_{s}") for s in ("down_done", "added", "first_added"))
                logits_ready = sem(ctx, f"{tag}_logits_ready")
                stats = sem(ctx, f"{tag}_measured")
                r_shift, r_exp = sem(ctx, f"{tag}_router_shifted"), sem(ctx, f"{tag}_router_exp")
                route = Count(sem(ctx, f"{tag}_router_steps"))
                combine_ready = sem(ctx, f"{tag}_combine_ready")
                ct_turned, ct_hi, ct_lo = (sem(ctx, f"{tag}_ct_{s}") for s in ("turned", "hi", "lo"))
                bias_ps, bias_added = sem(ctx, f"{tag}_bias_in_psum"), sem(ctx, f"{tag}_bias_added")
                lt_ps, lt_out, padded = (sem(ctx, f"{tag}_{s}") for s in ("logits_in_psum", "logits_out", "router_padded"))
                LOG = DN[:, 0, :].rearrange("p (t e) -> p t e", t=T)[:, :, 0:E]
                CT = DN[:, 1:3, :].rearrange("p a n -> p (a n)")
                SMALL = 5 if biased else 2
                UPS = 2 * NC

                def dram(name, e):
                    return A[name][bass.ds(e, 1), :, :].rearrange("a p n -> (a p) n")

                with nc.Block() as block:
                    @block.sync
                    def _(sp):
                        sp.dma_start(RW[:, :, :], A[f"{tag}_router"]).then_inc(small_in, 16)
                        sp.dma_start(BEFORE[:, :], A[f"before{E}"]).then_inc(small_in, 16)
                        if biased:
                            sp.dma_start(BIAS[:, :], A[f"{tag}_bias"]).then_inc(small_in, 16)
                            sp.dma_start(GB[:, :], A[f"{tag}_router_bias"]).then_inc(small_in, 16)
                            sp.dma_start(B2[:, :], A[f"{tag}_b2"]).then_inc(small_in, 16)

                        wu = WU[:, :, :].rearrange("p m n -> p (m n)")
                        sp.dma_start(wu, A[f"{tag}_up"][0]).then_inc(wu_in, 16)
                        sp.dma_start(WD[:, :], A[f"{tag}_down"][0]).then_inc(wd_in, 16)
                        with sp.Fori(1, NE) as e:
                            sp.wait_ge(wu_lo, NC * e)
                            sp.dma_start(wu, dram(f"{tag}_up", e)).then_inc(wu_in, 16)
                            sp.wait_ge(wd_lo, e)
                            sp.dma_start(WD[:, :], dram(f"{tag}_down", e)).then_inc(wd_in, 16)

                    @block.gpsimd
                    def _(pool):
                        def up_low(e, m):
                            pool.wait_ge(wu_hi, NC * e + m + 1)
                            pool.tensor_tensor(WUS[1][:, m, :], WU[:, m, :], WUS[0][:, m, :].bitcast(F32), ALU.subtract).then_inc(wu_lo, 1)

                        def down_low(e):
                            pool.wait_ge(wd_hi, e + 1)
                            pool.tensor_tensor(WDS[1][:, :], WD[:, :], WDS[0][:, :].bitcast(F32), ALU.subtract).then_inc(wd_lo, 1)

                        for part in RWS:
                            pool.memset(part[:, :, :].rearrange("p k e -> p (k e)").bitcast(F32), 0.0).then_inc(padded, 1)
                        for m in range(NC):
                            up_low(0, m)
                        with pool.Fori(0, NE - 1) as e:
                            down_low(e)
                            for m in range(NC):
                                up_low(e + 1, m)
                        down_low(NE - 1)

                    @block.scalar
                    def _(act):
                        def up_high(e, m):
                            act.wait_ge(wu_in, 16 * e + 16)
                            act.activation(WUS[0][:, m, :], WU[:, m, :], ACT.Copy).then_inc(wu_hi, 1)

                        def down_high(e):
                            act.wait_ge(wd_in, 16 * e + 16)
                            act.activation(WDS[0][:, :], WD[:, :], ACT.Copy).then_inc(wd_hi, 1)

                        def silu(e, k, first):
                            half, m = divmod(k, NC)
                            act.wait_ge(up_done, UPS * e + k + 1)
                            if not (first and k < 2):
                                act.wait_ge(h_full, UPS * e + k - 1)
                            if biased and k == 0:
                                act.wait_ge(unit_bias, e + 1)
                            bias = UB[:, 2 * m:2 * m + 1] if biased else 0.0
                            act.activation(HG[:, k % 2, :], G[:, k % 2, :], ACT.Silu, bias=bias).then_inc(silu_done, 1)

                        def high(e, k, first):
                            half, m = divmod(k, NC)
                            act.wait_ge(h_full, UPS * e + k + 1)
                            if not first:
                                act.wait_ge(down_done, 8 * e - 4 + 4 * half)
                            act.activation(HS[0][:, half, m, :], HF[:, k % 2, :], ACT.Copy).then_inc(h_hi, 1)

                        def step(e, first=False, second=False, more=True):
                            for k in range(UPS):
                                silu(e, k, first)
                                if k > 0:
                                    high(e, k - 1, first)
                                elif not first:
                                    high(e - 1, UPS - 1, second)
                                if biased and second and k == 1:
                                    act.wait_ge(ct_turned, 1)
                                    act.activation(CTS[0][:, :], CT[0:E + 1, :], ACT.Copy).then_inc(ct_hi, 1)
                                if k == NC:
                                    down_high(e)
                                if k >= NC and more:
                                    up_high(e + 1, k - NC)

                        nrm["deviation"](act)
                        up_high(0, 0)
                        nrm["scalar"](act)
                        for m in range(1, NC):
                            up_high(0, m)
                        for half in range(2):
                            act.wait_ge(lt_ps, half + 1)
                            act.activation(LT[:, half * HALF:(half + 1) * HALF], DN[0:EP, 1 + half, :], ACT.Copy).then_inc(lt_out, 1)
                        act.wait_ge(small_in, 16 * SMALL)
                        act.wait_ge(r_shift, 1)
                        act.activation(PR[:, 1, :, :], PR[:, 0, :, :], ACT.Exp).then_inc(r_exp, 1)
                        step(0, first=True)
                        step(1, second=True)
                        with act.Fori(2, NE - 1) as e:
                            step(e)
                        step(NE - 1, more=False)
                        high(NE - 1, UPS - 1, False)

                    @block.vector
                    def _(dve):
                        nrm["vector"](dve)
                        dve.wait_ge(small_in, 16 * SMALL)
                        dve.wait_ge(padded, 2)
                        small_split.inc(dve.tensor_copy(RWS[0][:, :, 0:E], RW[:, :, :]))
                        small_split.wait(dve)
                        small_split.inc(dve.tensor_tensor(RWS[1][:, :, 0:E], RW[:, :, :], RWS[0][:, :, 0:E].bitcast(F32), ALU.subtract))
                        if biased:
                            small_split.inc(dve.tensor_copy(B2S[0][:, :], B2[:, :]))
                            small_split.wait(dve)
                            small_split.inc(dve.tensor_tensor(B2S[1][:, :], B2[:, :], B2S[0][:, :].bitcast(F32), ALU.subtract))
                        nrm["vector_low"](dve)

                        def row(i):
                            return SM[:, i, :].unsqueeze(2).broadcast_to((P, T, E))
                        dve.wait_ge(logits_ready, 1)
                        route.inc(dve.tensor_reduce(SM[:, 0, :], LOG, AX, ALU.max))
                        route.wait(dve)
                        dve.tensor_tensor(PR[:, 0, :, :], LOG, row(0), ALU.subtract).then_inc(r_shift, 1)
                        rank_by = PR[:, 0 if biased else 2, :, :]
                        gt = CMP[:, 0, :].rearrange("p (t i j) -> p t i j", t=T, i=E)
                        eq = CMP[:, 1, :].rearrange("p (t i j) -> p t i j", t=T, i=E)

                        def router_softmax():
                            dve.wait_ge(r_exp, 1)
                            route.inc(dve.tensor_reduce(SM[:, 1, :], PR[:, 1, :, :], AX, ALU.add))
                            route.wait(dve)
                            route.inc(dve.reciprocal(SM[:, 2, :], SM[:, 1, :]))
                            route.wait(dve)
                            route.inc(dve.tensor_tensor(PR[:, 2, :, :], PR[:, 1, :, :], row(2), ALU.mult))
                            route.wait(dve)
                            if biased:
                                route.inc(dve.tensor_tensor(PR[:, 0, :, :], PR[:, 2, :, :], GB[:, :].unsqueeze(1).broadcast_to((P, T, E)), ALU.add))
                                route.wait(dve)

                        other = rank_by.unsqueeze(2).broadcast_to((P, T, E, E))
                        mine = rank_by.unsqueeze(3).broadcast_to((P, T, E, E))

                        def router_greater():
                            route.inc(dve.tensor_tensor(gt, other, mine, ALU.is_gt))

                        def router_equal():
                            route.inc(dve.tensor_tensor(eq, other, mine, ALU.is_equal))
                            route.wait(dve)

                        def router_combine():
                            eq2 = CMP[:, 1, :].rearrange("p (t n) -> p t n", t=T)
                            route.inc(dve.tensor_tensor(eq2, eq2, BEFORE[:, :].unsqueeze(1).broadcast_to((P, T, E * E)), ALU.mult))
                            route.wait(dve)
                            route.inc(dve.tensor_tensor(CMP[:, 0, :], CMP[:, 0, :], CMP[:, 1, :], ALU.add))
                            route.wait(dve)
                            route.inc(dve.tensor_reduce(PR[:, 1, :, :].rearrange("p t e -> p (t e)"), CMP[:, 0, :].rearrange("p (n j) -> p n j", j=E), AX, ALU.add))
                            route.wait(dve)
                            route.inc(dve.scalar_tensor_tensor(out=PR[:, 3, :, :], in0=PR[:, 1, :, :], scalar=float(TOP), in1=PR[:, 2, :, :], op0=ALU.is_lt, op1=ALU.mult))
                            route.wait(dve)
                            if not biased:
                                route.inc(dve.tensor_reduce(SM[:, 3, :], PR[:, 3, :, :], AX, ALU.add))
                                route.wait(dve)
                                route.inc(dve.reciprocal(SM[:, 4, :], SM[:, 3, :]))
                                route.wait(dve)
                                route.inc(dve.tensor_tensor(PR[:, 3, :, :], PR[:, 3, :, :], row(4), ALU.mult))
                                route.wait(dve)
                            dve.tensor_scalar(CG[:, 0:E, :].rearrange("p e t -> p t e"), PR[:, 3, :, :], GATE[:, gate:gate + 1], None, ALU.mult).then_inc(combine_ready, 1)
                            dve.tensor_scalar(CG[:, E:EC, :].rearrange("p e t -> p (e t)"), ONES[:, 0:(EC - E) * T], GATE[:, gate:gate + 1], None, ALU.mult).then_inc(combine_ready, 1)
                            dve.wait_ge(combine_ready, 2)

                        def full(e, k, first):
                            half, m = divmod(k, NC)
                            dve.wait_ge(silu_done, UPS * e + k + 1)
                            if not (first and k < 2):
                                dve.wait_ge(h_lo, UPS * e + k - 1)
                            if biased:
                                dve.scalar_tensor_tensor(out=HF[:, k % 2, :], in0=U[:, k % 2, :], scalar=BIAS[:, bass.ds(e * (2 * NC) + 2 * m + 1, 1)],
                                                         in1=HG[:, k % 2, :], op0=ALU.add, op1=ALU.mult).then_inc(h_full, 1)
                            else:
                                dve.tensor_tensor(HF[:, k % 2, :], U[:, k % 2, :], HG[:, k % 2, :], ALU.mult).then_inc(h_full, 1)

                        def low(e, k):
                            half, m = divmod(k, NC)
                            dve.wait_ge(h_hi, UPS * e + k + 1)
                            dve.tensor_tensor(HS[1][:, half, m, :], HF[:, k % 2, :], HS[0][:, half, m, :].bitcast(F32), ALU.subtract).then_inc(h_lo, 1)

                        def add(e, half, final=False):
                            for q in range(4):
                                t, n = 4 * half + q, 4 * half + q
                                dve.wait_ge(down_done, 8 * e + n + 1)
                                for o in range(NO):
                                    ins = dve.scalar_tensor_tensor(out=X[:, t, :], in0=DN[:, q, o * D:(o + 1) * D], scalar=CG[:, :, :].rearrange("p e t -> p (e t)")[:, bass.ds(e * (NO * T) + o * T + t, 1)],
                                                                   in1=X[:, t, :], op0=ALU.mult, op1=ALU.add)
                                    if o < NO - 1:
                                        ins.then_inc(first_added, 1)
                                        dve.wait_ge(first_added, 8 * e + n + 1)
                                    else:
                                        ins.then_inc(added, 1)
                                if final and biased:
                                    dve.wait_ge(added, 8 * e + n + 1)
                                    measure(dve, stats, t)

                        def unit_biases(e):
                            dve.tensor_scalar(UB[:, :], BIAS[:, bass.ds(e * (2 * NC), 2 * NC)], 1.0, None, ALU.mult).then_inc(unit_bias, 1)

                        def step(e, first=False, second=False, more=True):
                            for k in range(UPS):
                                full(e, k, first)
                                if k == UPS - 1 and biased and more:
                                    unit_biases(e + 1)
                                if k > 0:
                                    low(e, k - 1)
                                elif not first:
                                    low(e - 1, UPS - 1)
                                if biased and second and k == 1:
                                    dve.wait_ge(ct_hi, 1)
                                    dve.tensor_tensor(CTS[1][:, :], CT[0:E + 1, :], CTS[0][:, :].bitcast(F32), ALU.subtract).then_inc(ct_lo, 1)
                                if biased and second and k == NC - 1:
                                    for t in range(T):
                                        dve.wait_ge(bias_ps, t + 1)
                                        dve.tensor_tensor(X[:, t, :], DN[:, t % 4, 0:D], X[:, t, :], ALU.add).then_inc(bias_added, 1)
                                    dve.wait_ge(bias_added, T)
                                if k == NC - 1 and not first:
                                    add(e - 1, 1)
                                if first and k == 1:
                                    router_softmax()
                                if first and k == 2:
                                    router_greater()
                                if first and k == 4:
                                    router_equal()
                                if first and k == 5:
                                    router_combine()
                            add(e, 0, not more)
                        if biased:
                            unit_biases(0)
                        step(0, first=True)
                        step(1, second=True)
                        with dve.Fori(2, NE - 1) as e:
                            step(e)
                        step(NE - 1, more=False)
                        low(NE - 1, UPS - 1)
                        add(NE - 1, 1, True)

                    @block.tensor
                    def _(pe):
                        nrm["tensor"](pe)
                        pe.wait_ge(nrm["ready"], 4)
                        pe.wait_ge(small_split.sem, 4 if biased else 2)
                        for half in range(2):
                            at = slice(half * HALF, (half + 1) * HALF)
                            for k in range(KD):
                                last = mm3(pe, DN[0:EP, 1 + half, :], (RWS[0][:, k, :], RWS[1][:, k, :]), (xt[0][:, k, at], xt[1][:, k, at]), first=k == 0, last=k == KD - 1)
                            last.then_inc(lt_ps, 1)

                        def up(e, k, first):
                            half, m = divmod(k, NC)
                            if half == 0:
                                pe.wait_ge(wu_lo, NC * e + m + 1)
                            if not (first and k < 2):
                                pe.wait_ge(h_full, UPS * e + k - 1)
                            for mat, bank in ((0, G), (1, U)):
                                for c in range(KD):
                                    at = slice((2 * c + mat) * P, (2 * c + mat + 1) * P)
                                    last = mm3(pe, bank[:, k % 2, :], (WUS[0][:, m, at], WUS[1][:, m, at]),
                                               (xt[0][:, c, half * HALF:(half + 1) * HALF], xt[1][:, c, half * HALF:(half + 1) * HALF]), first=c == 0, last=c == KD - 1)
                            last.then_inc(up_done, 1)

                        def down(e, half, first):
                            pe.wait_ge(h_lo, UPS * e + NC * (half + 1))
                            if half == 0:
                                pe.wait_ge(wd_lo, e + 1)
                            for q in range(4):
                                if not (first and half == 0):
                                    pe.wait_ge(added, 8 * e + 4 * half + q - 3)
                                for o, rows in enumerate(OUTS):
                                    for j, (m, n) in enumerate(rows):
                                        last = mm3(pe, DN[:, q, o * D:(o + 1) * D], (HS[0][:, half, m, q * P:(q + 1) * P], HS[1][:, half, m, q * P:(q + 1) * P]),
                                                   (WDS[0][:, n * D:(n + 1) * D], WDS[1][:, n * D:(n + 1) * D]), first=j == 0, last=j == len(rows) - 1)
                                last.then_inc(down_done, 1)

                        def turn_logits():
                            pe.wait_ge(lt_out, 2)
                            for t in range(T):
                                last = pe.transpose(DN[:, 0, t * EP:(t + 1) * EP], LT[:, t * P:(t + 1) * P], IDENT[0:EP, 0:EP])
                            last.then_inc(logits_ready, 1)

                        def turn_weights():
                            pe.wait_ge(combine_ready, 2)
                            pe.wait_ge(added, 4)
                            for t in range(T):
                                last = pe.transpose(CT[0:E + 1, t * P:(t + 1) * P], CG[:, 0:E + 1, t], IDENT[:, :])
                            last.then_inc(ct_turned, 1)

                        def products_with_biases():
                            pe.wait_ge(ct_lo, 1)
                            for t in range(T):
                                if t >= 4:
                                    pe.wait_ge(bias_added, t - 3)
                                mm3(pe, DN[:, t % 4, 0:D], (CTS[0][:, t * P:(t + 1) * P], CTS[1][:, t * P:(t + 1) * P]), (B2S[0][:, :], B2S[1][:, :])).then_inc(bias_ps, 1)
                            pe.wait_ge(bias_added, T)

                        def step(e, first=False, second=False):
                            for k in range(NC):
                                up(e, k, first)
                                if first and k == 0:
                                    turn_logits()
                                if biased and second and k == 1:
                                    turn_weights()
                            if biased and second:
                                products_with_biases()
                            if not first:
                                down(e - 1, 1, False)
                            for k in range(NC, UPS):
                                up(e, k, first)
                            if first:
                                pe.wait_ge(r_shift, 1)
                            down(e, 0, first)
                        step(0, first=True)
                        step(1, second=True)
                        with pe.Fori(2, NE) as e:
                            step(e)
                        down(NE - 1, 1, False)

        def latent_chain(GS, Y, W):
            o_qr, o_kr, o_ck, o_wo, width = pair_columns(1)
            with ExitStack() as ctx:
                WS = split(ctx, "WS", [P, 2, width])
                KR = split(ctx, "KR", [P, 4, B * L])
                UU = split(ctx, "UU", [ROT, 4, 2, B * L])
                VV = KR
                PB = psum(ctx, "PB", [P, 4, 512])
                NB = psum(ctx, "NB", [P, 4, 512])
                nrm = norm(ctx, "a1", [NB[:, j, :] for j in range(4)])
                SECTIONS = (slice(o_kr, o_qr), slice(o_qr, width), slice(O_CQ, o_kr), slice(O_WQ, O_CQ))
                NS = len(SECTIONS)
                w_in = [sem(ctx, f"w_in_{c}") for c in range(NS)]
                w_hi, w_lo = sem(ctx, "w_hi"), sem(ctx, "w_lo")
                in_ps, part_hi, part_lo = sem(ctx, "in_psum"), sem(ctx, "part_hi"), sem(ctx, "part_lo")
                STEPS = 2 + 2 + 4 + 2 + 4
                ROUNDS = NP // 2

                def place(s, g):
                    if s < 2:
                        return R, 512, [part[0:R, 2 * s:2 * s + 2, :].rearrange("p h n -> p (h n)") for part in KR]
                    if s < 4:
                        return P, D, [part[:, bass.ds(g * (2 * D) + (s - 2) * D, D)] for part in Y]
                    if s < 8:
                        return ROT, 512, [part[:, s - 4, :, :].rearrange("p q n -> p (q n)") for part in UU]
                    if s < 10:
                        return P, 512, [part[:, 2 * (s - 8):2 * (s - 8) + 2, :].rearrange("p h n -> p (h n)") for part in VV]
                    return P, 512, None

                def g_parts(s, g, i):
                    return GS[i][:, :, :, bass.ds(g * (4 * L) + (s - 10) * L, L)]

                with nc.Block() as block:
                    @block.sync
                    def _(sp):
                        for g in range(ROUNDS):
                            for c, cols in enumerate(SECTIONS):
                                if g > 0:
                                    sp.wait_ge(w_lo, NS * (g - 1) + c + 1)
                                sp.dma_start(W[:, :, cols], A["L1_pairs"][2 * g:2 * g + 2, :, cols].rearrange("a p n -> p a n")).then_inc(w_in[c], 16)

                    @block.gpsimd
                    def _(pool):
                        with pool.Fori(0, ROUNDS) as g:
                            for c, cols in enumerate(SECTIONS):
                                pool.wait_ge(w_hi, NS * g + c + 1)
                                pool.tensor_tensor(WS[1][:, :, cols], W[:, :, cols], WS[0][:, :, cols].bitcast(F32), ALU.subtract).then_inc(w_lo, 1)

                    @block.scalar
                    def _(act):
                        def high(g, c):
                            act.wait_ge(w_in[c], 16 * g + 16)
                            act.activation(WS[0][:, :, SECTIONS[c]], W[:, :, SECTIONS[c]], ACT.Copy).then_inc(w_hi, 1)

                        AFTER = {5: 0, 9: 1, 11: 2, 13: 3}

                        def step(g, last=False):
                            for s in range(STEPS):
                                rows, n, dst = place(s, g)
                                act.wait_ge(in_ps, STEPS * g + s + 1)
                                if s < 10:
                                    act.activation(dst[0], PB[0:rows, s % 4, 0:n], ACT.Copy).then_inc(part_hi, 1)
                                else:
                                    act.activation(g_parts(s, g, 0), PB[:, s % 4, :].rearrange("p (k b l) -> p k b l", k=KD, b=B), ACT.Copy).then_inc(part_hi, 1)
                                if s in AFTER and not last:
                                    high(g + 1, AFTER[s])
                        nrm["deviation"](act)
                        for c in range(NS):
                            high(0, c)
                        nrm["scalar"](act)
                        with act.Fori(0, ROUNDS - 1) as g:
                            step(g)
                        step(ROUNDS - 1, last=True)

                    @block.vector
                    def _(dve):
                        nrm["vector"](dve)
                        nrm["vector_low"](dve)
                        with dve.Fori(0, ROUNDS) as g:
                            for s in range(STEPS):
                                rows, n, dst = place(s, g)
                                dve.wait_ge(part_hi, STEPS * g + s + 1)
                                if s < 10:
                                    dve.tensor_tensor(dst[1], PB[0:rows, s % 4, 0:n], dst[0].bitcast(F32), ALU.subtract).then_inc(part_lo, 1)
                                else:
                                    src = PB[:, s % 4, :].rearrange("p (k b l) -> p k b l", k=KD, b=B)
                                    dve.tensor_tensor(g_parts(s, g, 1), src, g_parts(s, g, 0).bitcast(F32), ALU.subtract).then_inc(part_lo, 1)

                    @block.tensor
                    def _(pe):
                        nrm["tensor"](pe)

                        def w(a, c, n, rows=P):
                            return WS[0][0:rows, a, c:c + n], WS[1][0:rows, a, c:c + n]

                        def step(g, first=False):
                            def free(s, need=None):
                                n = (s - 4 if s >= 4 else (s - 2 if s < 2 else s - 6)) if need is None else max(need, s - 4)
                                if not (first and n < 0):
                                    pe.wait_ge(part_lo, STEPS * g + n + 1)
                            pe.wait_ge(w_lo, NS * g + 1)
                            for s in range(2):
                                free(s)
                                for j in range(2):
                                    last = mm3(pe, PB[0:R, s % 4, j * 256:(j + 1) * 256], w(s, o_kr + R * j, R), (KV[0][:, :], KV[1][:, :]))
                                last.then_inc(in_ps, 1)
                            for s in range(2, 4):
                                free(s)
                                for j in range(2):
                                    last = mm3(pe, PB[:, s % 4, 0:D], w(s - 2, o_ck + P * j, P), w(s - 2, o_wo + D * j, D), first=j == 0, last=j == 1)
                                last.then_inc(in_ps, 1)
                            pe.wait_ge(w_lo, NS * g + 2)
                            for s in range(4, 8):
                                h = s - 4
                                free(s, need=h // 2)
                                for q in range(2):
                                    last = mm3(pe, PB[0:ROT, s % 4, q * 256:(q + 1) * 256], w(h // 2, o_qr + CQ * (h % 2) + ROT * q, ROT, R), (KR[0][0:R, h, :], KR[1][0:R, h, :]))
                                last.then_inc(in_ps, 1)
                            pe.wait_ge(w_lo, NS * g + 3)
                            for s in range(8, 10):
                                for j in range(2):
                                    h = 2 * (s - 8) + j
                                    free(s, need=4 + h)
                                    for q in range(2):
                                        last = mm3(pe, PB[:, s % 4, j * 256:(j + 1) * 256], w(h // 2, O_CQ + 2 * K * (h % 2) + K * q, K, ROT),
                                                   (UU[0][:, h, q, :], UU[1][:, h, q, :]), first=q == 0, last=q == 1)
                                last.then_inc(in_ps, 1)
                            pe.wait_ge(w_lo, NS * g + 4)
                            for s in range(10, 14):
                                h = s - 10
                                free(s, need=8 + h // 2)
                                for k in range(KD):
                                    last = mm3(pe, PB[:, s % 4, k * 256:(k + 1) * 256], w(h // 2, O_WQ + D * (h % 2) + P * k, P), (VV[0][:, h, :], VV[1][:, h, :]))
                                last.then_inc(in_ps, 1)
                        step(0, True)
                        with pe.Fori(1, ROUNDS) as g:
                            step(g)

        def plain_chain(tag, GS, VB, WO, CW, QO, MASK):
            with ExitStack() as ctx:
                CWS = split(ctx, "CWS", [DC, B * L + 2 * D])
                WQ = split(ctx, "WQ", [P, 2, D])
                KVF = sbuf(ctx, "KVF", [P, 4, B * L])
                KVH = sbuf(ctx, "KVH", [P, 4, B * L], F32R)
                KVL = sbuf(ctx, "KVL", [P, 4, B * L], F32R)
                KB = split(ctx, "KB", [P, 2, 512])
                PB = psum(ctx, "PB", [P, 4, 512])
                NB = psum(ctx, "NB", [P, 4, 512])
                nrm = norm(ctx, tag, [NB[:, j, :] for j in range(4)])
                w_hi, w_lo = sem(ctx, f"{tag}_w_hi"), sem(ctx, f"{tag}_w_lo")
                kv_ps, kv_hi, kv_lo = (sem(ctx, f"{tag}_kv_{s}") for s in ("in_psum", "hi", "lo"))
                kb_hi, kb_lo = sem(ctx, f"{tag}_kb_hi"), sem(ctx, f"{tag}_kb_lo")
                vb_hi, vb_lo = sem(ctx, f"{tag}_vb_hi"), sem(ctx, f"{tag}_vb_lo")
                g_ps, g_hi, g_lo = (sem(ctx, f"{tag}_g_{s}") for s in ("in_psum", "hi", "lo"))
                UNITS = [(b, j) for b in range(B) for j in range(2)]

                def spread(dst, src):
                    return (dst.rearrange("p (h l) -> p h l", h=8), src.bitcast(F32).unsqueeze(1).broadcast_to((P, 8, L)),
                            MASK[:, :].unsqueeze(2).broadcast_to((P, 8, L)), ALU.mult)

                with nc.Block() as block:
                    @block.tensor
                    def _(pe):
                        pe.wait_ge(w_lo, 1)
                        for j in range(2):
                            for q in range(2):
                                c = B * L + j * D + q * P
                                last = mm3(pe, PB[:, j, q * 256:(q + 1) * 256], (CWS[0][:, c:c + P], CWS[1][:, c:c + P]), (CWS[0][:, 0:B * L], CWS[1][:, 0:B * L]))
                            last.then_inc(kv_ps, 1)
                        nrm["tensor"](pe)
                        pe.wait_ge(w_lo, 3)
                        for u, (b, j) in enumerate(UNITS):
                            pe.wait_ge(kb_hi, u + 1)
                            pe.wait_ge(kb_lo, u + 1)
                            for k in range(KD):
                                n = 2 * u + k
                                if n >= 4:
                                    pe.wait_ge(g_lo, n - 3)
                                elif n < 2:
                                    pe.wait_ge(kv_lo, 2)
                                mm3(pe, PB[:, n % 4, :], (WQ[0][:, j, k * P:(k + 1) * P], WQ[1][:, j, k * P:(k + 1) * P]),
                                    (KB[0][:, u % 2, :], KB[1][:, u % 2, :])).then_inc(g_ps, 1)

                    @block.scalar
                    def _(act):
                        nrm["deviation"](act)
                        act.activation(CWS[0][:, :], CW[:, :], ACT.Copy).then_inc(w_hi, 1)
                        act.activation(WQ[0][:, :, :], QO[:, 0:2, :], ACT.Copy).then_inc(w_hi, 1)
                        act.activation(WO[0][:, :, :], QO[:, 2:4, :], ACT.Copy).then_inc(w_hi, 1)
                        for j in range(2):
                            act.wait_ge(kv_ps, j + 1)
                            act.activation(KVH[:, 2 * j:2 * j + 2, :].rearrange("p q n -> p (q n)"), PB[:, j, :], ACT.Copy).then_inc(kv_hi, 1)
                        nrm["scalar"](act)
                        for n in range(2 * len(UNITS)):
                            (b, j), k = UNITS[n // 2], n % 2
                            act.wait_ge(g_ps, n + 1)
                            act.activation(GS[0][:, k, b, j * 512:(j + 1) * 512], PB[:, n % 4, :], ACT.Copy).then_inc(g_hi, 1)

                    @block.gpsimd
                    def _(pool):
                        for n, (dst, src, full) in enumerate(((CWS[1][:, :], CWS[0][:, :], CW[:, :]), (WQ[1][:, :, :], WQ[0][:, :, :], QO[:, 0:2, :]),
                                                              (WO[1][:, :, :], WO[0][:, :, :], QO[:, 2:4, :]))):
                            pool.wait_ge(w_hi, n + 1)
                            pool.tensor_tensor(dst, full, src.bitcast(F32), ALU.subtract).then_inc(w_lo, 1)
                        pool.wait_ge(kv_lo, 2)
                        for u, (b, j) in enumerate(UNITS):
                            if u >= 2:
                                pool.wait_ge(g_ps, 2 * (u - 1))
                            pool.tensor_tensor(*spread(KB[1][:, u % 2, :], KVL[:, j, b * L:(b + 1) * L])).then_inc(kb_lo, 1)
                        for u, (b, j) in enumerate(UNITS):
                            pool.tensor_tensor(*spread(VB[1][:, j, b, :], KVL[:, 2 + j, b * L:(b + 1) * L])).then_inc(vb_lo, 1)

                    @block.vector
                    def _(dve):
                        nrm["vector"](dve)
                        for j in range(2):
                            dve.wait_ge(kv_hi, j + 1)
                            at = KVL[:, 2 * j:2 * j + 2, :].rearrange("p q n -> p (q n)")
                            dve.tensor_tensor(at, PB[:, j, :], KVH[:, 2 * j:2 * j + 2, :].bitcast(F32).rearrange("p q n -> p (q n)"), ALU.subtract).then_inc(kv_lo, 1)

                        def keys(u):
                            b, j = UNITS[u]
                            if u >= 2:
                                dve.wait_ge(g_ps, 2 * (u - 1))
                            dve.tensor_tensor(*spread(KB[0][:, u % 2, :], KVH[:, j, b * L:(b + 1) * L])).then_inc(kb_hi, 1)
                        keys(0)
                        keys(1)
                        nrm["vector_low"](dve)
                        for u, (b, j) in enumerate(UNITS):
                            for n in (2 * u, 2 * u + 1):
                                dve.wait_ge(g_hi, n + 1)
                                at = slice(j * 512, (j + 1) * 512)
                                dve.tensor_tensor(GS[1][:, n % 2, b, at], PB[:, n % 4, :], GS[0][:, n % 2, b, at].bitcast(F32), ALU.subtract).then_inc(g_lo, 1)
                            if u + 2 < len(UNITS):
                                keys(u + 2)
                            dve.tensor_tensor(*spread(VB[0][:, j, b, :], KVH[:, 2 + j, b * L:(b + 1) * L])).then_inc(vb_hi, 1)

        def attend(tag, GS, values, gate, scale, causal, ahead=()):
            with ExitStack() as ctx:
                Z = split(ctx, "Z", [P, 2, NP * D])
                DIFF = XN[:, :, :].rearrange("p t d -> p (t d)").rearrange("p (a n) -> p a n", a=2)
                PROB = sbuf(ctx, "PROB", [P, 2, H * L])
                AT = split(ctx, "ATT", [P, 2, NP * P])
                SM = sbuf(ctx, "SM", [P, 2, 3, H])
                SC = psum(ctx, "SC", [P, 2, 512])
                TR = psum(ctx, "TR", [P, 2, 512])
                ZP = psum(ctx, "ZP", [P, 2, 512])
                OP = psum(ctx, "OP", [P, 2, 512])
                scored = sem(ctx, f"{tag}_scored")
                smax, shifted, expd, ssum, normed = (sem(ctx, f"{tag}_{s}") for s in ("row_max", "shifted", "exponentials", "row_sums", "probabilities"))
                turned, at_hi, at_lo = (sem(ctx, f"{tag}_{s}") for s in ("turned", "at_hi", "at_lo"))
                z_ps, z_hi, z_lo = (sem(ctx, f"{tag}_{s}") for s in ("z_in_psum", "z_hi", "z_lo"))
                out_ps, added = sem(ctx, f"{tag}_out_in_psum"), sem(ctx, f"{tag}_added")
                stats = sem(ctx, f"{tag}_stats")
                fetched = sem(ctx, f"{tag}_fetched")
                ROUNDS = NP // 2

                def masks(t):
                    return causal and t % TB == 0

                def wide(ap):
                    return ap.rearrange("p (h l) -> p h l", l=L)

                def flat(bank):
                    return bank[:, :, :].rearrange("p a n -> p (a n)")

                with nc.Block() as block:
                    if ahead:
                        @block.sync
                        def _(sp):
                            fetch_ahead(sp, ahead, fetched)

                    @block.tensor
                    def _(pe):
                        def score(t):
                            b = t // TB
                            if t >= 1:
                                pe.wait_ge(shifted, t)
                            for j in range(2):
                                if masks(t):
                                    pe.matmul(SC[:, j, :].rearrange("p (h l) -> p h l", l=L), IDENTB[:, :], MASK[:, :].unsqueeze(1).broadcast_to((P, 8, L)), start=True, stop=False)
                                for k in range(KD):
                                    last = mm3(pe, SC[:, j, :], (xt[0][:, k, t * P:(t + 1) * P], xt[1][:, k, t * P:(t + 1) * P]),
                                               (GS[0][:, k, b, j * 512:(j + 1) * 512], GS[1][:, k, b, j * 512:(j + 1) * 512]), first=k == 0 and not masks(t), last=k == KD - 1)
                            last.then_inc(scored, 1)

                        def value(n):
                            b, r = divmod(n, ROUNDS)
                            if n >= 2:
                                pe.wait_ge(z_lo, n - 1)
                            for q in range(2):
                                a, w = values(b, 2 * r + q)
                                last = mm3(pe, ZP[:, n % 2, q * D:(q + 1) * D], a, w)
                            last.then_inc(z_ps, 1)

                        def turn(t):
                            pe.wait_ge(normed, t + 1)
                            if t >= 1:
                                pe.wait_ge(at_lo, t)
                            for pair in range(NP):
                                last = pe.transpose(TR[:, pair // 4, (pair % 4) * P:(pair % 4 + 1) * P], PROB[:, t % 2, pair * P:(pair + 1) * P], IDENT[:, :])
                            last.then_inc(turned, 1)

                        def mix(t):
                            pe.wait_ge(at_lo, t + 1)
                            pe.wait_ge(z_lo, ROUNDS * (t // TB + 1))
                            if t >= 2:
                                pe.wait_ge(added, t - 1)
                            for pair in range(NP):
                                last = mm3(pe, OP[:, t % 2, 0:D], (AT[0][:, t % 2, pair * P:(pair + 1) * P], AT[1][:, t % 2, pair * P:(pair + 1) * P]),
                                           (Z[0][:, t // TB % 2, pair * D:(pair + 1) * D], Z[1][:, t // TB % 2, pair * D:(pair + 1) * D]), first=pair == 0, last=pair == NP - 1)
                            last.then_inc(out_ps, 1)

                        for i in range(T + 2):
                            if i < T:
                                score(i)
                                value(2 * i)
                            if 1 <= i <= T:
                                turn(i - 1)
                            if i < T:
                                value(2 * i + 1)
                            if i >= 2:
                                mix(i - 2)

                    @block.scalar
                    def _(act):
                        def z_high(n):
                            b, r = divmod(n, ROUNDS)
                            act.wait_ge(z_ps, n + 1)
                            if b >= 2:
                                act.wait_ge(out_ps, TB * (b - 1))
                            act.activation(Z[0][:, b % 2, 2 * r * D:2 * (r + 1) * D], ZP[:, n % 2, :], ACT.Copy).then_inc(z_hi, 1)

                        for i in range(T + 1):
                            if i < T:
                                z_high(2 * i)
                                act.wait_ge(shifted, i + 1)
                                act.activation(DIFF[:, i % 2, :], DIFF[:, i % 2, :], ACT.Exp, scale=scale).then_inc(expd, 1)
                            if i >= 1:
                                act.wait_ge(turned, i)
                                if i >= 3:
                                    act.wait_ge(out_ps, i - 2)
                                act.activation(AT[0][:, (i - 1) % 2, :], flat(TR), ACT.Copy).then_inc(at_hi, 1)
                            if i < T:
                                z_high(2 * i + 1)

                    @block.gpsimd
                    def _(pool):
                        for t in range(T):
                            pool.wait_ge(ssum, 2 * t + 2)
                            if t >= 2:
                                pool.wait_ge(turned, t - 1)
                            pool.tensor_tensor(wide(PROB[:, t % 2, :]), wide(DIFF[:, t % 2, :]), SM[:, t % 2, 2, :].unsqueeze(2).broadcast_to((P, H, L)), ALU.mult).then_inc(normed, 1)

                    @block.vector
                    def _(dve):
                        def z_low(n):
                            b, r = divmod(n, ROUNDS)
                            at = slice(2 * r * D, 2 * (r + 1) * D)
                            dve.wait_ge(z_hi, n + 1)
                            dve.tensor_tensor(Z[1][:, b % 2, at], ZP[:, n % 2, :], Z[0][:, b % 2, at].bitcast(F32), ALU.subtract).then_inc(z_lo, 1)

                        def shift(t):
                            dve.wait_ge(scored, t + 1)
                            src = wide(flat(SC))
                            if t >= 2:
                                dve.wait_ge(normed, t - 1)
                            dve.tensor_reduce(SM[:, t % 2, 0, :], src, AX, ALU.max).then_inc(smax, 1)
                            dve.wait_ge(smax, t + 1)
                            dve.tensor_tensor(wide(DIFF[:, t % 2, :]), src, SM[:, t % 2, 0, :].unsqueeze(2).broadcast_to((P, H, L)), ALU.subtract).then_inc(shifted, 1)

                        def sums(t):
                            dve.wait_ge(expd, t + 1)
                            dve.tensor_reduce(SM[:, t % 2, 1, :], wide(DIFF[:, t % 2, :]), AX, ALU.add).then_inc(ssum, 1)
                            dve.wait_ge(ssum, 2 * t + 1)
                            dve.reciprocal(SM[:, t % 2, 2, :], SM[:, t % 2, 1, :]).then_inc(ssum, 1)

                        def add(t):
                            dve.wait_ge(out_ps, t + 1)
                            dve.scalar_tensor_tensor(out=X[:, t, :], in0=OP[:, t % 2, 0:D], scalar=GATE[:, gate:gate + 1], in1=X[:, t, :],
                                                     op0=ALU.mult, op1=ALU.add).then_inc(added, 1)
                            dve.wait_ge(added, t + 1)
                            measure(dve, stats, t)

                        for i in range(T + 2):
                            if i >= 3:
                                add(i - 3)
                            if i < T:
                                shift(i)
                                z_low(2 * i)
                                sums(i)
                            if 1 <= i <= T:
                                at = (i - 1) % 2
                                dve.wait_ge(at_hi, i)
                                dve.tensor_tensor(AT[1][:, at, :], flat(TR), AT[0][:, at, :].bitcast(F32), ALU.subtract).then_inc(at_lo, 1)
                            if i < T:
                                z_low(2 * i + 1)
                        add(T - 1)

        def ternary(gate, WT, ahead):
            NF = 8
            with ExitStack() as ctx:
                LE = sbuf(ctx, "LE", [P, 2048])
                WQT = sbuf(ctx, "WQT", [P, 2, 2048], F32R)
                ASUM = sbuf(ctx, "ASUM", [P, 2])
                THR = sbuf(ctx, "THR", [P, 2, 2])
                B1 = sbuf(ctx, "B1", [P, NF])
                B2 = sbuf(ctx, "B2", [P, D])
                B2G = sbuf(ctx, "B2G", [P, D])
                HF = sbuf(ctx, "HF", [P, 2, HALF])
                HS = split(ctx, "HS", [P, NF, B * S])
                UP = psum(ctx, "UP", [P, 4, 512])
                NB = psum(ctx, "NB", [P, 4, 512])
                nrm = norm(ctx, "f1", [NB[:, j, :] for j in range(4)])
                b_in, fetched = sem(ctx, "b_in"), sem(ctx, "fetched")
                quant = Count(sem(ctx, "quantise_steps"))
                sums_ready, mean_ps = sem(ctx, "sums_ready"), sem(ctx, "mean_in_psum")
                wq_ready = sem(ctx, "ternary_ready")
                b2_ready, b2_added = sem(ctx, "b2_ready"), sem(ctx, "b2_added")
                up_done, gelu_done, h_hi, h_lo = (sem(ctx, s) for s in ("up_done", "gelu_done", "h_hi", "h_lo"))
                down_done, added, stats = sem(ctx, "down_done"), sem(ctx, "added"), sem(ctx, "measured")
                CHUNKS = [(half, f) for half in range(2) for f in range(NF)]
                with nc.Block() as block:
                    @block.sync
                    def _(sp):
                        sp.dma_start(B1[:, :], A["f1_b1"]).then_inc(b_in, 16)
                        sp.dma_start(B2[:, :], A["f1_b2"]).then_inc(b_in, 16)
                        fetch_ahead(sp, ahead, fetched)

                    @block.gpsimd
                    def _(pool):
                        pool.wait_ge(b2_ready, 1)
                        pool.wait_ge(nrm["xn_ready"], T)
                        pool.tensor_tensor(X[:, :, :], X[:, :, :], B2G[:, :].unsqueeze(1).broadcast_to((P, T, D)), ALU.add).then_inc(b2_added, 1)

                    @block.vector
                    def _(dve):
                        for i in range(2):
                            dve.tensor_reduce(ASUM[:, i:i + 1], WT[:, i, :], AX, ALU.add, apply_absolute_value=True).then_inc(sums_ready, 1)
                        nrm["vector"](dve)
                        nrm["vector_low"](dve)
                        dve.wait_ge(mean_ps, 1)
                        quant.inc(dve.tensor_scalar(THR[:, 0, :], UP[:, 0, 0:2], 1.0 / (P * 2048), 0.7, ALU.mult, ALU.mult))
                        quant.wait(dve)
                        quant.inc(dve.tensor_scalar(THR[:, 1, :], THR[:, 0, :], -1.0, None, ALU.mult))
                        quant.wait(dve)
                        for i in range(2):
                            quant.inc(dve.tensor_scalar(LE[:, :], WT[:, i, :], THR[:, 1, i:i + 1], None, ALU.is_le))
                            quant.wait(dve)
                            dve.scalar_tensor_tensor(out=WQT[:, i, :], in0=WT[:, i, :], scalar=THR[:, 0, i:i + 1], in1=LE[:, :],
                                                     op0=ALU.is_ge, op1=ALU.subtract).then_inc(wq_ready, 1)
                            dve.wait_ge(wq_ready, i + 1)
                        dve.wait_ge(b_in, 32)
                        dve.tensor_scalar(B2G[:, :], B2[:, :], GATE[:, gate:gate + 1], None, ALU.mult).then_inc(b2_ready, 1)

                        def parts(n):
                            half, f = CHUNKS[n]
                            at = slice(half * HALF, (half + 1) * HALF)
                            dve.wait_ge(gelu_done, n + 1)
                            dve.tensor_copy(HS[0][:, f, at], HF[:, n % 2, :]).then_inc(h_hi, 1)
                            dve.wait_ge(h_hi, n + 1)
                            dve.tensor_tensor(HS[1][:, f, at], HF[:, n % 2, :], HS[0][:, f, at].bitcast(F32), ALU.subtract).then_inc(h_lo, 1)

                        def add(t):
                            if t == 0:
                                dve.wait_ge(b2_added, 1)
                            dve.wait_ge(down_done, t + 1)
                            dve.scalar_tensor_tensor(out=X[:, t, :], in0=NB[:, t % 4, 0:D], scalar=GATE[:, gate:gate + 1], in1=X[:, t, :],
                                                     op0=ALU.mult, op1=ALU.add).then_inc(added, 1)
                            dve.wait_ge(added, t + 1)
                            measure(dve, stats, t)
                        for n in range(2 * NF):
                            parts(n)
                        for t in range(T):
                            add(t)

                    @block.scalar
                    def _(act):
                        nrm["deviation"](act)
                        nrm["scalar"](act)
                        act.wait_ge(b_in, 32)
                        for n, (half, f) in enumerate(CHUNKS):
                            act.wait_ge(up_done, n + 1)
                            if n >= 2:
                                act.wait_ge(h_lo, n - 1)
                            act.activation(HF[:, n % 2, :], UP[:, n % 4, :], ACT.Gelu, bias=B1[:, f:f + 1]).then_inc(gelu_done, 1)

                    @block.tensor
                    def _(pe):
                        pe.wait_ge(sums_ready, 2)
                        pe.matmul(UP[:, 0, 0:2], ONES[:, :], ASUM[:, :], start=True, stop=True).then_inc(mean_ps, 1)
                        nrm["tensor"](pe)
                        pe.wait_ge(nrm["ready"], 4)
                        pe.wait_ge(wq_ready, 1)
                        for n, (half, f) in enumerate(CHUNKS):
                            if n >= 4:
                                pe.wait_ge(gelu_done, n - 3)
                            for k in range(KD):
                                for i in range(2):
                                    last = pe.matmul(UP[:, n % 4, :], WQT[:, 0, k * 1024 + f * P:k * 1024 + (f + 1) * P], xt[i][:, k, half * HALF:(half + 1) * HALF],
                                                     start=k + i == 0, stop=k + i == KD)
                            last.then_inc(up_done, 1)
                        pe.wait_ge(wq_ready, 2)
                        for t in range(T):
                            pe.wait_ge(h_lo, NF * (t // 4 + 1))
                            if t >= 4:
                                pe.wait_ge(added, t - 3)
                            for f in range(NF):
                                for i in range(2):
                                    last = pe.matmul(NB[:, t % 4, 0:D], HS[i][:, f, t * P:(t + 1) * P], WQT[:, 1, f * D:(f + 1) * D], start=f + i == 0, stop=f + i == NF)
                            last.then_inc(down_done, 1)

        def int8(gate, ahead):
            with ExitStack() as ctx:
                WF = sbuf(ctx, "WF", [P, KD, D])
                WR = sbuf(ctx, "WR", [P, KD, D])
                WQ = sbuf(ctx, "WQ8", [P, KD, D], BF16)
                WQT = sbuf(ctx, "WQT8", [P, KD, D], BF16)
                WM = sbuf(ctx, "WM", [P, 4, KD])
                WMH = sbuf(ctx, "WMH", [P, KD], F32R)
                WML = sbuf(ctx, "WML", [P, KD])
                IDENTR = sbuf(ctx, "IDENTR", [P, P], F32R)
                WSC = split(ctx, "WSC", [P, KD, P])
                WSB = sbuf(ctx, "WSB", [P, D])
                BI = sbuf(ctx, "BI", [P, D])
                BIG = sbuf(ctx, "BIG", [P, D])
                XR = sbuf(ctx, "XR", [P, T, D])
                XQ = sbuf(ctx, "XQ8", [P, T, D], BF16)
                XQT = sbuf(ctx, "XQT8", [P, KD, B * S], BF16)
                XM = sbuf(ctx, "XM", [P, 3, T])
                YS = sbuf(ctx, "YS", [P, 4, D])
                TP = psum(ctx, "TP", [P, 2, 1024], BF16)
                WP = psum(ctx, "WP", [P, 512], BF16)
                SP = psum(ctx, "SP", [P, 512])
                OP = psum(ctx, "OP", [P, 4, 512])
                nrm = norm(ctx, "f2", None)
                loaded, fetched = sem(ctx, "loaded"), sem(ctx, "fetched")
                wst = Count(sem(ctx, "weight_steps"))
                xst = Count(sem(ctx, "token_steps"))
                ws_ready, wq_ready, x_ready = sem(ctx, "scales_ready"), sem(ctx, "weights_ready"), sem(ctx, "tokens_ready")
                ws_ps, wt_ps, wt_ready, xt_ps, xt_sb = (sem(ctx, s) for s in ("scales_in_psum", "weights_turned", "weights_there", "tokens_turned", "tokens_there"))
                out_ps, added = sem(ctx, "out_in_psum"), sem(ctx, "added")
                bias_ready, bias_added = sem(ctx, "bias_ready"), sem(ctx, "bias_added")
                ysteps, stats = sem(ctx, "scaled"), sem(ctx, "measured")

                def rounded(dve, count, dst, tmp, src, inv):
                    count.inc(dve.tensor_scalar(tmp, src, inv, MAGIC, ALU.mult, ALU.add))
                    count.wait(dve)
                    count.inc(dve.tensor_scalar(tmp, tmp, MAGIC, 127.0, ALU.subtract, ALU.min))
                    count.wait(dve)
                    return dve.tensor_scalar(dst, tmp, -128.0, None, ALU.max)

                with nc.Block() as block:
                    @block.sync
                    def _(sp):
                        sp.dma_start(WF[:, :, :], A["f2_w"].rearrange("(k p) d -> p k d", p=P)).then_inc(loaded, 16)
                        sp.dma_start(BI[:, :], A["f2_bias"]).then_inc(loaded, 16)
                        fetch_ahead(sp, ahead, fetched)

                    @block.gpsimd
                    def _(pool):
                        pool.wait_ge(bias_ready, 1)
                        pool.wait_ge(nrm["xn_ready"], T)
                        pool.tensor_tensor(X[:, :, :], X[:, :, :], BIG[:, :].unsqueeze(1).broadcast_to((P, T, D)), ALU.add).then_inc(bias_added, 1)
                        pool.wait_ge(bias_added, 1)
                        for t in range(T):
                            pool.wait_ge(ysteps, t + 1)
                            pool.tensor_tensor(X[:, t, :], X[:, t, :], YS[:, t % 4, :], ALU.add).then_inc(added, 1)

                    @block.scalar
                    def _(act):
                        nrm["deviation"](act)
                        for h in range(2):
                            act.wait_ge(xt_ps, h + 1)
                            act.activation(XQT[:, :, h * HALF:(h + 1) * HALF], TP[:, h, :].rearrange("p (k n) -> p k n", k=KD), ACT.Copy).then_inc(xt_sb, 1)
                        act.wait_ge(wt_ps, 1)
                        act.activation(WQT[:, :, :].rearrange("p k o -> p (k o)"), WP[:, :], ACT.Copy).then_inc(wt_ready, 1)

                    @block.vector
                    def _(dve):
                        nrm["vector"](dve)
                        for h in range(2):
                            t4 = slice(4 * h, 4 * h + 4)
                            dve.wait_ge(nrm["xn_ready"], 4 * (h + 1))
                            xst.inc(dve.tensor_reduce(XM[:, 0, t4], XN[:, t4, :], AX, ALU.max, apply_absolute_value=True))
                            xst.wait(dve)
                            xst.inc(dve.tensor_scalar(XM[:, 1, t4], XM[:, 0, t4], 1.0 / 127.0, 1e-12, ALU.mult, ALU.max))
                            xst.wait(dve)
                            xst.inc(dve.reciprocal(XM[:, 2, t4], XM[:, 1, t4]))
                            xst.wait(dve)
                            for t in range(4 * h, 4 * h + 4):
                                xst.inc(dve.tensor_scalar(XR[:, t, :], XN[:, t, :], XM[:, 2, t:t + 1], MAGIC, ALU.mult, ALU.add))
                            xst.wait(dve)
                            xst.inc(dve.tensor_scalar(XR[:, t4, :], XR[:, t4, :], MAGIC, 127.0, ALU.subtract, ALU.min))
                            xst.wait(dve)
                            dve.tensor_scalar(XQ[:, t4, :], XR[:, t4, :], -128.0, None, ALU.max).then_inc(x_ready, 1)
                        dve.wait_ge(loaded, 32)
                        wst.inc(dve.tensor_reduce(WM[:, 0, :], WF[:, :, :], AX, ALU.max, apply_absolute_value=True))
                        wst.wait(dve)
                        wst.inc(dve.tensor_scalar(WM[:, 2, :], WM[:, 0, :], 1e-8, 1.0 / 127.0, ALU.max, ALU.mult))
                        wst.wait(dve)
                        wst.inc(dve.tensor_copy(WMH[:, :], WM[:, 2, :]))
                        wst.wait(dve)
                        wst.inc(dve.tensor_tensor(WML[:, :], WM[:, 2, :], WMH[:, :].bitcast(F32), ALU.subtract))
                        wst.wait(dve)
                        dve.tensor_copy(IDENTR[:, :], IDENT[:, :]).then_inc(ws_ready, 1)
                        for i, part in enumerate((WMH[:, :].bitcast(F32), WML[:, :])):
                            for k in range(KD):
                                dve.tensor_scalar(WSC[i][:, k, :], ONES[:, :], part[:, k:k + 1], None, ALU.mult).then_inc(ws_ready, 1)
                        wst.inc(dve.reciprocal(WM[:, 3, :], WM[:, 2, :]))
                        wst.wait(dve)
                        for k in range(KD):
                            rounded(dve, wst, WQ[:, k, :], WR[:, k, :], WF[:, k, :], WM[:, 3, k:k + 1]).then_inc(wq_ready, 1)
                        dve.tensor_scalar(BIG[:, :], BI[:, :], GATE[:, gate:gate + 1], None, ALU.mult).then_inc(bias_ready, 1)
                        dve.wait_ge(ws_ps, 1)
                        wst.inc(dve.tensor_scalar(WSB[:, :], SP[:, 0:D], GATE[:, gate:gate + 1], None, ALU.mult))
                        wst.wait(dve)
                        for t in range(T):
                            dve.wait_ge(out_ps, t + 1)
                            if t >= 4:
                                dve.wait_ge(added, t - 3)
                            dve.scalar_tensor_tensor(out=YS[:, t % 4, :], in0=OP[:, t % 4, 0:D], scalar=XM[:, 1, t:t + 1], in1=WSB[:, :],
                                                     op0=ALU.mult, op1=ALU.mult).then_inc(ysteps, 1)
                            if t >= 2:
                                dve.wait_ge(added, t - 1)
                                measure(dve, stats, t - 2)
                        for t in (T - 2, T - 1):
                            dve.wait_ge(added, t + 1)
                            measure(dve, stats, t)

                    @block.tensor
                    def _(pe):
                        def turn_tokens(h):
                            pe.wait_ge(x_ready, h + 1)
                            for k in range(KD):
                                for q in range(4):
                                    last = pe.transpose(TP[:, h, k * HALF + q * P:k * HALF + (q + 1) * P], XQ[:, 4 * h + q, k * P:(k + 1) * P], IDENTB[:, :])
                            last.then_inc(xt_ps, 1)
                        turn_tokens(0)
                        turn_tokens(1)
                        pe.wait_ge(ws_ready, 1 + 2 * KD)
                        for k in range(KD):
                            for i in range(2):
                                last = pe.matmul(SP[:, k * P:(k + 1) * P], WSC[i][:, k, :], IDENTR[:, :], start=i == 0, stop=i == 1)
                        last.then_inc(ws_ps, 1)
                        pe.wait_ge(wq_ready, KD)
                        for k in range(KD):
                            for o in range(KD):
                                last = pe.transpose(WP[:, k * D + o * P:k * D + (o + 1) * P], WQ[:, o, k * P:(k + 1) * P], IDENTB[:, :])
                        last.then_inc(wt_ps, 1)
                        pe.wait_ge(wt_ready, 1)
                        for t in range(T):
                            pe.wait_ge(xt_sb, t // 4 + 1)
                            if t >= 4:
                                pe.wait_ge(ysteps, t - 3)
                            for k in range(KD):
                                last = pe.matmul(OP[:, t % 4, 0:D], XQT[:, k, t * P:(t + 1) * P], WQT[:, k, :], start=k == 0, stop=k == KD - 1)
                            last.then_inc(out_ps, 1)

        with ExitStack() as ctx:
            phase[0] = "attn0_"
            Y = split(ctx, "Y", [P, NP * D])
            AT = split(ctx, "AT", [P, NP * B * S])
            latent_rope(Y, AT)
            phase[0] = "attn0_out_"
            latent_out(Y, AT, 0)
        phase[0] = "ffn0_"
        experts("f0", 4, 9, 3, 16, 6, True)
        with ExitStack() as mid:
            CW = sbuf(mid, "CW", [DC, B * L + 2 * D])
            QO = sbuf(mid, "QO", [P, 4, D])
            HM = sbuf(mid, "HEADMASK", [P, 8])
            with ExitStack() as layer1:
                width = pair_columns(1)[-1]
                STAGE = sbuf(layer1, "STAGE", [P, 2 * width])
                WT = STAGE[:, 0:2 * 2048].rearrange("p (i n) -> p i n", i=2)
                with ExitStack() as ctx:
                    phase[0] = "chain1_"
                    GS = split(ctx, "GS", [P, KD, B, H * L])
                    Y = split(ctx, "Y", [P, NP * D])
                    latent_chain(GS, Y, STAGE[:, :].rearrange("p (a n) -> p a n", a=2))

                    def latent_values(b, pair):
                        at = slice(pair * D, (pair + 1) * D)
                        return (KVB[0][:, b, :], KVB[1][:, b, :]), (Y[0][:, at], Y[1][:, at])
                    phase[0] = "attn1_"
                    attend("a1", GS, latent_values, 1, 1.0, False, [(WT, A["f1_w"])])
                phase[0] = "ffn1_"
                ternary(5, WT, [(CW[:, :], A["a2_cw"]), (HM[:, :], A["headmask"]), (QO[:, :, :], A["a2_qo"])])
            clear_semaphores()
            for layer in (2, 3):
                with ExitStack() as ctx:
                    phase[0] = f"chain{layer}_"
                    GS = split(ctx, "GS", [P, KD, B, H * L])
                    VB = split(ctx, "VB", [P, 2, B, 512])
                    WO = split(ctx, "WO", [P, 2, D])
                    plain_chain(f"a{layer}", GS, VB, WO, CW, QO, HM)

                    def values(b, pair):
                        j, c = pair // 4, (pair % 4) * P
                        return (VB[0][:, j, b, c:c + P], VB[1][:, j, b, c:c + P]), (WO[0][:, j, :], WO[1][:, j, :])
                    phase[0] = f"attn{layer}_"
                    attend(f"b{layer}", GS, values, layer, 0.25, True)
                if layer == 2:
                    phase[0] = "ffn2_"
                    int8(6, [(CW[:, :], A["a3_cw"]), (QO[:, :, :], A["a3_qo"])])
                    clear_semaphores()
        phase[0] = "ffn3_"
        experts("f3", 7, 9, 4, 8, 2, False)
        phase[0] = ""

        with ExitStack() as ctx:
            stored = sem(ctx, "stored")
            with nc.Block() as block:
                @block.sync
                def _(sp):
                    sp.dma_start(out.rearrange("(t p) d -> p t d", p=P), X[:, :, :]).then_inc(stored, 16)
                    sp.wait_ge(stored, 16)


def rope_table(length, dim):
    inv = (np.float32(1.0) / np.power(np.float32(10000.0), np.arange(0, dim, 2, dtype=np.float32) / np.float32(dim))).astype(np.float32)
    f = np.arange(length, dtype=np.float32)[:, None] * inv[None, :]
    return np.repeat(np.sin(f), 2, axis=-1).astype(np.float32), np.repeat(np.cos(f), 2, axis=-1).astype(np.float32)


def constants():
    sin, cos = rope_table(L, DC)
    sin = np.concatenate([-sin[:, :DC // 2], sin[:, DC // 2:]], axis=1)
    qsin, qcos = rope_table(S, CQ)
    c = {
        "ident": np.eye(P, dtype=np.float32),
        "kcos": np.tile(cos.T, (2, B)), "ksin": np.tile(sin.T, (2, B)),
        "qcos": np.stack([qcos.T[:ROT], qcos.T[ROT:]], 1), "qsin": np.stack([qsin.T[ROT:], -qsin.T[:ROT]], 1),
        "headmask": (np.arange(P)[:, None] // 16 == np.arange(8)[None, :]).astype(np.float32),
    }
    for e in (8, 16):
        c[f"before{e}"] = np.broadcast_to((np.arange(e)[None, :] < np.arange(e)[:, None]).astype(np.float32).reshape(1, e * e), (P, e * e))
    return {k: np.ascontiguousarray(v, dtype=np.float32) for k, v in c.items()}


def pairs(layer, Wq, w_kc_q, w_kc_kv, W_qr, W_kr, Wo):
    o_qr, o_kr, o_ck, o_wo, width = pair_columns(layer)
    w = np.zeros((NP, P, width), np.float32)
    for h in range(H):
        p, j = divmod(h, 2)
        w[p, :, O_WQ + D * j:O_WQ + D * (j + 1)] = Wq[h * K:(h + 1) * K]
        if layer == 0:
            w[p, :, O_CQ + CQ * j:O_CQ + CQ * (j + 1)] = w_kc_q[h]
        else:
            for q in range(2):
                c = O_CQ + 2 * K * j + K * q
                w[p, :ROT, c:c + K] = w_kc_q[h][:, ROT * q:ROT * (q + 1)].T
        w[p, :R, o_qr + CQ * j:o_qr + CQ * (j + 1)] = W_qr[h].T
        w[p, :DC, o_kr + R * j:o_kr + R * (j + 1)] = W_kr[h]
        w[p, :, o_ck + P * j + DC * j:o_ck + P * j + DC * (j + 1)] = w_kc_kv[h]
        w[p, :, o_wo + D * j:o_wo + D * (j + 1)] = Wo[:, h * K:(h + 1) * K].T
    return w


def expert_pairs(a):
    n, hid = 18, 176
    up = np.zeros((n // 2, P, 3, KD, 2, P), np.float32)
    down = np.zeros((n // 2, P, 4, D), np.float32)
    bias = np.zeros((P, n // 2, 3, 2), np.float32)
    for e in range(n):
        if e < 16:
            g, u, gb, ub, d = a["w1"][e], a["w3"][e], a["b1"][e], a["b3"][e], a["w2"][e]
        else:
            s = slice(hid * (e - 16), hid * (e - 15))
            g, u, gb, ub, d = a["ws1"][s], a["ws3"][s], a["bs1"][s], a["bs3"][s], a["ws2"][:, s]
        p, j = divmod(e, 2)
        for chunk, tile, to, rows in ((2 * j, 3 * j, 0, slice(0, P)), (1, 1 + j, 64 * j, slice(P, hid))):
            k = rows.stop - rows.start
            for m, w in ((0, g), (1, u)):
                up[p, :, chunk, :, m, to:to + k] = w[rows].T.reshape(KD, P, k).transpose(1, 0, 2)
            down[p, to:to + k, tile] = d[:, rows].T
            bias[to:to + k, p, chunk, 0], bias[to:to + k, p, chunk, 1] = gb[rows], ub[rows]
    return up.reshape(n // 2, P, -1), down.reshape(n // 2, P, -1), bias.reshape(P, -1)


def layout(i):
    i = {k: np.asarray(v) for k, v in i.items()}
    a = constants()
    a["x"] = i["x"].reshape(B * S, D)
    a["gates"] = np.broadcast_to(np.concatenate([i["g_xattn"], i["g_ffn"]])[None], (P, 8))
    ctxT = i["ctx_512"].reshape(B * L, DC).T
    a["kvT"] = np.concatenate([ctxT, ctxT])
    swapped = np.concatenate([ctxT[DC // 2:], ctxT[:DC // 2]])
    a["kvT_swapped"] = np.concatenate([swapped, swapped])
    for l in (0, 1):
        a[f"L{l}_pairs"] = pairs(l, *(i[f"L{l}_xattn_{n}"] for n in ("Wq", "w_kc_q", "w_kc_kv", "W_qr", "W_kr", "Wo")))
    f0 = {k[7:]: v for k, v in i.items() if k.startswith("L0_ffn_")}
    a["f0_up"], a["f0_down"], a["f0_bias"] = expert_pairs(f0)
    a["f0_router"] = f0["gate_w"].T.reshape(KD, P, 16).transpose(1, 0, 2)
    a["f0_router_bias"] = np.broadcast_to(f0["gate_b"][None], (P, 16))
    a["f0_b2"] = np.concatenate([f0["b2"], f0["bs2"][None]])
    w1, w2 = i["L1_ffn_w1"], i["L1_ffn_w2"]
    a["f1_w"] = np.stack([w1.T.reshape(KD, P, 1024).transpose(1, 0, 2).reshape(P, 2048), w2.T.reshape(8, P, D).transpose(1, 0, 2).reshape(P, 2048)], 1)
    a["f1_b1"] = i["L1_ffn_b1"].reshape(8, P).T
    a["f1_b2"] = np.broadcast_to(i["L1_ffn_b2"][None], (P, D))
    for l in (2, 3):
        a[f"a{l}_cw"] = np.concatenate([ctxT, i[f"L{l}_xattn_Wkv_expand"].T], axis=1)
        a[f"a{l}_qo"] = np.concatenate([i[f"L{l}_xattn_Wq"].reshape(2, P, D), i[f"L{l}_xattn_Wout"].T.reshape(2, P, D)]).transpose(1, 0, 2)
    a["f2_w"] = i["L2_ffn_weight"]
    a["f2_bias"] = np.broadcast_to(i["L2_ffn_bias"][None], (P, D))
    gu = np.concatenate([i["L3_ffn_w_gate_up"], i["L3_ffn_shared_gate_up"][None]])
    gu = gu.reshape(9, KD, P, 2, 4, P)
    a["f3_up"] = gu.transpose(0, 2, 4, 1, 3, 5).reshape(9, P, -1)
    dn = np.concatenate([i["L3_ffn_w_down"], i["L3_ffn_shared_down"][None]])
    a["f3_down"] = dn.reshape(9, 4, P, D).transpose(0, 2, 1, 3).reshape(9, P, -1)
    a["f3_router"] = i["L3_ffn_gate_w"].reshape(KD, P, 8).transpose(1, 0, 2)
    return {k: np.ascontiguousarray(v) for k, v in a.items()}


def kernel(**inputs):
    import concourse.bacc as bacc
    from concourse.bass_utils import run_bass_kernel_spmd

    nc = bacc.Bacc("TRN2", target_bir_lowering=False, num_devices=1)
    arrays = {f"in_{k}": v for k, v in layout(inputs).items()}
    aps = {k[3:]: nc.dram_tensor(k, v.shape, mybir.dt.from_np(v.dtype), kind="ExternalInput").ap() for k, v in arrays.items()}
    out = nc.dram_tensor("out_x", (B * S, D), F32, kind="ExternalOutput").ap()
    program(nc, aps, out)
    r = run_bass_kernel_spmd(nc, [arrays], core_ids=[0])
    return r.results[0]["out_x"].reshape(B, S, D)
```
